# Optimizing a Trainium2 kernel written in Bass

```python
import numpy as np
import jax
import jax.numpy as jnp

def _softmax(x, axis=-1):
    return jax.nn.softmax(x, axis=axis)

def _gelu(x):
    return jax.nn.gelu(x, approximate=True)

def _silu(x):
    return jax.nn.silu(x)

def _sigmoid(x):
    return jax.nn.sigmoid(x)

def _layernorm(x, axis=-1, eps=1e-05):
    m = jnp.mean(x, axis=axis, keepdims=True)
    v = jnp.var(x, axis=axis, keepdims=True)
    return (x - m) / jnp.sqrt(v + eps)

def _scatter_add(tgt, idx, src, axis=0):
    return tgt.at[idx].add(src)

def _segment_sum(src, seg, n):
    return jax.ops.segment_sum(src, seg, n)
kernel_name = 'mk_gnn_preln_d4_gnn_r64_b322f2'

def setup_inputs(seed: int=0):
    np.random.seed(seed)
    _w = jnp.asarray

    def _rec_inputs():
        import jax
        import jax.numpy as jnp
        _gk = jax.random.key(seed)
        x = -0.0003713 + 1 * jax.random.normal(jax.random.fold_in(_gk, 1), (100000, 128), jnp.float32)
        src = jax.random.randint(jax.random.fold_in(_gk, 2), (50000,), 0, 100000, jnp.int32)
        dst = jax.random.randint(jax.random.fold_in(_gk, 3), (50000,), 0, 100000, jnp.int32)
        _o = jnp.argsort(dst, stable=True)
        src = src[_o]
        dst = dst[_o]
        edge_attr_64 = 0.000167468 + 1.0002 * jax.random.normal(jax.random.fold_in(_gk, 11), (50000, 64), jnp.float32)
        edge_weight1 = 0.000937891 + 0.999965 * jax.random.normal(jax.random.fold_in(_gk, 13), (50000, 1), jnp.float32)
        return (x, src, dst, edge_attr_64, edge_weight1)
    x, src, dst, edge_attr_64, edge_weight1 = _rec_inputs()

    def _L0_gnn_setup():
        import jax, jax.numpy as jnp
        import numpy as np
        N_NODES = 100000
        N_EDGES = 25000
        IN_CH = 128
        HID = 128

        def _gcn_norm(edge_index, num_nodes):
            loop = jnp.arange(num_nodes, dtype=edge_index.dtype)
            src = jnp.concatenate([edge_index[0], loop])
            dst = jnp.concatenate([edge_index[1], loop])
            ones = jnp.ones(src.shape[0], dtype=jnp.float32)
            deg = jax.ops.segment_sum(ones, dst, num_segments=num_nodes)
            dis = jax.lax.rsqrt(deg)
            norm = dis[src] * dis[dst]
            return (src, dst, norm)

        def _gcn_layer(x, src, dst, norm, W, b):
            h = x @ W
            msg = h[src] * norm[:, None]
            out = jax.ops.segment_sum(msg, dst, num_segments=x.shape[0])
            return out + b
        key = jax.random.key(seed)
        k1, k2, k3, k4 = jax.random.split(key, 4)
        x = jax.random.normal(k1, (N_NODES, IN_CH), dtype=jnp.float32)
        edge_index = jax.random.randint(k2, (2, N_EDGES), 0, N_NODES, dtype=jnp.int64)
        W1 = jax.random.normal(k3, (IN_CH, HID), dtype=jnp.float32) * (1.0 / np.sqrt(IN_CH))
        W2 = jax.random.normal(k4, (HID, HID), dtype=jnp.float32) * (1.0 / np.sqrt(HID))
        b1 = jnp.zeros((HID,), dtype=jnp.float32)
        b2 = jnp.zeros((HID,), dtype=jnp.float32)
        return {'x': x, 'edge_index': edge_index, 'W1': W1, 'b1': b1, 'W2': W2, 'b2': b2}
    _L0_gnn_all = _L0_gnn_setup()
    _L0_gnn_in = {k: v for k, v in _L0_gnn_all.items() if k in ('W1', 'b1', 'W2', 'b2')}
    del _L0_gnn_all

    def _L1_gnn_setup():
        import jax, jax.numpy as jnp
        import numpy as np
        N_NODES = 50000
        N_EDGES = 12500
        D_MODEL = 128
        N_HEADS = 8
        D_HEAD = D_MODEL // N_HEADS
        EPS_BN = 1e-05

        def _batchnorm(h, g, b):
            mu = jnp.mean(h, axis=0, keepdims=True)
            var = jnp.var(h, axis=0, keepdims=True)
            return (h - mu) * jax.lax.rsqrt(var + EPS_BN) * g + b
        key = jax.random.key(seed)
        ks = jax.random.split(key, 16)
        s = 0.05
        inp = {'x': jax.random.normal(ks[0], (N_NODES, D_MODEL), jnp.float32), 'edge_attr': jax.random.normal(ks[1], (N_EDGES, 1), jnp.float32), 'edge_index': jax.random.randint(ks[2], (2, N_EDGES), 0, N_NODES, jnp.int32), 'Wq': jax.random.normal(ks[3], (D_MODEL, D_MODEL), jnp.float32) * s, 'Wk': jax.random.normal(ks[4], (D_MODEL, D_MODEL), jnp.float32) * s, 'We': jax.random.normal(ks[5], (1, D_MODEL), jnp.float32) * s, 'Wv': jax.random.normal(ks[6], (D_MODEL, D_MODEL), jnp.float32) * s, 'Wo': jax.random.normal(ks[7], (D_MODEL, D_MODEL), jnp.float32) * s, 'bo': jnp.zeros((D_MODEL,), jnp.float32), 'g1': jnp.ones((D_MODEL,), jnp.float32), 'b1': jnp.zeros((D_MODEL,), jnp.float32), 'W1': jax.random.normal(ks[8], (D_MODEL, 2 * D_MODEL), jnp.float32) * s, 'bf1': jnp.zeros((2 * D_MODEL,), jnp.float32), 'W2': jax.random.normal(ks[9], (2 * D_MODEL, D_MODEL), jnp.float32) * s, 'bf2': jnp.zeros((D_MODEL,), jnp.float32), 'g2': jnp.ones((D_MODEL,), jnp.float32), 'b2': jnp.zeros((D_MODEL,), jnp.float32)}
        return inp
    _L1_gnn_all = _L1_gnn_setup()
    _L1_gnn_in = {k: v for k, v in _L1_gnn_all.items() if k in ('Wq', 'Wk', 'We', 'Wv', 'Wo', 'bo', 'g1', 'b1', 'W1', 'bf1', 'W2', 'bf2', 'g2', 'b2')}
    del _L1_gnn_all

    def _L2_gnn_setup():
        import jax, jax.numpy as jnp
        import numpy as np
        N_NODES = 100000
        N_EDGES = 12500
        IN_DIM = 128
        NUM_HEADS = 8
        HEAD_DIM = 16
        key = jax.random.key(seed)
        ks = jax.random.split(key, 10)
        scale = 1.0 / np.sqrt(IN_DIM)
        return {'x': jax.random.normal(ks[0], (N_NODES, IN_DIM), dtype=jnp.float32), 'edge_index': jax.random.randint(ks[1], (2, N_EDGES), 0, N_NODES, dtype=jnp.int64), 'virt_h': jax.random.normal(ks[2], (1, IN_DIM), dtype=jnp.float32), 'virt_edge_index': jax.random.randint(ks[3], (2, 1), 0, 1, dtype=jnp.int64), 'Wq': jax.random.normal(ks[4], (IN_DIM, NUM_HEADS * HEAD_DIM), dtype=jnp.float32) * scale, 'bq': jnp.zeros((NUM_HEADS * HEAD_DIM,), dtype=jnp.float32), 'Wk': jax.random.normal(ks[5], (IN_DIM, NUM_HEADS * HEAD_DIM), dtype=jnp.float32) * scale, 'bk': jnp.zeros((NUM_HEADS * HEAD_DIM,), dtype=jnp.float32), 'Wv': jax.random.normal(ks[6], (IN_DIM, NUM_HEADS * HEAD_DIM), dtype=jnp.float32) * scale, 'bv': jnp.zeros((NUM_HEADS * HEAD_DIM,), dtype=jnp.float32)}
    _L2_gnn_all = _L2_gnn_setup()
    _L2_gnn_in = {k: v for k, v in _L2_gnn_all.items() if k in ('virt_h', 'virt_edge_index', 'Wq', 'bq', 'Wk', 'bk', 'Wv', 'bv')}
    del _L2_gnn_all

    def _L3_gnn_setup():
        import jax, jax.numpy as jnp
        import numpy as np
        LOG2 = float(np.log(2.0))

        def ssp(x):
            return jax.nn.softplus(x) - LOG2
        N, E, H, EC = (625, 10000, 128, 64)
        key = jax.random.key(seed)
        ks = jax.random.split(key, 12)
        s = lambda k, shape, fan_in: jax.random.normal(k, shape, jnp.float32) * (1.0 / np.sqrt(fan_in))
        return {'x': jax.random.normal(ks[0], (N, H), jnp.float32), 'edge_index': jax.random.randint(ks[1], (2, E), 0, N, jnp.int32), 'edge_attr': jax.random.normal(ks[2], (E, EC), jnp.float32), 'W_v': s(ks[3], (H, H), H), 'W_wv1': s(ks[4], (H, EC), EC), 'b_wv1': jnp.zeros((H,), jnp.float32), 'W_wv2': s(ks[5], (H, H), H), 'b_wv2': jnp.zeros((H,), jnp.float32), 'W_wvl': s(ks[6], (H, H), H), 'b_wvl': jnp.zeros((H,), jnp.float32), 'W_c': s(ks[7], (H, H), H), 'b_c': jnp.zeros((H,), jnp.float32), 'W_o': s(ks[8], (H, H), H), 'b_o': jnp.zeros((H,), jnp.float32)}
    _L3_gnn_all = _L3_gnn_setup()
    _L3_gnn_in = {k: v for k, v in _L3_gnn_all.items() if k in ('W_v', 'W_wv1', 'b_wv1', 'W_wv2', 'b_wv2', 'W_wvl', 'b_wvl', 'W_c', 'b_c', 'W_o', 'b_o')}
    del _L3_gnn_all
    return {'x': x, 'src': src, 'dst': dst, 'edge_attr_64': edge_attr_64, 'edge_weight1': edge_weight1, 'L0_gnn_W1': _L0_gnn_in['W1'], 'L0_gnn_b1': _L0_gnn_in['b1'], 'L0_gnn_W2': _L0_gnn_in['W2'], 'L0_gnn_b2': _L0_gnn_in['b2'], 'L1_gnn_Wq': _L1_gnn_in['Wq'], 'L1_gnn_Wk': _L1_gnn_in['Wk'], 'L1_gnn_We': _L1_gnn_in['We'], 'L1_gnn_Wv': _L1_gnn_in['Wv'], 'L1_gnn_Wo': _L1_gnn_in['Wo'], 'L1_gnn_bo': _L1_gnn_in['bo'], 'L1_gnn_g1': _L1_gnn_in['g1'], 'L1_gnn_b1': _L1_gnn_in['b1'], 'L1_gnn_W1': _L1_gnn_in['W1'], 'L1_gnn_bf1': _L1_gnn_in['bf1'], 'L1_gnn_W2': _L1_gnn_in['W2'], 'L1_gnn_bf2': _L1_gnn_in['bf2'], 'L1_gnn_g2': _L1_gnn_in['g2'], 'L1_gnn_b2': _L1_gnn_in['b2'], 'L2_gnn_virt_h': _L2_gnn_in['virt_h'], 'L2_gnn_virt_edge_index': _L2_gnn_in['virt_edge_index'], 'L2_gnn_Wq': _L2_gnn_in['Wq'], 'L2_gnn_bq': _L2_gnn_in['bq'], 'L2_gnn_Wk': _L2_gnn_in['Wk'], 'L2_gnn_bk': _L2_gnn_in['bk'], 'L2_gnn_Wv': _L2_gnn_in['Wv'], 'L2_gnn_bv': _L2_gnn_in['bv'], 'L3_gnn_W_v': _L3_gnn_in['W_v'], 'L3_gnn_W_wv1': _L3_gnn_in['W_wv1'], 'L3_gnn_b_wv1': _L3_gnn_in['b_wv1'], 'L3_gnn_W_wv2': _L3_gnn_in['W_wv2'], 'L3_gnn_b_wv2': _L3_gnn_in['b_wv2'], 'L3_gnn_W_wvl': _L3_gnn_in['W_wvl'], 'L3_gnn_b_wvl': _L3_gnn_in['b_wvl'], 'L3_gnn_W_c': _L3_gnn_in['W_c'], 'L3_gnn_b_c': _L3_gnn_in['b_c'], 'L3_gnn_W_o': _L3_gnn_in['W_o'], 'L3_gnn_b_o': _L3_gnn_in['b_o']}

def reference(x, src, dst, edge_attr_64, edge_weight1, L0_gnn_W1, L0_gnn_b1, L0_gnn_W2, L0_gnn_b2, L1_gnn_Wq, L1_gnn_Wk, L1_gnn_We, L1_gnn_Wv, L1_gnn_Wo, L1_gnn_bo, L1_gnn_g1, L1_gnn_b1, L1_gnn_W1, L1_gnn_bf1, L1_gnn_W2, L1_gnn_bf2, L1_gnn_g2, L1_gnn_b2, L2_gnn_virt_h, L2_gnn_virt_edge_index, L2_gnn_Wq, L2_gnn_bq, L2_gnn_Wk, L2_gnn_bk, L2_gnn_Wv, L2_gnn_bv, L3_gnn_W_v, L3_gnn_W_wv1, L3_gnn_b_wv1, L3_gnn_W_wv2, L3_gnn_b_wv2, L3_gnn_W_wvl, L3_gnn_b_wvl, L3_gnn_W_c, L3_gnn_b_c, L3_gnn_W_o, L3_gnn_b_o):
    import jax
    import jax.numpy as jnp

    def _L0_gnn_ref(x, edge_index, W1, b1, W2, b2):
        import jax, jax.numpy as jnp
        import numpy as np
        N_NODES = 100000
        N_EDGES = 25000
        IN_CH = 128
        HID = 128

        def _gcn_norm(edge_index, num_nodes):
            loop = jnp.arange(num_nodes, dtype=edge_index.dtype)
            src = jnp.concatenate([edge_index[0], loop])
            dst = jnp.concatenate([edge_index[1], loop])
            ones = jnp.ones(src.shape[0], dtype=jnp.float32)
            deg = jax.ops.segment_sum(ones, dst, num_segments=num_nodes)
            dis = jax.lax.rsqrt(deg)
            norm = dis[src] * dis[dst]
            return (src, dst, norm)

        def _gcn_layer(x, src, dst, norm, W, b):
            h = x @ W
            msg = h[src] * norm[:, None]
            out = jax.ops.segment_sum(msg, dst, num_segments=x.shape[0])
            return out + b
        n = x.shape[0]
        src, dst, norm = _gcn_norm(edge_index, n)
        h = jax.nn.relu(_gcn_layer(x, src, dst, norm, W1, b1))
        h = jax.nn.relu(_gcn_layer(h, src, dst, norm, W2, b2))
        return h

    def _L1_gnn_ref(x, edge_attr, edge_index, Wq, Wk, We, Wv, Wo, bo, g1, b1, W1, bf1, W2, bf2, g2, b2):
        import jax, jax.numpy as jnp
        import numpy as np
        N_NODES = 50000
        N_EDGES = 12500
        D_MODEL = 128
        N_HEADS = 8
        D_HEAD = D_MODEL // N_HEADS
        EPS_BN = 1e-05

        def _batchnorm(h, g, b):
            mu = jnp.mean(h, axis=0, keepdims=True)
            var = jnp.var(h, axis=0, keepdims=True)
            return (h - mu) * jax.lax.rsqrt(var + EPS_BN) * g + b
        N = x.shape[0]
        Q = (x @ Wq).reshape(N, N_HEADS, D_HEAD)
        K = (x @ Wk).reshape(N, N_HEADS, D_HEAD)
        V = (x @ Wv).reshape(N, N_HEADS, D_HEAD)
        E = (edge_attr @ We).reshape(-1, N_HEADS, D_HEAD)
        src_idx = edge_index[0]
        dst_idx = edge_index[1]
        score = K[src_idx] * Q[dst_idx] * (1.0 / np.sqrt(D_HEAD)) * E
        score = jnp.exp(jnp.clip(jnp.sum(score, axis=-1, keepdims=True), -5.0, 5.0))
        msg = V[src_idx] * score
        wV = jax.ops.segment_sum(msg, dst_idx, num_segments=N)
        Z = jax.ops.segment_sum(score, dst_idx, num_segments=N)
        h_attn = (wV / (Z + 1e-06)).reshape(N, D_MODEL)
        h = h_attn @ Wo + bo
        h = x + h
        h = _batchnorm(h, g1, b1)
        h_in2 = h
        h = jax.nn.relu(h @ W1 + bf1)
        h = h @ W2 + bf2
        h = h_in2 + h
        h = _batchnorm(h, g2, b2)
        return h

    def _L2_gnn_ref(x, edge_index, virt_h, virt_edge_index, Wq, bq, Wk, bk, Wv, bv):
        import jax, jax.numpy as jnp
        import numpy as np
        N_NODES = 100000
        N_EDGES = 12500
        IN_DIM = 128
        NUM_HEADS = 8
        HEAD_DIM = 16
        n = x.shape[0]
        H, D = (NUM_HEADS, HEAD_DIM)
        Q = (x @ Wq + bq).reshape(n, H, D)
        K = (x @ Wk + bk).reshape(n, H, D)
        V = (x @ Wv + bv).reshape(n, H, D)
        src = edge_index[0]
        dst = edge_index[1]
        dot = jnp.sum(K[src] * Q[dst], axis=-1, keepdims=True) / np.sqrt(D).astype(np.float32)
        score = jnp.exp(jnp.clip(dot, -5.0, 5.0))
        msg = V[src] * score
        wV = jax.ops.segment_sum(msg, dst, num_segments=n)
        Z = jax.ops.segment_sum(score, dst, num_segments=n)
        h_out = (wV / (Z + 1e-06)).reshape(n, H * D)
        return h_out

    def _L3_gnn_ref(x, edge_index, edge_attr, W_v, W_wv1, b_wv1, W_wv2, b_wv2, W_wvl, b_wvl, W_c, b_c, W_o, b_o):
        import jax, jax.numpy as jnp
        import numpy as np
        LOG2 = float(np.log(2.0))

        def ssp(x):
            return jax.nn.softplus(x) - LOG2
        N = x.shape[0]
        row, col = (edge_index[0], edge_index[1])
        h_values = x @ W_v.T
        Wv_edge = ssp(edge_attr @ W_wv1.T + b_wv1) @ W_wv2.T + b_wv2
        msg_j = Wv_edge * h_values[col] @ W_wvl.T + b_wvl
        aggr_msg = jax.ops.segment_sum(msg_j, row, num_segments=N)
        out = x @ W_c.T + b_c + aggr_msg
        return ssp(out) @ W_o.T + b_o
    edge_index = jnp.stack([src, dst])
    h = jnp.maximum(_layernorm(x, axis=-1), 0.0)
    x = x + _L0_gnn_ref(h, edge_index, L0_gnn_W1, L0_gnn_b1, L0_gnn_W2, L0_gnn_b2)
    h = jnp.maximum(_layernorm(x, axis=-1), 0.0)
    x = x + _L1_gnn_ref(h, edge_weight1, edge_index, L1_gnn_Wq, L1_gnn_Wk, L1_gnn_We, L1_gnn_Wv, L1_gnn_Wo, L1_gnn_bo, L1_gnn_g1, L1_gnn_b1, L1_gnn_W1, L1_gnn_bf1, L1_gnn_W2, L1_gnn_bf2, L1_gnn_g2, L1_gnn_b2)
    h = jnp.maximum(_layernorm(x, axis=-1), 0.0)
    x = x + _L2_gnn_ref(h, edge_index, L2_gnn_virt_h, L2_gnn_virt_edge_index, L2_gnn_Wq, L2_gnn_bq, L2_gnn_Wk, L2_gnn_bk, L2_gnn_Wv, L2_gnn_bv)
    h = jnp.maximum(_layernorm(x, axis=-1), 0.0)
    x = x + _L3_gnn_ref(h, edge_index, edge_attr_64, L3_gnn_W_v, L3_gnn_W_wv1, L3_gnn_b_wv1, L3_gnn_W_wv2, L3_gnn_b_wv2, L3_gnn_W_wvl, L3_gnn_b_wvl, L3_gnn_W_c, L3_gnn_b_c, L3_gnn_W_o, L3_gnn_b_o)
    return x

_drawn_inputs = setup_inputs


def setup_inputs(seed=0):
    import zlib

    import numpy as np

    out = dict(_drawn_inputs(seed))
    spreads = {'L0_gnn_b1': (0.0, 0.1),
     'L0_gnn_b2': (0.0, 0.1),
     'L1_gnn_bo': (0.0, 2.0),
     'L1_gnn_g1': (1.0, 0.2),
     'L1_gnn_b1': (0.0, 0.714),
     'L1_gnn_bf1': (0.0, 0.374),
     'L1_gnn_bf2': (0.0, 2.0),
     'L1_gnn_g2': (1.0, 0.2),
     'L1_gnn_b2': (0.0, 0.1),
     'L2_gnn_bq': (0.0, 2.0),
     'L2_gnn_bk': (0.0, 2.0),
     'L2_gnn_bv': (0.0, 0.1),
     'L3_gnn_b_wv1': (0.0, 0.8),
     'L3_gnn_b_wv2': (0.0, 0.539),
     'L3_gnn_b_wvl': (0.0, 0.377),
     'L3_gnn_b_c': (0.0, 0.31),
     'L3_gnn_b_o': (0.0, 0.1)}
    factors = {'edge_weight1': 8.0,
     'L1_gnn_Wq': 8.0,
     'L1_gnn_Wk': 8.0,
     'L1_gnn_We': 8.0,
     'L2_gnn_Wq': 2.857}
    for name, (base, spread) in spreads.items():
        noise = np.random.default_rng([zlib.crc32(name.encode()), seed]).standard_normal(out[name].shape)
        drawn = base * np.exp(spread * noise) if base else spread * noise
        out[name] = jnp.asarray(drawn.astype(out[name].dtype))
    for name, factor in factors.items():
        out[name] = (out[name] * factor).astype(out[name].dtype)
    return out
```

```python
from contextlib import ExitStack, contextmanager

import concourse.bass as bass
from concourse import mybir

F32 = mybir.dt.float32
F16 = mybir.dt.float16
I32 = mybir.dt.int32
ALU = mybir.AluOpType
ACT = mybir.ActivationFunctionType
AXIS_X = mybir.AxisListType.X

P = 128
D = 128
ROWS = 8
CHUNK = P * ROWS
LANES = 4
BLOCK = P * LANES
HEADS, HEAD_DIM = 8, 16
SUMS = D + HEADS
SPARE = BLOCK
SLOTS = 6
LN_EPS = 1e-5
BN_EPS = 1e-5
Z_EPS = 1e-6
TABLES = "natural_log_exp_and_others"
WQ_SCALE = 1.0 / HEAD_DIM ** 0.5

MATRICES = ["gcn_w1", "gcn_w2", "l1_k", "l1_v", "l1_q", "l1_o", "ffn_up0", "ffn_up1", "ffn_down0", "ffn_down1",
            "l2_k", "l2_v", "l2_q", "l3_c", "l3_out", "l3_v", "l3_wv2", "l3_wvl"]
COLUMNS = ["l1_bo", "l1_g1", "l1_b1", "l1_bf1a", "l1_bf1b", "l1_bf2", "l1_g2", "l1_b2", "l3_b_wv1", "l3_b_wv2"]
BROADCAST = ["gcn_b1", "gcn_b2", "l1_e", "l3_b_c", "l3_b_o", "l3_b_wvl"]
BIAS_KVQ = ["l2_bk", "l2_bv", "l2_bq"]


def reused(n, slots):
    return not isinstance(n, int) or n >= slots


def walk(eng, count, stages):
    deepest = max(lag for lag, _ in stages)
    first = deepest + SLOTS
    first += (count - first) % SLOTS

    def peeled(t):
        for lag, step in stages:
            if 0 <= t - lag < count:
                step(t - lag, (t - lag) % SLOTS, (t - lag) // SLOTS)

    for t in range(min(first, count + deepest)):
        peeled(t)
    if first < count:
        with eng.Fori(0, (count - first) // SLOTS) as i:
            for u in range(SLOTS):
                for lag, step in stages:
                    c = first + u - lag
                    step(i * SLOTS + c, c % SLOTS, i + c // SLOTS)
    for t in range(max(count, first), count + deepest):
        peeled(t)


def uses(count, s):
    return (count - s + SLOTS - 1) // SLOTS


@contextmanager
def phase(nc, name):
    sems = []
    with ExitStack() as ctx:

        def sbuf(what, shape, dtype=F32):
            return ctx.enter_context(nc.sbuf_tensor(f"{name}_{what}", shape, dtype))

        def psum(what, shape):
            return ctx.enter_context(nc.psum_tensor(f"{name}_{what}", shape, F32))

        def sem(what):
            sems.append(nc.alloc_semaphore(f"{name}_{what}"))
            return sems[-1]

        yield sbuf, psum, sem
        nc.clear_and_free_semaphores(sems)
        nc.all_engine_barrier()


def ln_state(sbuf, psum, sem, rows):
    st = {}
    st["rows"] = rows
    st["stats"] = sbuf("ln_stats", [P, SLOTS, rows, 6])
    st["mean2"] = sbuf("ln_mean2", [P, SLOTS, rows])
    st["gap"] = sbuf("ln_gap", [P, SLOTS, rows])
    st["within"] = sbuf("ln_within", [P, SLOTS, rows])
    st["between"] = sbuf("ln_between", [P, SLOTS, rows])
    st["var"] = sbuf("ln_var", [P, SLOTS, rows])
    st["logvar"] = sbuf("ln_logvar", [P, SLOTS, rows])
    st["scale"] = sbuf("ln_scale", [P, SLOTS, rows])
    st["shift"] = sbuf("ln_shift", [P, SLOTS, rows])
    st["eps"] = sbuf("ln_eps", [P, 1])
    st["stats_done"], st["sums_done"], st["between_done"], st["var_done"], st["log_done"], st["scale_done"], \
        st["shift_done"], st["applied"], st["eps_set"] = (
            sem(f"ln_{x}") for x in ("stats_done", "sums_done", "between_done", "var_done", "log_done",
                                        "scale_done", "shift_done", "applied", "eps_set"))
    return st


def ln_set_eps(st, nc):
    nc.vector.memset(st["eps"][:, :], LN_EPS).then_inc(st["eps_set"], 1)


def ln_measure(st, nc, dve, x, n, s):
    for r in range(st["rows"]):
        last = nc.vector.bn_stats(st["stats"][:, s, r, :], x[:, r, :])
    last.then_inc(st["stats_done"], 1)
    dve.wait_ge(st["stats_done"], n + 1)
    stats = st["stats"][:, s, :, :]
    nc.vector.tensor_tensor(st["gap"][:, s, :], stats[:, :, 1], stats[:, :, 4], ALU.subtract)
    nc.vector.tensor_tensor(st["mean2"][:, s, :], stats[:, :, 1], stats[:, :, 4], ALU.add)
    nc.vector.tensor_tensor(st["within"][:, s, :], stats[:, :, 2], stats[:, :, 5], ALU.add).then_inc(st["sums_done"], 1)
    dve.wait_ge(st["sums_done"], n + 1)
    nc.vector.scalar_tensor_tensor(out=st["between"][:, s, :], in0=st["gap"][:, s, :], scalar=0.25,
                                   in1=st["gap"][:, s, :], op0=ALU.mult, op1=ALU.mult).then_inc(st["between_done"], 1)
    dve.wait_ge(st["between_done"], n + 1)
    if reused(n, SLOTS):
        dve.wait_ge(st["log_done"], n - SLOTS + 1)
    nc.vector.scalar_tensor_tensor(out=st["var"][:, s, :], in0=st["within"][:, s, :], scalar=1.0 / D,
                                   in1=st["between"][:, s, :], op0=ALU.mult, op1=ALU.add).then_inc(st["var_done"], 1)


def ln_deviate(st, nc, act, n, s):
    act.wait_ge(st["var_done"], n + 1)
    nc.scalar.activation(st["logvar"][:, s, :], st["var"][:, s, :], ACT.Ln, bias=st["eps"][:, 0:1]).then_inc(st["log_done"], 1)
    act.wait_ge(st["log_done"], n + 1)
    nc.scalar.activation(st["scale"][:, s, :], st["logvar"][:, s, :], ACT.Exp, scale=-0.5).then_inc(st["scale_done"], 1)


def ln_centre(st, nc, dve, n, s):
    dve.wait_ge(st["scale_done"], n + 1)
    if reused(n, SLOTS):
        dve.wait_ge(st["applied"], n - SLOTS + 1)
    nc.vector.scalar_tensor_tensor(out=st["shift"][:, s, :], in0=st["mean2"][:, s, :], scalar=-0.5,
                                   in1=st["scale"][:, s, :], op0=ALU.mult, op1=ALU.mult).then_inc(st["shift_done"], 1)


def ln_apply(st, nc, act, out, x, n, s):
    act.wait_ge(st["shift_done"], n + 1)
    for r in range(st["rows"]):
        last = nc.scalar.activation(out[:, r, :], x[:, r, :], ACT.Relu, bias=st["shift"][:, s, r:r + 1],
                                    scale=st["scale"][:, s, r:r + 1])
    last.then_inc(st["applied"], 1)


def load_constants(nc, ctx, k, matrices, wv1, columns, broadcast, bias_kvq, node_cols):
    def keep(name, shape, dtype=F32):
        return ctx.enter_context(nc.sbuf_tensor(f"const_{name}", shape, dtype))

    k["matrices"] = keep("matrices", [P, len(MATRICES), D])
    k["wv1"] = keep("wv1", [64, D])
    k["columns"] = keep("columns", [P, len(COLUMNS)])
    k["rows"] = keep("rows", [P, len(BROADCAST), D])
    k["kvq_bias"] = keep("kvq_bias", [1, 3 * D])
    k["ones_row"] = keep("ones_row", [1, P])
    k["identity"] = keep("identity", [P, P])
    k["earlier"] = keep("earlier", [P, BLOCK])
    k["spare_rows"] = keep("spare_rows", [P, LANES])
    k["dis"] = keep("dis", [P, node_cols])
    k["bn"] = keep("bn", [P, 4])
    k["W"] = {m: k["matrices"][:, i, :] for i, m in enumerate(MATRICES)}
    k["col"] = {m: k["columns"][:, i:i + 1] for i, m in enumerate(COLUMNS)}
    k["row"] = {m: k["rows"][:, i, :] for i, m in enumerate(BROADCAST)}
    spare_first = node_cols * P
    with phase(nc, "constants") as (sbuf, psum, sem):
        loaded = sem("loaded")
        filled = sem("filled")
        made = sem("made")
        scaled = sem("scaled")
        with nc.Block() as block:

            @block.sync
            def _(sp):
                sp.dma_start(k["matrices"][:, :, :], matrices.rearrange("p (m d) -> p m d", d=D)).then_inc(loaded, 16)
                sp.dma_start(k["wv1"][:, :], wv1).then_inc(loaded, 16)
                sp.dma_start(k["columns"][:, :], columns).then_inc(loaded, 16)
                sp.dma_start(k["rows"][:, :, :].rearrange("p m d -> p (m d)"), broadcast.to_broadcast([P, len(BROADCAST) * D])).then_inc(loaded, 16)
                sp.dma_start(k["kvq_bias"][:, :], bias_kvq).then_inc(loaded, 16)

            @block.gpsimd
            def _(pool):
                nc.gpsimd.memset(k["identity"][:, :], 0.0)
                nc.gpsimd.memset(k["earlier"][:, :], 1.0).then_inc(filled, 1)
                pool.wait_ge(filled, 1)
                nc.gpsimd.affine_select(out=k["identity"][:, :], in_=k["identity"][:, :], compare_op=ALU.not_equal, fill=1.0,
                                        base=0, pattern=[[-1, P]], channel_multiplier=1)
                nc.gpsimd.affine_select(out=k["earlier"][:, BLOCK - P:], in_=k["earlier"][:, BLOCK - P:], compare_op=ALU.is_gt,
                                        fill=0.0, base=0, pattern=[[-1, P]], channel_multiplier=1)
                nc.gpsimd.iota(k["spare_rows"][:, :], pattern=[[P, LANES]], base=spare_first, channel_multiplier=1,
                               allow_small_or_imprecise_dtypes=True).then_inc(made, 1)

            @block.vector
            def _(dve):
                nc.vector.memset(k["ones_row"][:, :], 1.0)
                dve.wait_ge(loaded, 5 * 16)
                nc.vector.scalar_tensor_tensor(out=k["W"]["l1_q"], in0=k["W"]["l1_q"], scalar=WQ_SCALE, in1=k["row"]["l1_e"],
                                               op0=ALU.mult, op1=ALU.mult)
                nc.vector.tensor_scalar(k["W"]["l2_q"], k["W"]["l2_q"], WQ_SCALE, None, ALU.mult)
                nc.vector.tensor_scalar(k["kvq_bias"][:, 2 * D:], k["kvq_bias"][:, 2 * D:], WQ_SCALE, None, ALU.mult).then_inc(scaled, 1)


def degrees(nc, k, dst_cols, accumulator, last_accumulator, n_blocks, n_chunks):
    cols = n_chunks * ROWS
    half = cols // 2
    with phase(nc, "degrees") as (sbuf, psum, sem):
        keys = sbuf("keys", [P, n_blocks * LANES], I32)
        part_i = sbuf("part_i", [P, n_blocks * LANES], I32)
        high_i = sbuf("high_i", [P, n_blocks * LANES], I32)
        low_i = sbuf("low_i", [P, n_blocks * LANES], I32)
        part = sbuf("part", [P, n_blocks * LANES])
        col = sbuf("col", [P, n_blocks * LANES])
        numbers = sbuf("numbers", [P, cols], F16)
        hot_part = sbuf("hot_part", [P, SLOTS, LANES, P], F16)
        hot_col = sbuf("hot_col", [P, SLOTS, LANES, cols], F16)
        zeros = sbuf("zeros", [P, ROWS * D])
        log_deg = sbuf("log_deg", [P, cols])
        counts = psum("counts", [P, 2, 512])
        keys_in, split, numbered, hot, counted, zeros_set, zeroed, logged, ended = (
            sem(x) for x in ("keys_in", "split", "numbered", "hot", "counted", "zeros_set", "zeroed", "logged", "ended"))
        with nc.Block() as block:

            @block.sync
            def _(sp):
                sp.dma_start(keys[:, :], dst_cols).then_inc(keys_in, 16)
                sp.wait_ge(zeros_set, 1)
                rows = accumulator.rearrange("(c p r) d -> c p (r d)", p=P, r=LANES)
                with sp.Fori(0, accumulator.shape[0] // BLOCK) as i:
                    sp.dma_start(rows[bass.ds(i, 1), :, :].rearrange("c p w -> (c p) w"), zeros[:, 0:LANES * D]).then_inc(zeroed, 16)
                spare = last_accumulator[n_chunks * CHUNK:, :].rearrange("(p r) d -> p (r d)", p=P)
                sp.dma_start(spare, zeros[:, 0:LANES * D]).then_inc(zeroed, 16)
                sp.wait_ge(zeroed, 16 * (accumulator.shape[0] // BLOCK + 1))

            @block.gpsimd
            def _(pool):
                nc.gpsimd.iota(numbers[:, :], pattern=[[1, cols]], base=0, channel_multiplier=0,
                               allow_small_or_imprecise_dtypes=True).then_inc(numbered, 1)

            @block.vector
            def _(dve):
                nc.vector.memset(zeros[:, :], 0.0).then_inc(zeros_set, 1)
                dve.wait_ge(keys_in, 16)
                nc.vector.tensor_scalar(part_i[:, :], keys[:, :], 3, P - 1, ALU.logical_shift_right, ALU.bitwise_and)
                nc.vector.tensor_scalar(high_i[:, :], keys[:, :], 10, 3, ALU.logical_shift_right, ALU.logical_shift_left)
                nc.vector.tensor_scalar(low_i[:, :], keys[:, :], ROWS - 1, None, ALU.bitwise_and).then_inc(split, 1)
                dve.wait_ge(split, 1)
                nc.vector.tensor_copy(part[:, :], part_i[:, :])
                nc.vector.tensor_tensor(col[:, :], high_i[:, :], low_i[:, :], ALU.add).then_inc(split, 1)
                dve.wait_ge(split, 2)
                dve.wait_ge(numbered, 1)

                def one_hot(n, s, turn):
                    if reused(n, SLOTS):
                        dve.wait_ge(counted, n - SLOTS + 1)
                    for lane in range(LANES):
                        at = bass.ds(n * LANES + lane, 1)
                        nc.vector.tensor_scalar(hot_part[:, s, lane, :], numbers[:, 0:P], part[:, at], None, ALU.is_equal)
                        last = nc.vector.tensor_scalar(hot_col[:, s, lane, :], numbers[:, :], col[:, at], None, ALU.is_equal)
                    last.then_inc(hot, 1)

                walk(dve, n_blocks, [(0, one_hot)])

            @block.tensor
            def _(pe):
                def count(n, s, turn):
                    pe.wait_ge(hot, n + 1)
                    for lane in range(LANES):
                        for h in range(2):
                            start = isinstance(n, int) and n == 0 and lane == 0
                            stop = isinstance(n, int) and n == n_blocks - 1 and lane == LANES - 1
                            last = nc.tensor.matmul(counts[:, h, 0:half], hot_part[:, s, lane, :],
                                                    hot_col[:, s, lane, h * half:(h + 1) * half], start=start, stop=stop)
                    last.then_inc(counted, 1)

                walk(pe, n_blocks - 1, [(0, count)])
                count(n_blocks - 1, (n_blocks - 1) % SLOTS, 0)

            @block.scalar
            def _(act):
                act.preload_act_table_set(TABLES)
                act.wait_ge(counted, n_blocks)
                nc.scalar.activation(log_deg[:, :].rearrange("p (h c) -> p h c", h=2), counts[:, :, 0:half], ACT.Ln, bias=1.0).then_inc(logged, 1)
                act.wait_ge(logged, 1)
                nc.scalar.activation(k["dis"][:, :], log_deg[:, :], ACT.Exp, scale=-0.5).then_inc(ended, 1)


def chunk_of(table, n, width=D):
    t = table[0:table.shape[0] // CHUNK * CHUNK, :].rearrange("(c p r) d -> c p (r d)", p=P, r=ROWS)
    return t[bass.ds(n, 1), :, :].rearrange("c p w -> (c p) w")


def norm_nodes(nc, k, x, table, n_chunks):
    with phase(nc, "norm_nodes") as (sbuf, psum, sem):
        xs = sbuf("xs", [P, SLOTS, ROWS, D])
        out = sbuf("out", [P, SLOTS, ROWS, D])
        ln = ln_state(sbuf, psum, sem, ROWS)
        scale = sbuf("scale", [P, SLOTS, ROWS])
        loaded = [sem(f"loaded{s}") for s in range(SLOTS)]
        stored = [sem(f"stored{s}") for s in range(SLOTS)]
        scaled = sem("scaled")
        with nc.Block() as block:

            @block.sync
            def _(sp):
                def load(n, s, turn):
                    if reused(n, SLOTS):
                        sp.wait_ge(ln["applied"], n - SLOTS + 1)
                    sp.dma_start(xs[:, s, :, :].rearrange("p r d -> p (r d)"), chunk_of(x, n)).then_inc(loaded[s], 16)

                def store(n, s, turn):
                    sp.wait_ge(ln["applied"], n + 1)
                    sp.dma_start(chunk_of(table, n), out[:, s, :, :].rearrange("p r d -> p (r d)")).then_inc(stored[s], 16)

                walk(sp, n_chunks, [(0, load), (3, store)])
                for s in range(SLOTS):
                    sp.wait_ge(stored[s], 16 * uses(n_chunks, s))

            @block.vector
            def _(dve):
                ln_set_eps(ln, nc)

                def measure(n, s, turn):
                    dve.wait_ge(loaded[s], turn * 16 + 16)
                    ln_measure(ln, nc, dve, xs[:, s, :, :], n, s)

                def centre(n, s, turn):
                    dve.wait_ge(ln["scale_done"], n + 1)
                    if reused(n, SLOTS):
                        dve.wait_ge(ln["applied"], n - SLOTS + 1)
                    nc.vector.tensor_tensor(scale[:, s, :], ln["scale"][:, s, :], k["dis"][:, bass.ds(n * ROWS, ROWS)], ALU.mult).then_inc(scaled, 1)
                    dve.wait_ge(scaled, n + 1)
                    nc.vector.scalar_tensor_tensor(out=ln["shift"][:, s, :], in0=ln["mean2"][:, s, :], scalar=-0.5,
                                                   in1=scale[:, s, :], op0=ALU.mult, op1=ALU.mult).then_inc(ln["shift_done"], 1)

                walk(dve, n_chunks, [(1, centre), (0, measure)])

            @block.scalar
            def _(act):
                act.preload_act_table_set(TABLES)
                act.wait_ge(ln["eps_set"], 1)

                def deviate(n, s, turn):
                    if reused(n, SLOTS):
                        act.wait_ge(scaled, n - SLOTS + 1)
                    ln_deviate(ln, nc, act, n, s)

                def apply(n, s, turn):
                    if reused(n, SLOTS):
                        act.wait_ge(stored[s], turn * 16)
                    act.wait_ge(ln["shift_done"], n + 1)
                    for r in range(ROWS):
                        last = nc.scalar.activation(out[:, s, r, :], xs[:, s, r, :], ACT.Relu, bias=ln["shift"][:, s, r:r + 1],
                                                    scale=scale[:, s, r:r + 1])
                    last.then_inc(ln["applied"], 1)

                walk(act, n_chunks, [(1, apply), (0, deviate)])


def merge_state(sbuf, psum, sem, width):
    st = {}
    st["width"] = width
    st["key_rows"] = sbuf("key_rows", [P, SLOTS, BLOCK], I32)
    st["key"] = sbuf("key", [P, SLOTS, LANES])
    st["same"] = sbuf("same", [P, 2, LANES, BLOCK])
    st["masked"] = sbuf("masked", [P, LANES, BLOCK], F16)
    st["before"] = sbuf("before", [P, SLOTS, LANES])
    st["away"] = sbuf("away", [P, SLOTS, LANES])
    st["step"] = sbuf("step", [P, SLOTS, LANES])
    st["target"] = sbuf("target", [P, SLOTS, LANES], I32)
    st["sums"] = sbuf("sums", [P, 2, LANES, width])
    st["psum"] = psum("merge_psum", [P, 2, 512])
    st["keys_in"] = [sem(f"keys_in{s}") for s in range(SLOTS)]
    st["key_ready"], st["same_ready"], st["before_ready"], st["step_ready"], st["target_ready"], st["merged"], \
        st["sums_ready"], st["scattered"] = (
            sem(x) for x in ("key_ready", "same_ready", "before_ready", "step_ready", "target_ready", "merged",
                                "sums_ready", "scattered"))
    return st


def merge_load(st, sp, key_rows, n, s):
    sp.dma_start(st["key_rows"][:, s, :], key_rows[bass.ds(n, 1), :].to_broadcast([P, BLOCK])).then_inc(st["keys_in"][s], 16)


def merge_compare(st, nc, dve, k, key_cols, n, s, turn):
    dve.wait_ge(st["keys_in"][s], turn * 16 + 16)
    nc.vector.tensor_copy(st["key"][:, s, :], key_cols).then_inc(st["key_ready"], 1)
    dve.wait_ge(st["key_ready"], n + 1)
    if reused(n, 2):
        dve.wait_ge(st["merged"], n - 1)
    for lane in range(LANES):
        upto = (lane + 1) * P
        last = nc.vector.tensor_scalar(st["same"][:, s % 2, lane, 0:upto], st["key_rows"][:, s, 0:upto],
                                       st["key"][:, s, lane:lane + 1], None, ALU.is_equal)
    last.then_inc(st["same_ready"], 1)
    dve.wait_ge(st["same_ready"], n + 1)
    for lane in range(LANES):
        upto = (lane + 1) * P
        last = nc.vector.tensor_tensor_reduce(out=st["masked"][:, lane, 0:upto], in0=st["same"][:, s % 2, lane, 0:upto],
                                              in1=k["earlier"][:, BLOCK - upto:], scale=1.0, scalar=0.0, op0=ALU.mult,
                                              op1=ALU.add, accum_out=st["before"][:, s, lane:lane + 1])
    nc.vector.tensor_tensor(st["away"][:, s, :], k["spare_rows"][:, :], st["key"][:, s, :], ALU.subtract).then_inc(st["before_ready"], 1)
    dve.wait_ge(st["before_ready"], n + 1)
    nc.vector.scalar_tensor_tensor(out=st["step"][:, s, :], in0=st["before"][:, s, :], scalar=1.0,
                                   in1=st["away"][:, s, :], op0=ALU.min, op1=ALU.mult).then_inc(st["step_ready"], 1)
    dve.wait_ge(st["step_ready"], n + 1)
    if reused(n, SLOTS):
        dve.wait_ge(st["scattered"], (n - SLOTS + 1) * LANES * 16)
    nc.vector.tensor_tensor(st["target"][:, s, :], st["step"][:, s, :], st["key"][:, s, :], ALU.add).then_inc(st["target_ready"], 1)


def merge_merge(st, nc, pe, message, n, s):
    pe.wait_ge(st["same_ready"], n + 1)
    if reused(n, 1):
        pe.wait_ge(st["sums_ready"], n)
    for to in range(LANES):
        at = (to % 2) * st["width"]
        for lane in range(to, LANES):
            last = nc.tensor.matmul(st["psum"][:, to // 2, at:at + st["width"]],
                                    st["same"][:, s % 2, lane, to * P:(to + 1) * P], message(lane),
                                    start=lane == to, stop=lane == LANES - 1)
    last.then_inc(st["merged"], 1)


def merge_keep(st, nc, act, n, s):
    act.wait_ge(st["merged"], n + 1)
    if reused(n, 2):
        act.wait_ge(st["scattered"], (n - 1) * LANES * 16)
    nc.scalar.activation(st["sums"][:, s % 2, :, :].rearrange("p (b l) w -> p b (l w)", b=2),
                         st["psum"][:, :, 0:2 * st["width"]], ACT.Copy).then_inc(st["sums_ready"], 1)


def merge_scatter(st, nc, pool, accumulator, n, s):
    pool.wait_ge(st["sums_ready"], n + 1)
    pool.wait_ge(st["target_ready"], n + 1)
    if reused(n, 1):
        pool.wait_ge(st["scattered"], n * LANES * 16)
    pool.sem_inc(st["pool_passed"])
    for lane in range(LANES):
        pool.indirect_dma_start(accumulator, bass.IndirectOffsetOnAxis(ap=st["target"][:, s, lane:lane + 1], axis=0),
                                st["sums"][:, s % 2, lane, :], None, compute_op=ALU.add).then_inc(st["scattered"], 16)


def gather(pool, rows, table, numbers, lanes, done):
    for lane in range(lanes):
        pool.indirect_dma_start(rows[:, lane, :], None, table, bass.IndirectOffsetOnAxis(ap=numbers[:, lane:lane + 1], axis=0)).then_inc(done, 16)


def zero_state(sbuf, psum, sem, accumulator, n_blocks):
    st = {}
    st["acc"] = accumulator
    st["n_blocks"] = n_blocks
    if accumulator is not None:
        st["rows"], st["width"] = accumulator.shape
        st["part"] = st["rows"] // BLOCK
        st["per"] = -(-st["part"] // n_blocks)
        st["zeros"] = sbuf("zeros", [P, LANES * st["width"]])
        st["zeros_set"] = sem("zeros_set")
        st["zeroed"] = sem("zeroed")
    return st


def zero_fill(st, nc):
    if st["acc"] is not None:
        nc.vector.memset(st["zeros"][:, :], 0.0).then_inc(st["zeros_set"], 1)


def zero_begin(st, sp):
    if st["acc"] is not None:
        sp.wait_ge(st["zeros_set"], 1)


def zero_step(st, sp, first, count):
    if st["acc"] is not None:
        parts = st["acc"].rearrange("(c p r) d -> c p (r d)", p=P, r=LANES)
        for c in range(count):
            sp.dma_start(parts[bass.ds(first + c, 1), :, :].rearrange("c p w -> (c p) w"), st["zeros"][:, :]).then_inc(st["zeroed"], 16)


def zero_end(st, sp):
    if st["acc"] is not None:
        done = st["part"] // st["n_blocks"] * st["n_blocks"]
        zero_step(st, sp, done, st["part"] - done)
        sp.wait_ge(st["zeroed"], 16 * st["part"])


def sum_over_edges(nc, k, name, ends, key_rows, table, accumulator, zero_next, n_blocks):
    with phase(nc, name) as (sbuf, psum, sem):
        end = sbuf("end", [P, SLOTS, 2 * LANES], I32)
        rows = sbuf("rows", [P, SLOTS, LANES, D])
        ends_in = [sem(f"ends_in{s}") for s in range(SLOTS)]
        gathered = [sem(f"gathered{s}") for s in range(SLOTS)]
        mg = merge_state(sbuf, psum, sem, D)
        mg["pool_passed"] = sem("pool_passed")
        zero = zero_state(sbuf, psum, sem, zero_next, n_blocks)
        with nc.Block() as block:

            @block.sync
            def _(sp):
                zero_begin(zero, sp)

                def load(n, s, turn):
                    if reused(n, SLOTS):
                        sp.wait_ge(mg["scattered"], (n - SLOTS + 1) * LANES * 16)
                    sp.dma_start(end[:, s, :], ends[bass.ds(n, 1), :, :].rearrange("b p w -> (b p) w")).then_inc(ends_in[s], 16)
                    merge_load(mg, sp, key_rows, n, s)

                def clear(n, s, turn):
                    if zero["acc"] is not None:
                        each = zero["part"] // n_blocks
                        zero_step(zero, sp, n * each, each)

                walk(sp, n_blocks, [(0, load), (0, clear)])
                zero_end(zero, sp)

            @block.gpsimd
            def _(pool):
                def fetch(n, s, turn):
                    if reused(n, SLOTS):
                        pool.wait_ge(mg["merged"], n - SLOTS + 1)
                    pool.wait_ge(ends_in[s], turn * 16 + 16)
                    pool.sem_inc(mg["pool_passed"])
                    gather(pool, rows[:, s, :, :], table, end[:, s, 0:LANES], LANES, gathered[s])

                def add(n, s, turn):
                    merge_scatter(mg, nc, pool, accumulator, n, s)

                walk(pool, n_blocks, [(0, fetch), (1, add)])
                pool.wait_ge(mg["scattered"], n_blocks * LANES * 16)

            @block.vector
            def _(dve):
                zero_fill(zero, nc)

                def compare(n, s, turn):
                    dve.wait_ge(ends_in[s], turn * 16 + 16)
                    merge_compare(mg, nc, dve, k, end[:, s, LANES:], n, s, turn)

                walk(dve, n_blocks, [(0, compare)])

            @block.tensor
            def _(pe):
                def merge(n, s, turn):
                    pe.wait_ge(gathered[s], (turn + 1) * LANES * 16)
                    merge_merge(mg, nc, pe, lambda lane: rows[:, s, lane, :], n, s)

                walk(pe, n_blocks, [(0, merge)])

            @block.scalar
            def _(act):
                walk(act, n_blocks, [(0, lambda n, s, turn: merge_keep(mg, nc, act, n, s))])


def flat(tile):
    return tile.rearrange("p r d -> p (r d)")


def banks(psum):
    return psum.rearrange("p b (r d) -> p (b r) d", d=D)


def gcn_nodes(nc, k, name, accumulator, table, weight, bias, x, out, n_chunks):
    with phase(nc, name) as (sbuf, psum, sem):
        acc = sbuf("acc", [P, SLOTS, ROWS, D])
        tab = sbuf("tab", [P, SLOTS, ROWS, D])
        xs = sbuf("xs", [P, SLOTS, ROWS, D]) if x is not None else None
        total_T = sbuf("total_T", [P, 2, ROWS, D])
        y = sbuf("y", [P, 2, ROWS, D])
        result = sbuf("result", [P, SLOTS, ROWS, D])
        turned = [psum(f"turned{s}", [P, 2, 512]) for s in range(2)]
        product = [psum(f"product{s}", [P, 2, 512]) for s in range(2)]
        loaded = [sem(f"loaded{s}") for s in range(SLOTS)]
        stored = [sem(f"stored{s}") for s in range(SLOTS)]
        summed, transposed, copied, multiplied, biased, finished = (
            sem(s) for s in ("summed", "transposed", "copied", "multiplied", "biased", "finished"))
        loads = 2 + (x is not None)
        with nc.Block() as block:

            @block.sync
            def _(sp):
                def load(n, s, turn):
                    if reused(n, SLOTS):
                        sp.wait_ge(finished if x is not None else summed, n - SLOTS + 1)
                    sp.dma_start(flat(acc[:, s, :, :]), chunk_of(accumulator, n)).then_inc(loaded[s], 16)
                    sp.dma_start(flat(tab[:, s, :, :]), chunk_of(table, n)).then_inc(loaded[s], 16)
                    if x is not None:
                        sp.dma_start(flat(xs[:, s, :, :]), chunk_of(x, n)).then_inc(loaded[s], 16)

                def store(n, s, turn):
                    sp.wait_ge(finished, n + 1)
                    sp.dma_start(chunk_of(out, n), flat(result[:, s, :, :])).then_inc(stored[s], 16)

                walk(sp, n_chunks, [(0, load), (4, store)])
                for s in range(SLOTS):
                    sp.wait_ge(stored[s], 16 * uses(n_chunks, s))

            @block.vector
            def _(dve):
                def total(n, s, turn):
                    dve.wait_ge(loaded[s], (turn + 1) * 16 * loads)
                    if reused(n, SLOTS):
                        dve.wait_ge(transposed, n - SLOTS + 1)
                    nc.vector.tensor_tensor(acc[:, s, :, :], acc[:, s, :, :], tab[:, s, :, :], ALU.add).then_inc(summed, 1)

                def add_bias(n, s, turn):
                    dve.wait_ge(multiplied, n + 1)
                    if reused(n, 2) and x is None:
                        dve.wait_ge(finished, n - 1)
                    for r in range(ROWS):
                        last = nc.vector.scalar_tensor_tensor(out=y[:, s % 2, r, :], in0=banks(product[s % 2][:, :, :])[:, r, :],
                                                              scalar=k["dis"][:, bass.ds(n * ROWS + r, 1)], in1=bias,
                                                              op0=ALU.mult, op1=ALU.add)
                    last.then_inc(biased, 1)
                    if x is not None:
                        dve.wait_ge(biased, n + 1)
                        if reused(n, SLOTS):
                            dve.wait_ge(stored[s], turn * 16)
                        nc.vector.scalar_tensor_tensor(out=flat(result[:, s, :, :]), in0=flat(y[:, s % 2, :, :]), scalar=0.0,
                                                       in1=flat(xs[:, s, :, :]), op0=ALU.max, op1=ALU.add).then_inc(finished, 1)

                walk(dve, n_chunks, [(2, add_bias), (0, total)])

            @block.tensor
            def _(pe):
                def turn_over(n, s, turn):
                    pe.wait_ge(summed, n + 1)
                    if reused(n, 2):
                        pe.wait_ge(copied, n - 1)
                    for r in range(ROWS):
                        last = nc.tensor.transpose(banks(turned[s % 2][:, :, :])[:, r, :], acc[:, s, r, :], k["identity"][:, :])
                    last.then_inc(transposed, 1)

                def multiply(n, s, turn):
                    pe.wait_ge(copied, n + 1)
                    if reused(n, 2):
                        pe.wait_ge(biased, n - 1)
                    for r in range(ROWS):
                        last = nc.tensor.matmul(banks(product[s % 2][:, :, :])[:, r, :], total_T[:, s % 2, r, :], weight,
                                                start=True, stop=True)
                    last.then_inc(multiplied, 1)

                walk(pe, n_chunks, [(1, multiply), (0, turn_over)])

            @block.scalar
            def _(act):
                def copy(n, s, turn):
                    act.wait_ge(transposed, n + 1)
                    if reused(n, 2):
                        act.wait_ge(multiplied, n - 1)
                    nc.scalar.activation(flat(total_T[:, s % 2, :, :]), turned[s % 2][:, :, :].rearrange("p b w -> p (b w)"),
                                         ACT.Copy).then_inc(copied, 1)

                def rectify(n, s, turn):
                    act.wait_ge(biased, n + 1)
                    if reused(n, SLOTS):
                        act.wait_ge(stored[s], turn * 16)
                    for r in range(ROWS):
                        last = nc.scalar.activation(result[:, s, r, :], y[:, s % 2, r, :], ACT.Relu,
                                                    scale=k["dis"][:, bass.ds(n * ROWS + r, 1)])
                    last.then_inc(finished, 1)

                walk(act, n_chunks, ([(2, rectify)] if x is None else []) + [(0, copy)])


def attention_over_edges(nc, k, name, ends, key_rows, edge_weight, nodes, weights, bias, accumulator, zero_next, n_blocks):
    with phase(nc, name) as (sbuf, psum, sem):
        end = sbuf("end", [P, SLOTS, 2 * LANES], I32)
        rows = sbuf("rows", [P, SLOTS, 2 * LANES, D])
        normed = sbuf("normed", [P, 2 * LANES, D])
        normed_T = sbuf("normed_T", [P, 2 * LANES, D])
        query = sbuf("query", [P, LANES, D])
        terms = sbuf("terms", [P, LANES, D])
        dots = sbuf("dots", [P, LANES, HEADS])
        weighted = sbuf("weighted", [P, LANES, HEADS])
        clipped = sbuf("clipped", [P, LANES, HEADS])
        message = sbuf("message", [P, 2, LANES, SUMS])
        factor = sbuf("factor", [P, SLOTS, LANES])
        turned = psum("turned", [P, 2, 512])
        kvq = psum("kvq", [P, LANES, 512])
        ends_in = [sem(f"ends_in{s}") for s in range(SLOTS)]
        gathered = [sem(f"gathered{s}") for s in range(SLOTS)]
        transposed, copied, projected, query_ready, terms_ready, dots_ready, weighted_ready, clipped_ready, score_ready, \
            message_ready = (sem(x) for x in (
                "transposed", "copied", "projected", "query_ready", "terms_ready", "dots_ready", "weighted_ready",
                "clipped_ready", "score_ready", "message_ready"))
        ln = ln_state(sbuf, psum, sem, 2 * LANES)
        mg = merge_state(sbuf, psum, sem, SUMS)
        mg["pool_passed"] = sem("pool_passed")
        zero = zero_state(sbuf, psum, sem, zero_next, n_blocks)
        end_loads = 1 + (edge_weight is not None)
        w_at = MATRICES.index(weights)
        w_kv = k["matrices"][:, w_at:w_at + 2, :].rearrange("p m d -> p (m d)")
        w_q = k["matrices"][:, w_at + 2, :]
        with nc.Block() as block:

            @block.sync
            def _(sp):
                zero_begin(zero, sp)

                def load(n, s, turn):
                    if reused(n, SLOTS):
                        sp.wait_ge(mg["target_ready"], n - SLOTS + 1)
                    sp.dma_start(end[:, s, :], ends[bass.ds(n, 1), :, :].rearrange("b p w -> (b p) w")).then_inc(ends_in[s], 16)
                    if edge_weight is not None:
                        sp.dma_start(factor[:, s, :], edge_weight[bass.ds(n, 1), :, :].rearrange("b p w -> (b p) w")).then_inc(ends_in[s], 16)
                    merge_load(mg, sp, key_rows, n, s)

                def clear(n, s, turn):
                    if zero["acc"] is not None:
                        each = zero["part"] // n_blocks
                        zero_step(zero, sp, n * each, each)

                walk(sp, n_blocks, [(0, load), (0, clear)])
                zero_end(zero, sp)

            @block.gpsimd
            def _(pool):
                def fetch(n, s, turn):
                    if reused(n, SLOTS):
                        pool.wait_ge(ln["applied"], n - SLOTS + 1)
                    pool.wait_ge(ends_in[s], (turn + 1) * 16 * end_loads)
                    pool.sem_inc(mg["pool_passed"])
                    gather(pool, rows[:, s, :, :], nodes, end[:, s, :], 2 * LANES, gathered[s])

                walk(pool, n_blocks, [(0, fetch), (5, lambda n, s, turn: merge_scatter(mg, nc, pool, accumulator, n, s))])
                pool.wait_ge(mg["scattered"], n_blocks * LANES * 16)

            @block.vector
            def _(dve):
                zero_fill(zero, nc)
                ln_set_eps(ln, nc)

                def measure(n, s, turn):
                    dve.wait_ge(gathered[s], (turn + 1) * 2 * LANES * 16)
                    ln_measure(ln, nc, dve, rows[:, s, :, :], n, s)

                def compare(n, s, turn):
                    dve.wait_ge(ends_in[s], (turn + 1) * 16 * end_loads)
                    merge_compare(mg, nc, dve, k, end[:, s, LANES:], n, s, turn)

                def attend(n, s, turn):
                    dve.wait_ge(query_ready, n + 1)
                    nc.vector.tensor_tensor(terms[:, :, :], kvq[:, :, 0:D], query[:, :, :], ALU.mult).then_inc(terms_ready, 1)
                    dve.wait_ge(terms_ready, n + 1)
                    nc.vector.tensor_reduce(dots[:, :, :].rearrange("p l h -> p (l h)"),
                                            terms[:, :, :].rearrange("p l (h d) -> p (l h) d", d=HEAD_DIM),
                                            AXIS_X, ALU.add).then_inc(dots_ready, 1)
                    dve.wait_ge(dots_ready, n + 1)
                    source = dots
                    if edge_weight is not None:
                        nc.vector.tensor_tensor(weighted[:, :, :], dots[:, :, :],
                                                factor[:, s, :].unsqueeze(2).to_broadcast([P, LANES, HEADS]),
                                                ALU.mult).then_inc(weighted_ready, 1)
                        dve.wait_ge(weighted_ready, n + 1)
                        source = weighted
                    if reused(n, 1):
                        dve.wait_ge(score_ready, n)
                    nc.vector.tensor_scalar(clipped[:, :, :], source[:, :, :], 5.0, -5.0, ALU.min, ALU.max).then_inc(clipped_ready, 1)
                    dve.wait_ge(score_ready, n + 1)
                    m = message[:, s % 2, :, :]
                    for lane in range(LANES):
                        last = nc.vector.tensor_tensor(m[:, lane, 0:D].rearrange("p (h d) -> p h d", d=HEAD_DIM),
                                                       kvq[:, lane, D:2 * D].rearrange("p (h d) -> p h d", d=HEAD_DIM),
                                                       m[:, lane, D:SUMS].unsqueeze(2).to_broadcast([P, HEADS, HEAD_DIM]), ALU.mult)
                    last.then_inc(message_ready, 1)

                walk(dve, n_blocks, [(3, attend), (1, measure), (3, compare), (1, lambda n, s, turn: ln_centre(ln, nc, dve, n, s))])

            @block.tensor
            def _(pe):
                def merge(n, s, turn):
                    pe.wait_ge(message_ready, n + 1)
                    merge_merge(mg, nc, pe, lambda lane: message[:, s % 2, lane, :], n, s)

                def project(n, s, turn):
                    pe.wait_ge(copied, n + 1)
                    if reused(n, 1):
                        pe.wait_ge(message_ready, n)
                    for lane in range(LANES):
                        if bias is not None:
                            nc.tensor.matmul(kvq[:, lane, 0:3 * D], k["ones_row"][:, :], bias, start=True, stop=False)
                        nc.tensor.matmul(kvq[:, lane, 0:2 * D], normed_T[:, lane, :], w_kv, start=bias is None, stop=bias is None)
                        last = nc.tensor.matmul(kvq[:, lane, 2 * D:3 * D], normed_T[:, LANES + lane, :], w_q,
                                                start=bias is None, stop=True)
                    last.then_inc(projected, 1)

                def turn_over(n, s, turn):
                    pe.wait_ge(ln["applied"], n + 1)
                    for r in range(2 * LANES):
                        last = nc.tensor.transpose(banks(turned[:, :, :])[:, r, :], normed[:, r, :], k["identity"][:, :])
                    last.then_inc(transposed, 1)

                walk(pe, n_blocks, [(4, merge), (2, project), (1, turn_over)])

            @block.scalar
            def _(act):
                act.preload_act_table_set(TABLES)
                act.wait_ge(ln["eps_set"], 1)

                def copy_query(n, s, turn):
                    act.wait_ge(projected, n + 1)
                    if reused(n, 1):
                        act.wait_ge(terms_ready, n)
                    nc.scalar.activation(query[:, :, :], kvq[:, :, 2 * D:3 * D], ACT.Copy).then_inc(query_ready, 1)

                def score(n, s, turn):
                    act.wait_ge(clipped_ready, n + 1)
                    if reused(n, 2):
                        act.wait_ge(mg["merged"], n - 1)
                    nc.scalar.activation(message[:, s % 2, :, D:SUMS], clipped[:, :, :], ACT.Exp).then_inc(score_ready, 1)

                def norm(n, s, turn):
                    if reused(n, 1):
                        act.wait_ge(transposed, n)
                    ln_apply(ln, nc, act, normed[:, :, :], rows[:, s, :, :], n, s)

                def copy(n, s, turn):
                    act.wait_ge(transposed, n + 1)
                    if reused(n, 1):
                        act.wait_ge(projected, n)
                    nc.scalar.activation(flat(normed_T[:, :, :]), turned[:, :, :].rearrange("p b w -> p (b w)"), ACT.Copy).then_inc(copied, 1)

                walk(act, n_blocks, [(3, score), (4, lambda n, s, turn: merge_keep(mg, nc, act, n, s)),
                                     (1, lambda n, s, turn: ln_deviate(ln, nc, act, n, s)), (1, norm), (2, copy_query), (1, copy)])


"""Mean and variance of each feature over all nodes, features on the partitions, and the affine map
of the batch norm that follows from them."""


def bn_state(sbuf, psum, sem, halves):
    st = {}
    st["halves"] = halves
    st["part"] = sbuf("bn_part", [P, SLOTS, 2, 6])
    st["parts"] = sbuf("bn_parts", [P, halves, 6])
    st["moments"] = sbuf("bn_moments", [P, 2])
    st["logvar"] = sbuf("bn_logvar", [P, 1])
    st["rstd"] = sbuf("bn_rstd", [P, 1])
    st["shift"] = sbuf("bn_shift", [P, 1])
    st["eps"] = sbuf("bn_eps", [P, 1])
    st["part_done"], st["parts_done"], st["eps_set"], st["moments_done"], st["log_done"], st["rstd_done"], st["scale_done"], \
        st["shift_done"] = (sem(f"bn_{x}") for x in (
            "part_done", "parts_done", "eps_set", "moments_done", "log_done", "rstd_done", "scale_done", "shift_done"))
    return st


def bn_add(st, nc, dve, pieces, n, s):
    for i, piece in enumerate(pieces):
        last = nc.vector.bn_stats(st["part"][:, s, i, :], piece)
    last.then_inc(st["part_done"], 1)
    dve.wait_ge(st["part_done"], n + 1)
    c = len(pieces)
    nc.vector.tensor_scalar(st["parts"][:, bass.ds(n * c, c), :], st["part"][:, s, 0:c, :], 1.0, None, ALU.mult).then_inc(st["parts_done"], 1)


def bn_finish_vector(st, nc, dve, tiles, gain, offset, scale_out, shift_out):
    dve.wait_ge(st["parts_done"], tiles)
    nc.vector.bn_aggr(st["moments"][:, :], st["parts"][:, :, :].rearrange("p c w -> p (c w)")).then_inc(st["moments_done"], 1)
    dve.wait_ge(st["rstd_done"], 1)
    nc.vector.tensor_tensor(scale_out, st["rstd"][:, :], gain, ALU.mult).then_inc(st["scale_done"], 1)
    dve.wait_ge(st["scale_done"], 1)
    nc.vector.tensor_tensor(st["shift"][:, :], st["moments"][:, 0:1], scale_out, ALU.mult).then_inc(st["shift_done"], 1)
    dve.wait_ge(st["shift_done"], 1)
    nc.vector.tensor_tensor(shift_out, offset, st["shift"][:, :], ALU.subtract).then_inc(st["shift_done"], 1)


def bn_finish_scalar(st, nc, act):
    act.wait_ge(st["moments_done"], 1)
    nc.scalar.activation(st["logvar"][:, :], st["moments"][:, 1:2], ACT.Ln, bias=st["eps"][:, 0:1]).then_inc(st["log_done"], 1)
    act.wait_ge(st["log_done"], 1)
    nc.scalar.activation(st["rstd"][:, :], st["logvar"][:, :], ACT.Exp, scale=-0.5).then_inc(st["rstd_done"], 1)


def heads_state(sbuf, psum, sem):
    st = {}
    st["weight"] = sbuf("head_weight", [P, SLOTS, ROWS, HEADS])
    st["inverse"] = sbuf("head_inverse", [P, SLOTS, ROWS, HEADS])
    st["weight_done"], st["inverse_done"], st["mean_done"] = (sem(f"head_{x}") for x in ("weight_done", "inverse_done", "mean_done"))
    return st


def heads_divide(st, nc, dve, out, sums, n, s):
    nc.vector.tensor_scalar(st["weight"][:, s, :, :], sums[:, :, D:SUMS], Z_EPS, None, ALU.add).then_inc(st["weight_done"], 1)
    dve.wait_ge(st["weight_done"], n + 1)
    nc.vector.reciprocal(st["inverse"][:, s, :, :], st["weight"][:, s, :, :]).then_inc(st["inverse_done"], 1)
    dve.wait_ge(st["inverse_done"], n + 1)
    nc.vector.tensor_tensor(out.rearrange("p r (h d) -> p r h d", d=HEAD_DIM),
                            sums[:, :, 0:D].rearrange("p r (h d) -> p r h d", d=HEAD_DIM),
                            st["inverse"][:, s, :, :].unsqueeze(3).to_broadcast([P, ROWS, HEADS, HEAD_DIM]),
                            ALU.mult).then_inc(st["mean_done"], 1)


def column_chunk(table, n, width=CHUNK):
    return table[bass.ds(n, 1), :, :].rearrange("c p w -> (c p) w")


def attention1_nodes(nc, k, x, sums, y_T, n_chunks, last_valid):
    with phase(nc, "l1_nodes") as (sbuf, psum, sem):
        xs = sbuf("xs", [P, SLOTS, ROWS, D])
        acc = sbuf("acc", [P, SLOTS, ROWS, SUMS])
        att = sbuf("att", [P, 2, ROWS, D])
        att_T = sbuf("att_T", [P, 2, 2, 512])
        normed = sbuf("normed", [P, 2, ROWS, D])
        y = sbuf("y", [P, SLOTS, CHUNK])
        turned = [psum(f"turned{s}", [P, 2, 512]) for s in range(2)]
        total = [psum(f"total{s}", [P, 2, 512]) for s in range(2)]
        loaded = [sem(f"loaded{s}") for s in range(SLOTS)]
        stored = [sem(f"stored{s}") for s in range(SLOTS)]
        transposed, copied, totalled, y_ready = (sem(x) for x in ("transposed", "copied", "totalled", "y_ready"))
        ln = ln_state(sbuf, psum, sem, ROWS)
        heads = heads_state(sbuf, psum, sem)
        bn = bn_state(sbuf, psum, sem, 2 * n_chunks)
        with nc.Block() as block:

            @block.sync
            def _(sp):
                def load(n, s, turn):
                    if reused(n, SLOTS):
                        sp.wait_ge(ln["applied"], n - SLOTS + 1)
                    sp.dma_start(flat(xs[:, s, :, :]), chunk_of(x, n)).then_inc(loaded[s], 16)
                    sp.dma_start(flat(acc[:, s, :, :]), chunk_of(sums, n)).then_inc(loaded[s], 16)

                def store(n, s, turn):
                    sp.wait_ge(y_ready, n + 1)
                    sp.dma_start(column_chunk(y_T, n), y[:, s, :]).then_inc(stored[s], 16)

                walk(sp, n_chunks, [(0, load), (4, store)])
                for s in range(SLOTS):
                    sp.wait_ge(stored[s], 16 * uses(n_chunks, s))

            @block.vector
            def _(dve):
                nc.vector.memset(bn["eps"][:, :], BN_EPS)
                ln_set_eps(ln, nc)

                def divide(n, s, turn):
                    dve.wait_ge(loaded[s], (turn + 1) * 32)
                    if reused(n, 2):
                        dve.wait_ge(transposed, n - 1)
                    heads_divide(heads, nc, dve, att[:, s % 2, :, :], acc[:, s, :, :], n, s)
                    ln_measure(ln, nc, dve, xs[:, s, :, :], n, s)

                def stats(n, s, turn):
                    dve.wait_ge(y_ready, n + 1)
                    halves = [y[:, s, h * 512:(h + 1) * 512] for h in range(2)]
                    if isinstance(n, int) and n == n_chunks - 1:
                        halves = [h.rearrange("p (r q) -> p r q", q=P)[:, :, 0:last_valid] for h in halves]
                    bn_add(bn, nc, dve, halves, n, s)

                walk(dve, n_chunks, [(1, lambda n, s, turn: ln_centre(ln, nc, dve, n, s)), (0, divide), (3, stats)])
                bn_finish_vector(bn, nc, dve, n_chunks, k["col"]["l1_g1"], k["col"]["l1_b1"], k["bn"][:, 0:1], k["bn"][:, 1:2])

            @block.tensor
            def _(pe):
                def turn_over(n, s, turn):
                    pe.wait_ge(heads["mean_done"], n + 1)
                    if reused(n, 2):
                        pe.wait_ge(copied, n - 1)
                    for r in range(ROWS):
                        last = nc.tensor.transpose(banks(turned[s % 2][:, :, :])[:, r, :], att[:, s % 2, r, :], k["identity"][:, :])
                    last.then_inc(transposed, 1)

                def add_up(n, s, turn):
                    pe.wait_ge(copied, n + 1)
                    pe.wait_ge(ln["applied"], n + 1)
                    if reused(n, 2):
                        pe.wait_ge(y_ready, n - 1)
                    for h in range(2):
                        nc.tensor.matmul(total[s % 2][:, h, :], k["W"]["l1_o"], att_T[:, s % 2, h, :], start=True, stop=False)
                        for r in range(LANES):
                            last = nc.tensor.matmul(total[s % 2][:, h, r * P:(r + 1) * P], normed[:, s % 2, h * LANES + r, :],
                                                    k["identity"][:, :], start=False, stop=r == LANES - 1)
                    last.then_inc(totalled, 1)

                walk(pe, n_chunks, [(2, add_up), (0, turn_over)])

            @block.scalar
            def _(act):
                act.preload_act_table_set(TABLES)
                act.wait_ge(ln["eps_set"], 1)

                def copy(n, s, turn):
                    act.wait_ge(transposed, n + 1)
                    if reused(n, 2):
                        act.wait_ge(totalled, n - 1)
                    nc.scalar.activation(att_T[:, s % 2, :, :], turned[s % 2][:, :, :], ACT.Copy).then_inc(copied, 1)

                def norm(n, s, turn):
                    if reused(n, 2):
                        act.wait_ge(totalled, n - 1)
                    ln_apply(ln, nc, act, normed[:, s % 2, :, :], xs[:, s, :, :], n, s)

                def take(n, s, turn):
                    act.wait_ge(totalled, n + 1)
                    if reused(n, SLOTS):
                        act.wait_ge(stored[s], turn * 16)
                        act.wait_ge(bn["part_done"], n - SLOTS + 1)
                    nc.scalar.activation(y[:, s, :], total[s % 2][:, :, :].rearrange("p b w -> p (b w)"), ACT.Identity,
                                         bias=k["col"]["l1_bo"]).then_inc(y_ready, 1)

                walk(act, n_chunks, [(1, norm), (2, take), (0, lambda n, s, turn: ln_deviate(ln, nc, act, n, s)), (0, copy)])
                bn_finish_scalar(bn, nc, act)


def feed_forward(nc, k, y_T, z_T, n_chunks, last_valid):
    tiles = 2 * n_chunks
    half = CHUNK // 2
    with phase(nc, "ffn") as (sbuf, psum, sem):
        ys = sbuf("ys", [P, SLOTS, half])
        normed = sbuf("normed", [P, SLOTS, half])
        hidden = sbuf("hidden", [P, 2, 2, half])
        z = sbuf("z", [P, SLOTS, half])
        up = [psum(f"up{s}", [P, 2, 512]) for s in range(2)]
        down = [psum(f"down{s}", [P, 512]) for s in range(2)]
        loaded = [sem(f"loaded{s}") for s in range(SLOTS)]
        stored = [sem(f"stored{s}") for s in range(SLOTS)]
        normed_ready, raised, hidden_ready, lowered, z_ready, eps_set = (
            sem(x) for x in ("normed_ready", "raised", "hidden_ready", "lowered", "z_ready", "eps_set"))
        bn = bn_state(sbuf, psum, sem, tiles)
        with nc.Block() as block:

            def half_of(table, n_slot_even, chunk):
                return column_chunk(table, chunk)[:, n_slot_even * half:(n_slot_even + 1) * half]

            @block.sync
            def _(sp):
                def load(n, s, turn):
                    if reused(n, SLOTS):
                        sp.wait_ge(normed_ready, n - SLOTS + 1)
                    sp.dma_start(ys[:, s, :], half_of(y_T, s % 2, turn * (SLOTS // 2) + s // 2)).then_inc(loaded[s], 16)

                def store(n, s, turn):
                    sp.wait_ge(z_ready, n + 1)
                    sp.dma_start(half_of(z_T, s % 2, turn * (SLOTS // 2) + s // 2), z[:, s, :]).then_inc(stored[s], 16)

                walk(sp, tiles, [(0, load), (3, store)])
                for s in range(SLOTS):
                    sp.wait_ge(stored[s], 16 * uses(tiles, s))

            @block.vector
            def _(dve):
                nc.vector.memset(bn["eps"][:, :], BN_EPS).then_inc(eps_set, 1)

                def norm(n, s, turn):
                    dve.wait_ge(loaded[s], (turn + 1) * 16)
                    nc.vector.tensor_scalar(normed[:, s, :], ys[:, s, :], k["bn"][:, 0:1], k["bn"][:, 1:2], ALU.mult, ALU.add).then_inc(normed_ready, 1)

                def add(n, s, turn):
                    dve.wait_ge(lowered, n + 1)
                    if reused(n, SLOTS):
                        dve.wait_ge(stored[s], turn * 16)
                    nc.vector.scalar_tensor_tensor(out=z[:, s, :], in0=down[s % 2][:, :], scalar=k["col"]["l1_bf2"],
                                                   in1=normed[:, s, :], op0=ALU.add, op1=ALU.add).then_inc(z_ready, 1)
                    dve.wait_ge(z_ready, n + 1)
                    piece = z[:, s, :]
                    if isinstance(n, int) and n >= tiles - 2:
                        piece = piece.rearrange("p (r q) -> p r q", q=P)[:, :, 0:last_valid]
                    bn_add(bn, nc, dve, [piece], n, s)

                walk(dve, tiles, [(0, norm), (2, add)])
                bn_finish_vector(bn, nc, dve, tiles, k["col"]["l1_g2"], k["col"]["l1_b2"], k["bn"][:, 2:3], k["bn"][:, 3:4])

            @block.tensor
            def _(pe):
                def raise_(n, s, turn):
                    pe.wait_ge(normed_ready, n + 1)
                    if reused(n, 2):
                        pe.wait_ge(hidden_ready, n - 1)
                    for f in range(2):
                        last = nc.tensor.matmul(up[s % 2][:, f, :], k["W"][f"ffn_up{f}"], normed[:, s, :], start=True, stop=True)
                    last.then_inc(raised, 1)

                def lower(n, s, turn):
                    pe.wait_ge(hidden_ready, n + 1)
                    if reused(n, 2):
                        pe.wait_ge(z_ready, n - 1)
                    for f in range(2):
                        last = nc.tensor.matmul(down[s % 2][:, :], k["W"][f"ffn_down{f}"], hidden[:, s % 2, f, :], start=f == 0, stop=f == 1)
                    last.then_inc(lowered, 1)

                walk(pe, tiles, [(0, raise_), (1, lower)])

            @block.scalar
            def _(act):
                act.preload_act_table_set(TABLES)

                def rectify(n, s, turn):
                    act.wait_ge(raised, n + 1)
                    if reused(n, 2):
                        act.wait_ge(lowered, n - 1)
                    for f, b in enumerate(("l1_bf1a", "l1_bf1b")):
                        last = nc.scalar.activation(hidden[:, s % 2, f, :], up[s % 2][:, f, :], ACT.Relu, bias=k["col"][b])
                    last.then_inc(hidden_ready, 1)

                walk(act, tiles, [(0, rectify)])
                act.wait_ge(eps_set, 1)
                bn_finish_scalar(bn, nc, act)


def add_layer1(nc, k, x, z_T, out, n_chunks):
    with phase(nc, "l1_add") as (sbuf, psum, sem):
        xs = sbuf("xs", [P, SLOTS, ROWS, D])
        zs = sbuf("zs", [P, SLOTS, ROWS, D])
        normed = sbuf("normed", [P, 2, ROWS, D])
        result = sbuf("result", [P, SLOTS, ROWS, D])
        turned = [psum(f"turned{s}", [P, 2, 512]) for s in range(2)]
        loaded = [sem(f"loaded{s}") for s in range(SLOTS)]
        stored = [sem(f"stored{s}") for s in range(SLOTS)]
        normed_ready, transposed, finished = (sem(x) for x in ("normed_ready", "transposed", "finished"))
        with nc.Block() as block:

            @block.sync
            def _(sp):
                def load(n, s, turn):
                    if reused(n, SLOTS):
                        sp.wait_ge(finished, n - SLOTS + 1)
                    sp.dma_start(flat(zs[:, s, :, :]), column_chunk(z_T, n)).then_inc(loaded[s], 16)
                    sp.dma_start(flat(xs[:, s, :, :]), chunk_of(x, n)).then_inc(loaded[s], 16)

                def store(n, s, turn):
                    sp.wait_ge(finished, n + 1)
                    sp.dma_start(chunk_of(out, n), flat(result[:, s, :, :])).then_inc(stored[s], 16)

                walk(sp, n_chunks, [(0, load), (2, store)])
                for s in range(SLOTS):
                    sp.wait_ge(stored[s], 16 * uses(n_chunks, s))

            @block.scalar
            def _(act):
                def norm(n, s, turn):
                    act.wait_ge(loaded[s], (turn + 1) * 32)
                    if reused(n, 2):
                        act.wait_ge(transposed, n - 1)
                    nc.scalar.activation(flat(normed[:, s % 2, :, :]), flat(zs[:, s, :, :]), ACT.Identity, bias=k["bn"][:, 3:4],
                                         scale=k["bn"][:, 2:3]).then_inc(normed_ready, 1)

                walk(act, n_chunks, [(0, norm)])

            @block.tensor
            def _(pe):
                def turn_over(n, s, turn):
                    pe.wait_ge(normed_ready, n + 1)
                    if reused(n, 2):
                        pe.wait_ge(finished, n - 1)
                    for r in range(ROWS):
                        last = nc.tensor.transpose(banks(turned[s % 2][:, :, :])[:, r, :], normed[:, s % 2, r, :], k["identity"][:, :])
                    last.then_inc(transposed, 1)

                walk(pe, n_chunks, [(0, turn_over)])

            @block.vector
            def _(dve):
                def add(n, s, turn):
                    dve.wait_ge(transposed, n + 1)
                    if reused(n, SLOTS):
                        dve.wait_ge(stored[s], turn * 16)
                    nc.vector.tensor_tensor(flat(result[:, s, :, :]), turned[s % 2][:, :, :].rearrange("p b w -> p (b w)"),
                                            flat(xs[:, s, :, :]), ALU.add).then_inc(finished, 1)

                walk(dve, n_chunks, [(0, add)])


def attention2_nodes(nc, k, x, sums, x_out, accumulator, n_chunks):
    with phase(nc, "l2_nodes") as (sbuf, psum, sem):
        xs = sbuf("xs", [P, SLOTS, ROWS, D])
        acc = sbuf("acc", [P, SLOTS, ROWS, SUMS])
        att = sbuf("att", [P, 2, ROWS, D])
        new = sbuf("new", [P, SLOTS, ROWS, D])
        normed = sbuf("normed", [P, 2, ROWS, D])
        normed_T = sbuf("normed_T", [P, 2, ROWS, D])
        own = sbuf("own", [P, SLOTS, ROWS, D])
        turned = [psum(f"turned{s}", [P, 2, 512]) for s in range(2)]
        product = [psum(f"product{s}", [P, 2, 512]) for s in range(2)]
        loaded = [sem(f"loaded{s}") for s in range(SLOTS)]
        new_stored = [sem(f"new_stored{s}") for s in range(SLOTS)]
        own_stored = [sem(f"own_stored{s}") for s in range(SLOTS)]
        new_ready, transposed, copied, multiplied, own_ready = (
            sem(x) for x in ("new_ready", "transposed", "copied", "multiplied", "own_ready"))
        ln = ln_state(sbuf, psum, sem, ROWS)
        heads = heads_state(sbuf, psum, sem)
        with nc.Block() as block:

            @block.sync
            def _(sp):
                def load(n, s, turn):
                    if reused(n, SLOTS):
                        sp.wait_ge(new_ready, n - SLOTS + 1)
                    sp.dma_start(flat(xs[:, s, :, :]), chunk_of(x, n)).then_inc(loaded[s], 16)
                    sp.dma_start(flat(acc[:, s, :, :]), chunk_of(sums, n)).then_inc(loaded[s], 16)

                def store_new(n, s, turn):
                    sp.wait_ge(new_ready, n + 1)
                    sp.dma_start(chunk_of(x_out, n), flat(new[:, s, :, :])).then_inc(new_stored[s], 16)

                def store_own(n, s, turn):
                    sp.wait_ge(own_ready, n + 1)
                    sp.dma_start(chunk_of(accumulator, n), flat(own[:, s, :, :])).then_inc(own_stored[s], 16)

                walk(sp, n_chunks, [(0, load), (2, store_new), (5, store_own)])
                for s in range(SLOTS):
                    sp.wait_ge(new_stored[s], 16 * uses(n_chunks, s))
                    sp.wait_ge(own_stored[s], 16 * uses(n_chunks, s))

            @block.vector
            def _(dve):
                ln_set_eps(ln, nc)

                def add(n, s, turn):
                    dve.wait_ge(loaded[s], (turn + 1) * 32)
                    heads_divide(heads, nc, dve, att[:, s % 2, :, :], acc[:, s, :, :], n, s)
                    dve.wait_ge(heads["mean_done"], n + 1)
                    if reused(n, SLOTS):
                        dve.wait_ge(new_stored[s], turn * 16)
                        dve.wait_ge(ln["applied"], n - SLOTS + 1)
                    nc.vector.tensor_tensor(flat(new[:, s, :, :]), flat(xs[:, s, :, :]), flat(att[:, s % 2, :, :]), ALU.add).then_inc(new_ready, 1)
                    dve.wait_ge(new_ready, n + 1)
                    ln_measure(ln, nc, dve, new[:, s, :, :], n, s)

                def add_bias(n, s, turn):
                    dve.wait_ge(multiplied, n + 1)
                    if reused(n, SLOTS):
                        dve.wait_ge(own_stored[s], turn * 16)
                    nc.vector.tensor_tensor(own[:, s, :, :], banks(product[s % 2][:, :, :]),
                                            k["row"]["l3_b_c"].unsqueeze(1).to_broadcast([P, ROWS, D]), ALU.add).then_inc(own_ready, 1)

                walk(dve, n_chunks, [(3, add_bias), (1, lambda n, s, turn: ln_centre(ln, nc, dve, n, s)), (0, add)])

            @block.tensor
            def _(pe):
                def turn_over(n, s, turn):
                    pe.wait_ge(ln["applied"], n + 1)
                    if reused(n, 2):
                        pe.wait_ge(copied, n - 1)
                    for r in range(ROWS):
                        last = nc.tensor.transpose(banks(turned[s % 2][:, :, :])[:, r, :], normed[:, s % 2, r, :], k["identity"][:, :])
                    last.then_inc(transposed, 1)

                def multiply(n, s, turn):
                    pe.wait_ge(copied, n + 1)
                    if reused(n, 2):
                        pe.wait_ge(own_ready, n - 1)
                    for r in range(ROWS):
                        last = nc.tensor.matmul(banks(product[s % 2][:, :, :])[:, r, :], normed_T[:, s % 2, r, :], k["W"]["l3_c"],
                                                start=True, stop=True)
                    last.then_inc(multiplied, 1)

                walk(pe, n_chunks, [(2, multiply), (1, turn_over)])

            @block.scalar
            def _(act):
                act.preload_act_table_set(TABLES)
                act.wait_ge(ln["eps_set"], 1)

                def norm(n, s, turn):
                    if reused(n, 2):
                        act.wait_ge(transposed, n - 1)
                    ln_apply(ln, nc, act, normed[:, s % 2, :, :], new[:, s, :, :], n, s)

                def copy(n, s, turn):
                    act.wait_ge(transposed, n + 1)
                    if reused(n, 2):
                        act.wait_ge(multiplied, n - 1)
                    nc.scalar.activation(flat(normed_T[:, s % 2, :, :]), turned[s % 2][:, :, :].rearrange("p b w -> p (b w)"),
                                         ACT.Copy).then_inc(copied, 1)

                walk(act, n_chunks, [(2, copy), (1, norm), (0, lambda n, s, turn: ln_deviate(ln, nc, act, n, s))])


def softplus_state(sbuf, psum, sem, width):
    st = {}
    st["size"] = sbuf("sp_size", [P, 2, width])
    st["decay"] = sbuf("sp_decay", [P, 2, width])
    st["tail"] = sbuf("sp_tail", [P, 2, width])
    st["half"] = sbuf("sp_half", [P, 1])
    st["half_set"], st["size_done"], st["decay_done"], st["tail_done"], st["done"] = (
        sem(f"sp_{x}") for x in ("half_set", "size_done", "decay_done", "tail_done", "done"))
    return st


def softplus_set_half(st, nc):
    nc.vector.memset(st["half"][:, :], 0.5).then_inc(st["half_set"], 1)


def softplus_tails(st, nc, act, x, bias, n, s):
    u = s % 2
    nc.scalar.activation(st["size"][:, u, :], x, ACT.Abs, **({} if bias is None else {"bias": bias})).then_inc(st["size_done"], 1)
    act.wait_ge(st["size_done"], n + 1)
    nc.scalar.activation(st["decay"][:, u, :], st["size"][:, u, :], ACT.Exp, scale=-1.0).then_inc(st["decay_done"], 1)
    act.wait_ge(st["decay_done"], n + 1)
    if reused(n, 2):
        act.wait_ge(st["done"], n - 1)
    nc.scalar.activation(st["tail"][:, u, :], st["decay"][:, u, :], ACT.Ln, scale=0.5, bias=st["half"][:, 0:1]).then_inc(st["tail_done"], 1)


def messages_over_edges(nc, k, ends, key_rows, edge_T, nodes, accumulator, n_blocks):
    with phase(nc, "l3_edges") as (sbuf, psum, sem):
        end = sbuf("end", [P, SLOTS, 2 * LANES], I32)
        rows = sbuf("rows", [P, SLOTS, LANES, D])
        edge = sbuf("edge", [64, SLOTS, BLOCK])
        normed = sbuf("normed", [P, LANES, D])
        normed_T = sbuf("normed_T", [P, BLOCK])
        positive = sbuf("positive", [P, BLOCK])
        soft = sbuf("soft", [P, 2, BLOCK])
        value = sbuf("value", [P, BLOCK])
        gated = sbuf("gated", [P, BLOCK])
        message = sbuf("message", [P, 2, LANES, D])
        pre_psum, gate_psum, turned, value_psum, message_psum = (
            psum(x, [P, 512]) for x in ("pre_psum", "gate_psum", "turned", "value_psum", "message_psum"))
        ends_in = [sem(f"ends_in{s}") for s in range(SLOTS)]
        edge_in = [sem(f"edge_in{s}") for s in range(SLOTS)]
        gathered = [sem(f"gathered{s}") for s in range(SLOTS)]
        pre_ready, gate_ready, transposed, copied, value_done, value_ready, gated_ready, message_done, \
            message_ready = (sem(x) for x in (
                "pre_ready", "gate_ready", "transposed", "copied", "value_done", "value_ready",
                "gated_ready", "message_done", "message_ready"))
        ln = ln_state(sbuf, psum, sem, LANES)
        sp_ = softplus_state(sbuf, psum, sem, BLOCK)
        mg = merge_state(sbuf, psum, sem, D)
        mg["pool_passed"] = sem("pool_passed")
        with nc.Block() as block:

            @block.sync
            def _(sp):
                def load(n, s, turn):
                    if reused(n, SLOTS):
                        sp.wait_ge(mg["target_ready"], n - SLOTS + 1)
                    sp.dma_start(end[:, s, :], ends[bass.ds(n, 1), :, :].rearrange("b p w -> (b p) w")).then_inc(ends_in[s], 16)
                    sp.dma_start(edge[:, s, :], edge_T[:, bass.ds(n * BLOCK, BLOCK)]).then_inc(edge_in[s], 16)
                    merge_load(mg, sp, key_rows, n, s)

                walk(sp, n_blocks, [(0, load)])

            @block.gpsimd
            def _(pool):
                def fetch(n, s, turn):
                    if reused(n, SLOTS):
                        pool.wait_ge(ln["applied"], n - SLOTS + 1)
                    pool.wait_ge(ends_in[s], turn * 16 + 16)
                    pool.sem_inc(mg["pool_passed"])
                    gather(pool, rows[:, s, :, :], nodes, end[:, s, LANES:], LANES, gathered[s])

                walk(pool, n_blocks, [(0, fetch), (6, lambda n, s, turn: merge_scatter(mg, nc, pool, accumulator, n, s))])
                pool.wait_ge(mg["scattered"], n_blocks * LANES * 16)

            @block.vector
            def _(dve):
                ln_set_eps(ln, nc)
                softplus_set_half(sp_, nc)

                def soften(n, s, turn):
                    dve.wait_ge(sp_["tail_done"], n + 1)
                    if reused(n, 2):
                        dve.wait_ge(gate_ready, n - 1)
                    nc.vector.tensor_tensor(soft[:, s % 2, :], positive[:, :], sp_["tail"][:, s % 2, :], ALU.add).then_inc(sp_["done"], 1)

                def measure(n, s, turn):
                    dve.wait_ge(gathered[s], (turn + 1) * LANES * 16)
                    ln_measure(ln, nc, dve, rows[:, s, :, :], n, s)

                def compare(n, s, turn):
                    dve.wait_ge(ends_in[s], (turn + 1) * 16)
                    merge_compare(mg, nc, dve, k, end[:, s, 0:LANES], n, s, turn)

                def compose(n, s, turn):
                    dve.wait_ge(message_done, n + 1)
                    if reused(n, 2):
                        dve.wait_ge(mg["merged"], n - 1)
                    nc.vector.tensor_tensor(message[:, s % 2, :, :], message_psum[:, :].rearrange("p (l d) -> p l d", d=D),
                                            k["row"]["l3_b_wvl"].unsqueeze(1).to_broadcast([P, LANES, D]), ALU.add).then_inc(message_ready, 1)

                def gate(n, s, turn):
                    dve.wait_ge(gate_ready, n + 1)
                    dve.wait_ge(value_ready, n + 1)
                    if reused(n, 1):
                        dve.wait_ge(message_done, n)
                    nc.vector.scalar_tensor_tensor(out=gated[:, :], in0=gate_psum[:, :], scalar=k["col"]["l3_b_wv2"], in1=value[:, :],
                                                   op0=ALU.add, op1=ALU.mult).then_inc(gated_ready, 1)

                walk(dve, n_blocks, [(3, gate), (4, compose), (1, measure), (4, compare),
                                     (1, lambda n, s, turn: ln_centre(ln, nc, dve, n, s)), (1, soften)])

            @block.tensor
            def _(pe):
                def merge(n, s, turn):
                    pe.wait_ge(message_ready, n + 1)
                    merge_merge(mg, nc, pe, lambda lane: message[:, s % 2, lane, :], n, s)

                def gate(n, s, turn):
                    pe.wait_ge(sp_["done"], n + 1)
                    if reused(n, 1):
                        pe.wait_ge(gated_ready, n)
                    nc.tensor.matmul(gate_psum[:, :], k["W"]["l3_wv2"], soft[:, s % 2, :], start=True, stop=True).then_inc(gate_ready, 1)
                    pe.wait_ge(copied, n + 1)
                    nc.tensor.matmul(value_psum[:, :], k["W"]["l3_v"], normed_T[:, :], start=True, stop=True).then_inc(value_done, 1)

                def express(n, s, turn):
                    pe.wait_ge(gated_ready, n + 1)
                    if reused(n, 1):
                        pe.wait_ge(message_ready, n)
                    for lane in range(LANES):
                        last = nc.tensor.matmul(message_psum[:, lane * D:(lane + 1) * D], gated[:, lane * P:(lane + 1) * P], k["W"]["l3_wvl"],
                                                start=True, stop=True)
                    last.then_inc(message_done, 1)

                def embed(n, s, turn):
                    pe.wait_ge(edge_in[s], (turn + 1) * 16)
                    if reused(n, 1):
                        pe.wait_ge(sp_["size_done"], n)
                    nc.tensor.matmul(pre_psum[:, :], k["wv1"][:, :], edge[:, s, :], start=True, stop=True).then_inc(pre_ready, 1)

                def turn_over(n, s, turn):
                    pe.wait_ge(ln["applied"], n + 1)
                    for r in range(LANES):
                        last = nc.tensor.transpose(turned[:, r * P:(r + 1) * P], normed[:, r, :], k["identity"][:, :])
                    last.then_inc(transposed, 1)

                walk(pe, n_blocks, [(5, merge), (3, express), (2, gate), (0, embed), (1, turn_over)])

            @block.scalar
            def _(act):
                act.preload_act_table_set(TABLES)
                act.wait_ge(ln["eps_set"], 1)
                act.wait_ge(sp_["half_set"], 1)

                def copy_value(n, s, turn):
                    act.wait_ge(value_done, n + 1)
                    if reused(n, 1):
                        act.wait_ge(gated_ready, n)
                    nc.scalar.activation(value[:, :], value_psum[:, :], ACT.Copy).then_inc(value_ready, 1)

                def tails(n, s, turn):
                    act.wait_ge(pre_ready, n + 1)
                    if reused(n, 1):
                        act.wait_ge(sp_["done"], n)
                    nc.scalar.activation(positive[:, :], pre_psum[:, :], ACT.Relu, bias=k["col"]["l3_b_wv1"])
                    softplus_tails(sp_, nc, act, pre_psum[:, :], k["col"]["l3_b_wv1"], n, s)

                def norm(n, s, turn):
                    if reused(n, 1):
                        act.wait_ge(transposed, n)
                    ln_apply(ln, nc, act, normed[:, :, :], rows[:, s, :, :], n, s)

                def copy(n, s, turn):
                    act.wait_ge(transposed, n + 1)
                    if reused(n, 1):
                        act.wait_ge(value_done, n)
                    nc.scalar.activation(normed_T[:, :], turned[:, :], ACT.Copy).then_inc(copied, 1)

                walk(act, n_blocks, [(5, lambda n, s, turn: merge_keep(mg, nc, act, n, s)),
                                     (1, lambda n, s, turn: ln_deviate(ln, nc, act, n, s)), (2, copy_value), (1, norm), (1, copy), (0, tails)])


def output_nodes(nc, k, x, accumulator, out, n_chunks):
    with phase(nc, "l3_nodes") as (sbuf, psum, sem):
        xs = sbuf("xs", [P, SLOTS, ROWS, D])
        acc = sbuf("acc", [P, SLOTS, ROWS, D])
        biased = sbuf("biased", [P, 2, ROWS, D])
        soft = sbuf("soft", [P, 2, ROWS, D])
        soft_T = sbuf("soft_T", [P, 2, ROWS, D])
        result = sbuf("result", [P, SLOTS, ROWS, D])
        turned = [psum(f"turned{s}", [P, 2, 512]) for s in range(2)]
        product = [psum(f"product{s}", [P, 2, 512]) for s in range(2)]
        loaded = [sem(f"loaded{s}") for s in range(SLOTS)]
        stored = [sem(f"stored{s}") for s in range(SLOTS)]
        biased_ready, transposed, copied, multiplied, finished = (
            sem(x) for x in ("biased_ready", "transposed", "copied", "multiplied", "finished"))
        sp_ = softplus_state(sbuf, psum, sem, ROWS * D)
        with nc.Block() as block:

            @block.sync
            def _(sp):
                def load(n, s, turn):
                    if reused(n, SLOTS):
                        sp.wait_ge(finished, n - SLOTS + 1)
                    sp.dma_start(flat(acc[:, s, :, :]), chunk_of(accumulator, n)).then_inc(loaded[s], 16)
                    sp.dma_start(flat(xs[:, s, :, :]), chunk_of(x, n)).then_inc(loaded[s], 16)

                def store(n, s, turn):
                    sp.wait_ge(finished, n + 1)
                    sp.dma_start(chunk_of(out, n), flat(result[:, s, :, :])).then_inc(stored[s], 16)

                walk(sp, n_chunks, [(0, load), (4, store)])
                for s in range(SLOTS):
                    sp.wait_ge(stored[s], 16 * uses(n_chunks, s))

            @block.vector
            def _(dve):
                softplus_set_half(sp_, nc)

                def soften(n, s, turn):
                    dve.wait_ge(sp_["tail_done"], n + 1)
                    if reused(n, 2):
                        dve.wait_ge(transposed, n - 1)
                    nc.vector.scalar_tensor_tensor(out=flat(soft[:, s % 2, :, :]), in0=flat(acc[:, s, :, :]), scalar=0.0,
                                                   in1=sp_["tail"][:, s % 2, :], op0=ALU.max, op1=ALU.add).then_inc(sp_["done"], 1)
                    if reused(n, 2):
                        dve.wait_ge(finished, n - 1)
                    nc.vector.tensor_tensor(biased[:, s % 2, :, :], xs[:, s, :, :],
                                            k["row"]["l3_b_o"].unsqueeze(1).to_broadcast([P, ROWS, D]), ALU.add).then_inc(biased_ready, 1)

                def add(n, s, turn):
                    dve.wait_ge(biased_ready, n + 1)
                    dve.wait_ge(multiplied, n + 1)
                    if reused(n, SLOTS):
                        dve.wait_ge(stored[s], turn * 16)
                    nc.vector.tensor_tensor(flat(result[:, s, :, :]), product[s % 2][:, :, :].rearrange("p b w -> p (b w)"),
                                            flat(biased[:, s % 2, :, :]), ALU.add).then_inc(finished, 1)

                walk(dve, n_chunks, [(3, add), (1, soften)])

            @block.tensor
            def _(pe):
                def turn_over(n, s, turn):
                    pe.wait_ge(sp_["done"], n + 1)
                    if reused(n, 2):
                        pe.wait_ge(copied, n - 1)
                    for r in range(ROWS):
                        last = nc.tensor.transpose(banks(turned[s % 2][:, :, :])[:, r, :], soft[:, s % 2, r, :], k["identity"][:, :])
                    last.then_inc(transposed, 1)

                def multiply(n, s, turn):
                    pe.wait_ge(copied, n + 1)
                    if reused(n, 2):
                        pe.wait_ge(finished, n - 1)
                    for r in range(ROWS):
                        last = nc.tensor.matmul(banks(product[s % 2][:, :, :])[:, r, :], soft_T[:, s % 2, r, :], k["W"]["l3_out"],
                                                start=True, stop=True)
                    last.then_inc(multiplied, 1)

                walk(pe, n_chunks, [(2, multiply), (1, turn_over)])

            @block.scalar
            def _(act):
                act.preload_act_table_set(TABLES)
                act.wait_ge(sp_["half_set"], 1)

                def tails(n, s, turn):
                    act.wait_ge(loaded[s], (turn + 1) * 32)
                    softplus_tails(sp_, nc, act, flat(acc[:, s, :, :]), None, n, s)

                def copy(n, s, turn):
                    act.wait_ge(transposed, n + 1)
                    if reused(n, 2):
                        act.wait_ge(multiplied, n - 1)
                    nc.scalar.activation(flat(soft_T[:, s % 2, :, :]), turned[s % 2][:, :, :].rearrange("p b w -> p (b w)"),
                                         ACT.Copy).then_inc(copied, 1)

                walk(act, n_chunks, [(2, copy), (0, tails)])


def build(nc, x, ends, dst_cols, dst_rows, src_rows, edge_T, edge_weight, matrices, wv1, columns, broadcast, bias_kvq,
          out, n_nodes):
    n_chunks = x.shape[0] // CHUNK
    n_blocks = ends.shape[0]
    last = n_nodes - (n_chunks - 1) * CHUNK
    assert last % ROWS == 0 and n_chunks * ROWS >= P
    n_pad = n_chunks * CHUNK

    def dram(name, shape):
        return nc.dram_tensor(name, shape, F32).ap()

    gcn_table1, gcn_table2, x1, x2, x3 = (dram(t, [n_pad, D]) for t in ("gcn_table1", "gcn_table2", "x1", "x2", "x3"))
    gcn_sum1, gcn_sum2, l3_sum = (dram(t, [n_pad + SPARE, D]) for t in ("gcn_sum1", "gcn_sum2", "l3_sum"))
    l1_sum, l2_sum = (dram(t, [n_pad + SPARE, SUMS]) for t in ("l1_sum", "l2_sum"))
    y_T, z_T = (dram(t, [n_chunks, P, CHUNK]) for t in ("y_T", "z_T"))
    k = {}
    with ExitStack() as ctx:
        load_constants(nc, ctx, k, matrices, wv1, columns, broadcast, bias_kvq, n_chunks * ROWS)
        degrees(nc, k, dst_cols, gcn_sum1, l3_sum, n_blocks, n_chunks)
        norm_nodes(nc, k, x, gcn_table1, n_chunks)
        sum_over_edges(nc, k, "gcn1_edges", ends, dst_rows, gcn_table1, gcn_sum1, gcn_sum2, n_blocks)
        gcn_nodes(nc, k, "gcn1_nodes", gcn_sum1, gcn_table1, k["W"]["gcn_w1"], k["row"]["gcn_b1"], None, gcn_table2, n_chunks)
        sum_over_edges(nc, k, "gcn2_edges", ends, dst_rows, gcn_table2, gcn_sum2, l1_sum, n_blocks)
        gcn_nodes(nc, k, "gcn2_nodes", gcn_sum2, gcn_table2, k["W"]["gcn_w2"], k["row"]["gcn_b2"], x, x1, n_chunks)
        attention_over_edges(nc, k, "l1_edges", ends, dst_rows, edge_weight, x1, "l1_k", None, l1_sum, l2_sum, n_blocks)
        attention1_nodes(nc, k, x1, l1_sum, y_T, n_chunks, last // ROWS)
        feed_forward(nc, k, y_T, z_T, n_chunks, last // ROWS)
        add_layer1(nc, k, x1, z_T, x2, n_chunks)
        attention_over_edges(nc, k, "l2_edges", ends, dst_rows, None, x2, "l2_k", k["kvq_bias"][:, :], l2_sum, None, n_blocks)
        attention2_nodes(nc, k, x2, l2_sum, x3, l3_sum, n_chunks)
        messages_over_edges(nc, k, ends, src_rows, edge_T, x3, l3_sum, n_blocks)
        output_nodes(nc, k, x3, l3_sum, out, n_chunks)


def kernel(**inputs):
    import concourse.bacc as bacc
    import numpy as np
    from concourse.bass_utils import run_bass_kernel_spmd

    a = {name: np.asarray(v) for name, v in inputs.items()}
    n_nodes, n_edges = a["x"].shape[0], a["src"].shape[0]
    n_chunks, n_blocks = -(-n_nodes // CHUNK), -(-n_edges // BLOCK)
    n_pad, e_pad = n_chunks * CHUNK, n_blocks * BLOCK

    def pad_rows(v, rows, fill=0):
        return np.concatenate([v, np.full((rows - v.shape[0],) + v.shape[1:], fill, v.dtype)])

    assert n_pad > n_nodes or e_pad == n_edges
    src, dst = (pad_rows(a[s].astype(np.int32), e_pad, n_nodes).reshape(n_blocks, P, LANES) for s in ("src", "dst"))

    def lanes_first(v):
        return v.transpose(0, 2, 1).reshape(n_blocks, BLOCK)

    edge = pad_rows(a["edge_attr_64"], e_pad).reshape(n_blocks, P, LANES, 64).transpose(3, 0, 2, 1).reshape(64, e_pad)
    mats = {"gcn_w1": a["L0_gnn_W1"], "gcn_w2": a["L0_gnn_W2"], "l1_k": a["L1_gnn_Wk"], "l1_v": a["L1_gnn_Wv"],
            "l1_q": a["L1_gnn_Wq"], "l1_o": a["L1_gnn_Wo"], "ffn_up0": a["L1_gnn_W1"][:, :D], "ffn_up1": a["L1_gnn_W1"][:, D:],
            "ffn_down0": a["L1_gnn_W2"][:D], "ffn_down1": a["L1_gnn_W2"][D:], "l2_k": a["L2_gnn_Wk"], "l2_v": a["L2_gnn_Wv"],
            "l2_q": a["L2_gnn_Wq"], "l3_c": a["L3_gnn_W_c"].T, "l3_out": a["L3_gnn_W_o"].T, "l3_v": a["L3_gnn_W_v"].T,
            "l3_wv2": a["L3_gnn_W_wv2"].T, "l3_wvl": a["L3_gnn_W_wvl"].T}
    cols = {"l1_bo": a["L1_gnn_bo"], "l1_g1": a["L1_gnn_g1"], "l1_b1": a["L1_gnn_b1"], "l1_bf1a": a["L1_gnn_bf1"][:D],
            "l1_bf1b": a["L1_gnn_bf1"][D:], "l1_bf2": a["L1_gnn_bf2"], "l1_g2": a["L1_gnn_g2"], "l1_b2": a["L1_gnn_b2"],
            "l3_b_wv1": a["L3_gnn_b_wv1"], "l3_b_wv2": a["L3_gnn_b_wv2"]}
    rows = {"gcn_b1": a["L0_gnn_b1"], "gcn_b2": a["L0_gnn_b2"], "l1_e": a["L1_gnn_We"][0], "l3_b_c": a["L3_gnn_b_c"],
            "l3_b_o": a["L3_gnn_b_o"], "l3_b_wvl": a["L3_gnn_b_wvl"]}
    kvq = {"l2_bk": a["L2_gnn_bk"], "l2_bv": a["L2_gnn_bv"], "l2_bq": a["L2_gnn_bq"]}
    arrays = {
        "in_x": pad_rows(a["x"], n_pad),
        "in_ends": np.concatenate([src, dst], axis=2),
        "in_dst_cols": dst.transpose(1, 0, 2).reshape(P, n_blocks * LANES),
        "in_dst_rows": lanes_first(dst),
        "in_src_rows": lanes_first(src),
        "in_edge_T": edge,
        "in_edge_weight": pad_rows(a["edge_weight1"], e_pad).reshape(n_blocks, P, LANES),
        "in_matrices": np.concatenate([mats[m] for m in MATRICES], axis=1),
        "in_wv1": a["L3_gnn_W_wv1"].T,
        "in_columns": np.stack([cols[m] for m in COLUMNS], axis=1),
        "in_broadcast": np.concatenate([rows[m] for m in BROADCAST])[None],
        "in_bias_kvq": np.concatenate([kvq[m] for m in BIAS_KVQ])[None],
    }
    arrays = {name: np.ascontiguousarray(v) for name, v in arrays.items()}
    nc = bacc.Bacc("TRN2", target_bir_lowering=False, num_devices=1)
    args = {name: nc.dram_tensor(name, v.shape, mybir.dt.from_np(v.dtype), kind="ExternalInput").ap() for name, v in arrays.items()}
    out = nc.dram_tensor("out_nodes", [n_pad, D], F32, kind="ExternalOutput").ap()
    build(nc, args["in_x"], args["in_ends"], args["in_dst_cols"], args["in_dst_rows"], args["in_src_rows"], args["in_edge_T"],
          args["in_edge_weight"], args["in_matrices"], args["in_wv1"], args["in_columns"], args["in_broadcast"],
          args["in_bias_kvq"], out, n_nodes)
    result = run_bass_kernel_spmd(nc, [arrays], core_ids=[0])
    return result.results[0]["out_nodes"][:n_nodes]
```

```python
from contextlib import ExitStack, contextmanager

import concourse.bass as bass
from concourse import mybir

F32 = mybir.dt.float32
F16 = mybir.dt.float16
BF16 = mybir.dt.bfloat16
I32 = mybir.dt.int32
ALU = mybir.AluOpType
ACT = mybir.ActivationFunctionType
AXIS_X = mybir.AxisListType.X

P = 128
D = 128
ROWS = 8
CHUNK = P * ROWS
LANES = 4
BLOCK = P * LANES
HEADS, HEAD_DIM = 8, 16
SUMS = D + HEADS
SPARE = BLOCK
SLOTS = 6
BEHIND = 2
LN_EPS = 1e-5
BN_EPS = 1e-5
Z_EPS = 1e-6
TABLES = "natural_log_exp_and_others"
WQ_SCALE = 1.0 / HEAD_DIM ** 0.5

MATRICES = ["gcn_w1", "gcn_w2", "l1_k", "l1_v", "l1_q", "l1_o", "ffn_up0", "ffn_up1", "ffn_down0", "ffn_down1",
            "l2_k", "l2_v", "l2_q", "l3_c", "l3_out", "l3_v", "l3_wv2", "l3_wvl"]
COLUMNS = ["l1_bo", "l1_g1", "l1_b1", "l1_bf1a", "l1_bf1b", "l1_bf2", "l1_g2", "l1_b2", "l3_b_wv1", "l3_b_wv2"]
BROADCAST = ["gcn_b1", "gcn_b2", "l1_e", "l3_b_o", "l3_b_wvl"]
BIASES = ["l2_bk", "l2_bv", "l2_bq", "l3_b_c"]
PARTS = 3


def reused(n, slots):
    return not isinstance(n, int) or n >= slots


def walk(eng, count, stages):
    deepest = max(lag for lag, _ in stages)
    first = deepest + SLOTS
    first += (count - first) % SLOTS

    def peeled(t):
        for lag, step in stages:
            if 0 <= t - lag < count:
                step(t - lag, (t - lag) % SLOTS, (t - lag) // SLOTS)

    for t in range(min(first, count + deepest)):
        peeled(t)
    if first < count:
        with eng.Fori(0, (count - first) // SLOTS) as i:
            for u in range(SLOTS):
                for lag, step in stages:
                    c = first + u - lag
                    step(i * SLOTS + c, c % SLOTS, i + c // SLOTS)
    for t in range(max(count, first), count + deepest):
        peeled(t)


def uses(count, s):
    return (count - s + SLOTS - 1) // SLOTS


@contextmanager
def phase(nc, name):
    sems = []
    with ExitStack() as ctx:

        def sbuf(what, shape, dtype=F32):
            return ctx.enter_context(nc.sbuf_tensor(f"{name}_{what}", shape, dtype))

        def psum(what, shape):
            return ctx.enter_context(nc.psum_tensor(f"{name}_{what}", shape, F32))

        def sem(what):
            sems.append(nc.alloc_semaphore(f"{name}_{what}"))
            return sems[-1]

        yield sbuf, psum, sem
        nc.clear_and_free_semaphores(sems)
        nc.all_engine_barrier()


def ln_state(sbuf, psum, sem, rows):
    st = {}
    st["rows"] = rows
    st["stats"] = sbuf("ln_stats", [P, SLOTS, rows, 6])
    st["mean2"] = sbuf("ln_mean2", [P, SLOTS, rows])
    st["gap"] = sbuf("ln_gap", [P, SLOTS, rows])
    st["within"] = sbuf("ln_within", [P, SLOTS, rows])
    st["between"] = sbuf("ln_between", [P, SLOTS, rows])
    st["var"] = sbuf("ln_var", [P, SLOTS, rows])
    st["logvar"] = sbuf("ln_logvar", [P, SLOTS, rows])
    st["scale"] = sbuf("ln_scale", [P, SLOTS, rows])
    st["shift"] = sbuf("ln_shift", [P, SLOTS, rows])
    st["eps"] = sbuf("ln_eps", [P, 1])
    st["stats_done"], st["sums_done"], st["between_done"], st["var_done"], st["log_done"], st["scale_done"], \
        st["shift_done"], st["applied"], st["eps_set"] = (
            sem(f"ln_{x}") for x in ("stats_done", "sums_done", "between_done", "var_done", "log_done",
                                        "scale_done", "shift_done", "applied", "eps_set"))
    return st


def ln_set_eps(st, nc):
    nc.vector.memset(st["eps"][:, :], LN_EPS).then_inc(st["eps_set"], 1)


def ln_count(st, nc, x, s):
    for r in range(st["rows"]):
        last = nc.vector.bn_stats(st["stats"][:, s, r, :], x[:, r, :])
    last.then_inc(st["stats_done"], 1)


def ln_sums(st, nc, dve, n, s):
    dve.wait_ge(st["stats_done"], n + 1)
    stats = st["stats"][:, s, :, :]
    nc.vector.tensor_tensor(st["gap"][:, s, :], stats[:, :, 1], stats[:, :, 4], ALU.subtract)
    nc.vector.tensor_tensor(st["mean2"][:, s, :], stats[:, :, 1], stats[:, :, 4], ALU.add)
    nc.vector.tensor_tensor(st["within"][:, s, :], stats[:, :, 2], stats[:, :, 5], ALU.add).then_inc(st["sums_done"], 1)


def ln_between(st, nc, dve, n, s):
    dve.wait_ge(st["sums_done"], n + 1)
    nc.vector.scalar_tensor_tensor(out=st["between"][:, s, :], in0=st["gap"][:, s, :], scalar=0.25,
                                   in1=st["gap"][:, s, :], op0=ALU.mult, op1=ALU.mult).then_inc(st["between_done"], 1)


def ln_var(st, nc, dve, n, s):
    dve.wait_ge(st["between_done"], n + 1)
    if reused(n, SLOTS):
        dve.wait_ge(st["log_done"], n - SLOTS + 1)
    nc.vector.scalar_tensor_tensor(out=st["var"][:, s, :], in0=st["within"][:, s, :], scalar=1.0 / D,
                                   in1=st["between"][:, s, :], op0=ALU.mult, op1=ALU.add).then_inc(st["var_done"], 1)


def ln_measure(st, nc, dve, x, n, s):
    ln_count(st, nc, x, s)
    ln_sums(st, nc, dve, n, s)
    ln_between(st, nc, dve, n, s)
    ln_var(st, nc, dve, n, s)


def ln_deviate(st, nc, act, n, s):
    act.wait_ge(st["var_done"], n + 1)
    nc.scalar.activation(st["logvar"][:, s, :], st["var"][:, s, :], ACT.Ln, bias=st["eps"][:, 0:1]).then_inc(st["log_done"], 1)
    act.wait_ge(st["log_done"], n + 1)
    nc.scalar.activation(st["scale"][:, s, :], st["logvar"][:, s, :], ACT.Exp, scale=-0.5).then_inc(st["scale_done"], 1)


def ln_centre(st, nc, dve, n, s):
    dve.wait_ge(st["scale_done"], n + 1)
    if reused(n, SLOTS):
        dve.wait_ge(st["applied"], n - SLOTS + 1)
    nc.vector.scalar_tensor_tensor(out=st["shift"][:, s, :], in0=st["mean2"][:, s, :], scalar=-0.5,
                                   in1=st["scale"][:, s, :], op0=ALU.mult, op1=ALU.mult).then_inc(st["shift_done"], 1)


def ln_apply(st, nc, act, out, x, n, s):
    act.wait_ge(st["shift_done"], n + 1)
    for r in range(st["rows"]):
        last = nc.scalar.activation(out[:, r, :], x[:, r, :], ACT.Relu, bias=st["shift"][:, s, r:r + 1],
                                    scale=st["scale"][:, s, r:r + 1])
    last.then_inc(st["applied"], 1)


def load_constants(nc, ctx, k, matrices, wv1, columns, broadcast, biases, node_cols):
    def keep(name, shape, dtype=F32):
        return ctx.enter_context(nc.sbuf_tensor(f"const_{name}", shape, dtype))

    k["matrices"] = keep("matrices", [P, len(MATRICES), D])
    k["wv1"] = keep("wv1", [64, D])
    k["columns"] = keep("columns", [P, len(COLUMNS)])
    k["rows"] = keep("rows", [P, len(BROADCAST), D])
    k["bias_parts"] = keep("bias_parts", [PARTS, len(BIASES) * D], BF16)
    k["bias"] = {m: k["bias_parts"][:, i * D:(i + 1) * D] for i, m in enumerate(BIASES)}
    k["ones"] = keep("ones", [PARTS, P], BF16)
    k["identity"] = keep("identity", [P, P])
    k["earlier"] = keep("earlier", [P, BLOCK])
    k["spare_rows"] = keep("spare_rows", [P, LANES])
    k["dis"] = keep("dis", [P, node_cols])
    k["bn"] = keep("bn", [P, 4])
    k["in_time"] = keep("in_time", [1, 1], I32)
    k["W"] = {m: k["matrices"][:, i, :] for i, m in enumerate(MATRICES)}
    k["col"] = {m: k["columns"][:, i:i + 1] for i, m in enumerate(COLUMNS)}
    k["row"] = {m: k["rows"][:, i, :] for i, m in enumerate(BROADCAST)}
    spare_first = node_cols * P
    with phase(nc, "constants") as (sbuf, psum, sem):
        loaded = sem("loaded")
        filled = sem("filled")
        made = sem("made")
        scaled = sem("scaled")
        spread = sem("spread")
        bias = sbuf("bias", [PARTS, len(BIASES) * D])
        parts = [sbuf(f"part{i}", [PARTS, len(BIASES) * D], BF16) for i in range(PARTS)]
        rest = [bias] + [sbuf(f"rest{i}", [PARTS, len(BIASES) * D]) for i in range(1, PARTS)]
        with nc.Block() as block:

            @block.sync
            def _(sp):
                sp.dma_start(k["matrices"][:, :, :], matrices.rearrange("p (m d) -> p m d", d=D)).then_inc(loaded, 16)
                sp.dma_start(k["wv1"][:, :], wv1).then_inc(loaded, 16)
                sp.dma_start(k["columns"][:, :], columns).then_inc(loaded, 16)
                sp.dma_start(k["rows"][:, :, :].rearrange("p m d -> p (m d)"), broadcast.to_broadcast([P, len(BROADCAST) * D])).then_inc(loaded, 16)
                sp.dma_start(bias[:, :], biases.to_broadcast([PARTS, len(BIASES) * D])).then_inc(loaded, 16)
                sp.wait_ge(scaled, 2 * PARTS)
                for i in range(PARTS):
                    sp.dma_start(k["bias_parts"][i:i + 1, :], parts[i][i:i + 1, :]).then_inc(spread, 16)
                sp.wait_ge(spread, 16 * PARTS)

            @block.gpsimd
            def _(pool):
                nc.gpsimd.memset(k["identity"][:, :], 0.0)
                nc.gpsimd.memset(k["earlier"][:, :], 1.0).then_inc(filled, 1)
                pool.wait_ge(filled, 1)
                nc.gpsimd.affine_select(out=k["identity"][:, :], in_=k["identity"][:, :], compare_op=ALU.not_equal, fill=1.0,
                                        base=0, pattern=[[-1, P]], channel_multiplier=1)
                nc.gpsimd.affine_select(out=k["earlier"][:, BLOCK - P:], in_=k["earlier"][:, BLOCK - P:], compare_op=ALU.is_gt,
                                        fill=0.0, base=0, pattern=[[-1, P]], channel_multiplier=1)
                nc.gpsimd.iota(k["spare_rows"][:, :], pattern=[[P, LANES]], base=spare_first, channel_multiplier=1,
                               allow_small_or_imprecise_dtypes=True).then_inc(made, 1)

            @block.vector
            def _(dve):
                nc.vector.memset(k["ones"][:, :], 1.0)
                dve.wait_ge(loaded, 5 * 16)
                nc.vector.scalar_tensor_tensor(out=k["W"]["l1_q"], in0=k["W"]["l1_q"], scalar=WQ_SCALE, in1=k["row"]["l1_e"],
                                               op0=ALU.mult, op1=ALU.mult)
                nc.vector.tensor_scalar(k["W"]["l2_q"], k["W"]["l2_q"], WQ_SCALE, None, ALU.mult)
                nc.vector.tensor_scalar(bias[:, 2 * D:3 * D], bias[:, 2 * D:3 * D], WQ_SCALE, None, ALU.mult).then_inc(scaled, 1)
                for i in range(PARTS):
                    dve.wait_ge(scaled, 2 * i + 1)
                    nc.vector.tensor_copy(parts[i][:, :], rest[i][:, :]).then_inc(scaled, 1)
                    if i < PARTS - 1:
                        dve.wait_ge(scaled, 2 * i + 2)
                        nc.vector.tensor_tensor(rest[i + 1][:, :], rest[i][:, :], parts[i][:, :], ALU.subtract).then_inc(scaled, 1)


def degrees(nc, k, dst_cols, accumulators, n_blocks, n_chunks):
    cols = n_chunks * ROWS
    half = cols // 2
    with phase(nc, "degrees") as (sbuf, psum, sem):
        keys = sbuf("keys", [P, n_blocks * LANES], I32)
        part_i = sbuf("part_i", [P, n_blocks * LANES], I32)
        high_i = sbuf("high_i", [P, n_blocks * LANES], I32)
        low_i = sbuf("low_i", [P, n_blocks * LANES], I32)
        part = sbuf("part", [P, n_blocks * LANES])
        col = sbuf("col", [P, n_blocks * LANES])
        numbers = sbuf("numbers", [P, cols], F16)
        hot_part = sbuf("hot_part", [P, SLOTS, LANES, P], F16)
        hot_col = sbuf("hot_col", [P, SLOTS, LANES, cols], F16)
        zeros = sbuf("zeros", [P, LANES * D])
        log_deg = sbuf("log_deg", [P, cols])
        chunk_i = sbuf("chunk_i", [P, n_blocks * LANES], I32)
        block_i = sbuf("block_i", [P, n_blocks * LANES], I32)
        ahead = sbuf("ahead", [P, n_blocks * LANES])
        least = sbuf("least", [P, 1])
        least_of_all = sbuf("least_of_all", [1, 1])
        least_T = psum("least_T", [P, 512])
        counts = psum("counts", [P, 2, 512])
        keys_in, split, numbered, hot, counted, zeros_set, zeroed, logged, ended, least_ready, least_turned = (
            sem(x) for x in ("keys_in", "split", "numbered", "hot", "counted", "zeros_set", "zeroed", "logged", "ended",
                             "least_ready", "least_turned"))
        with nc.Block() as block:

            @block.sync
            def _(sp):
                sp.dma_start(keys[:, :], dst_cols).then_inc(keys_in, 16)
                sp.wait_ge(zeros_set, 1)
                for accumulator in accumulators:
                    spare = accumulator[n_chunks * CHUNK:, :].rearrange("(p r) d -> p (r d)", p=P)
                    sp.dma_start(spare, zeros[:, :]).then_inc(zeroed, 16)
                sp.wait_ge(zeroed, 16 * len(accumulators))

            @block.gpsimd
            def _(pool):
                nc.gpsimd.iota(block_i[:, :], pattern=[[1, n_blocks], [0, LANES]], base=0, channel_multiplier=0)
                nc.gpsimd.iota(numbers[:, :], pattern=[[1, cols]], base=0, channel_multiplier=0,
                               allow_small_or_imprecise_dtypes=True).then_inc(numbered, 1)

            @block.vector
            def _(dve):
                nc.vector.memset(zeros[:, :], 0.0).then_inc(zeros_set, 1)
                dve.wait_ge(keys_in, 16)
                nc.vector.tensor_scalar(part_i[:, :], keys[:, :], 3, P - 1, ALU.logical_shift_right, ALU.bitwise_and)
                nc.vector.tensor_scalar(high_i[:, :], keys[:, :], 10, 3, ALU.logical_shift_right, ALU.logical_shift_left)
                nc.vector.tensor_scalar(chunk_i[:, :], keys[:, :], 10, None, ALU.logical_shift_right)
                nc.vector.tensor_scalar(low_i[:, :], keys[:, :], ROWS - 1, None, ALU.bitwise_and).then_inc(split, 1)
                dve.wait_ge(split, 1)
                nc.vector.tensor_copy(part[:, :], part_i[:, :])
                nc.vector.tensor_tensor(col[:, :], high_i[:, :], low_i[:, :], ALU.add).then_inc(split, 1)
                dve.wait_ge(numbered, 1)
                nc.vector.tensor_tensor(ahead[:, :], chunk_i[:, :], block_i[:, :], ALU.subtract).then_inc(split, 1)
                dve.wait_ge(split, 3)
                nc.vector.tensor_reduce(least[:, :], ahead[:, :], AXIS_X, ALU.min).then_inc(least_ready, 1)

                def one_hot(n, s, turn):
                    if reused(n, SLOTS):
                        dve.wait_ge(counted, n - SLOTS + 1)
                    for lane in range(LANES):
                        at = bass.ds(n * LANES + lane, 1)
                        nc.vector.tensor_scalar(hot_part[:, s, lane, :], numbers[:, 0:P], part[:, at], None, ALU.is_equal)
                        last = nc.vector.tensor_scalar(hot_col[:, s, lane, :], numbers[:, :], col[:, at], None, ALU.is_equal)
                    last.then_inc(hot, 1)

                walk(dve, n_blocks, [(0, one_hot)])
                dve.wait_ge(least_turned, 1)
                nc.vector.tensor_reduce(least_of_all[:, :], least_T[0:1, 0:P], AXIS_X, ALU.min).then_inc(least_ready, 1)
                dve.wait_ge(least_ready, 2)
                nc.vector.tensor_scalar(k["in_time"][:, :], least_of_all[:, :], float(-BEHIND), None, ALU.is_ge).then_inc(ended, 1)

            @block.tensor
            def _(pe):
                def count(n, s, turn):
                    pe.wait_ge(hot, n + 1)
                    for lane in range(LANES):
                        for h in range(2):
                            start = isinstance(n, int) and n == 0 and lane == 0
                            stop = isinstance(n, int) and n == n_blocks - 1 and lane == LANES - 1
                            last = nc.tensor.matmul(counts[:, h, 0:half], hot_part[:, s, lane, :],
                                                    hot_col[:, s, lane, h * half:(h + 1) * half], start=start, stop=stop)
                    last.then_inc(counted, 1)

                pe.wait_ge(least_ready, 1)
                nc.tensor.transpose(least_T[0:1, 0:P], least[:, :], k["identity"][:, :]).then_inc(least_turned, 1)
                walk(pe, n_blocks - 1, [(0, count)])
                count(n_blocks - 1, (n_blocks - 1) % SLOTS, 0)

            @block.scalar
            def _(act):
                act.preload_act_table_set(TABLES)
                act.wait_ge(counted, n_blocks)
                nc.scalar.activation(log_deg[:, :].rearrange("p (h c) -> p h c", h=2), counts[:, :, 0:half], ACT.Ln, bias=1.0).then_inc(logged, 1)
                act.wait_ge(logged, 1)
                nc.scalar.activation(k["dis"][:, :], log_deg[:, :], ACT.Exp, scale=-0.5).then_inc(ended, 1)


def chunk_of(table, n, width=D):
    t = table[0:table.shape[0] // CHUNK * CHUNK, :].rearrange("(c p r) d -> c p (r d)", p=P, r=ROWS)
    return t[bass.ds(n, 1), :, :].rearrange("c p w -> (c p) w")


def norm_nodes(nc, k, x, table, accumulator, n_chunks):
    with phase(nc, "norm_nodes") as (sbuf, psum, sem):
        xs = sbuf("xs", [P, SLOTS, ROWS, D])
        out = sbuf("out", [P, SLOTS, ROWS, D])
        ln = ln_state(sbuf, psum, sem, ROWS)
        scale = sbuf("scale", [P, SLOTS, ROWS])
        loaded = [sem(f"loaded{s}") for s in range(SLOTS)]
        stored = [sem(f"stored{s}") for s in range(SLOTS)]
        scaled = sem("scaled")
        with nc.Block() as block:

            @block.sync
            def _(sp):
                def load(n, s, turn):
                    if reused(n, SLOTS):
                        sp.wait_ge(ln["applied"], n - SLOTS + 1)
                    sp.dma_start(xs[:, s, :, :].rearrange("p r d -> p (r d)"), chunk_of(x, n)).then_inc(loaded[s], 16)

                def store(n, s, turn):
                    sp.wait_ge(ln["applied"], n + 1)
                    sp.dma_start(chunk_of(table, n), flat(out[:, s, :, :])).then_inc(stored[s], 16)
                    sp.dma_start(chunk_of(accumulator, n), flat(out[:, s, :, :])).then_inc(stored[s], 16)

                walk(sp, n_chunks, [(0, load), (3, store)])
                for s in range(SLOTS):
                    sp.wait_ge(stored[s], 32 * uses(n_chunks, s))

            @block.vector
            def _(dve):
                ln_set_eps(ln, nc)

                def measure(n, s, turn):
                    dve.wait_ge(loaded[s], turn * 16 + 16)
                    ln_measure(ln, nc, dve, xs[:, s, :, :], n, s)

                def centre(n, s, turn):
                    dve.wait_ge(ln["scale_done"], n + 1)
                    if reused(n, SLOTS):
                        dve.wait_ge(ln["applied"], n - SLOTS + 1)
                    nc.vector.tensor_tensor(scale[:, s, :], ln["scale"][:, s, :], k["dis"][:, bass.ds(n * ROWS, ROWS)], ALU.mult).then_inc(scaled, 1)
                    dve.wait_ge(scaled, n + 1)
                    nc.vector.scalar_tensor_tensor(out=ln["shift"][:, s, :], in0=ln["mean2"][:, s, :], scalar=-0.5,
                                                   in1=scale[:, s, :], op0=ALU.mult, op1=ALU.mult).then_inc(ln["shift_done"], 1)

                walk(dve, n_chunks, [(1, centre), (0, measure)])

            @block.scalar
            def _(act):
                act.preload_act_table_set(TABLES)
                act.wait_ge(ln["eps_set"], 1)

                def deviate(n, s, turn):
                    if reused(n, SLOTS):
                        act.wait_ge(scaled, n - SLOTS + 1)
                    ln_deviate(ln, nc, act, n, s)

                def apply(n, s, turn):
                    if reused(n, SLOTS):
                        act.wait_ge(stored[s], turn * 32)
                    act.wait_ge(ln["shift_done"], n + 1)
                    for r in range(ROWS):
                        last = nc.scalar.activation(out[:, s, r, :], xs[:, s, r, :], ACT.Relu, bias=ln["shift"][:, s, r:r + 1],
                                                    scale=scale[:, s, r:r + 1])
                    last.then_inc(ln["applied"], 1)

                walk(act, n_chunks, [(1, apply), (0, deviate)])


def merge_state(sbuf, psum, sem, width):
    st = {}
    st["width"] = width
    st["key_rows"] = sbuf("key_rows", [P, SLOTS, BLOCK], I32)
    st["key"] = sbuf("key", [P, SLOTS, LANES])
    st["same"] = sbuf("same", [P, 2, LANES, BLOCK])
    st["masked"] = sbuf("masked", [P, LANES, BLOCK], F16)
    st["before"] = sbuf("before", [P, SLOTS, LANES])
    st["away"] = sbuf("away", [P, SLOTS, LANES])
    st["step"] = sbuf("step", [P, SLOTS, LANES])
    st["target"] = sbuf("target", [P, SLOTS, LANES], I32)
    st["sums"] = sbuf("sums", [P, 2, LANES, width])
    st["psum"] = psum("merge_psum", [P, 2, 512])
    st["keys_in"] = [sem(f"keys_in{s}") for s in range(SLOTS)]
    st["key_ready"], st["same_ready"], st["before_ready"], st["step_ready"], st["target_ready"], st["merged"], \
        st["sums_ready"], st["scattered"] = (
            sem(x) for x in ("key_ready", "same_ready", "before_ready", "step_ready", "target_ready", "merged",
                                "sums_ready", "scattered"))
    return st


def merge_load(st, sp, key_rows, n, s):
    sp.dma_start(st["key_rows"][:, s, :], key_rows[bass.ds(n, 1), :].to_broadcast([P, BLOCK])).then_inc(st["keys_in"][s], 16)


def merge_compare(st, nc, dve, k, key_cols, n, s, turn):
    dve.wait_ge(st["keys_in"][s], turn * 16 + 16)
    nc.vector.tensor_copy(st["key"][:, s, :], key_cols).then_inc(st["key_ready"], 1)
    dve.wait_ge(st["key_ready"], n + 1)
    if reused(n, 2):
        dve.wait_ge(st["merged"], n - 1)
    for lane in range(LANES):
        upto = (lane + 1) * P
        last = nc.vector.tensor_scalar(st["same"][:, s % 2, lane, 0:upto], st["key_rows"][:, s, 0:upto],
                                       st["key"][:, s, lane:lane + 1], None, ALU.is_equal)
    last.then_inc(st["same_ready"], 1)
    dve.wait_ge(st["same_ready"], n + 1)
    for lane in range(LANES):
        upto = (lane + 1) * P
        last = nc.vector.tensor_tensor_reduce(out=st["masked"][:, lane, 0:upto], in0=st["same"][:, s % 2, lane, 0:upto],
                                              in1=k["earlier"][:, BLOCK - upto:], scale=1.0, scalar=0.0, op0=ALU.mult,
                                              op1=ALU.add, accum_out=st["before"][:, s, lane:lane + 1])
    nc.vector.tensor_tensor(st["away"][:, s, :], k["spare_rows"][:, :], st["key"][:, s, :], ALU.subtract).then_inc(st["before_ready"], 1)
    dve.wait_ge(st["before_ready"], n + 1)
    nc.vector.scalar_tensor_tensor(out=st["step"][:, s, :], in0=st["before"][:, s, :], scalar=1.0,
                                   in1=st["away"][:, s, :], op0=ALU.min, op1=ALU.mult).then_inc(st["step_ready"], 1)
    dve.wait_ge(st["step_ready"], n + 1)
    if reused(n, SLOTS):
        dve.wait_ge(st["scattered"], (n - SLOTS + 1) * LANES * 16)
    nc.vector.tensor_tensor(st["target"][:, s, :], st["step"][:, s, :], st["key"][:, s, :], ALU.add).then_inc(st["target_ready"], 1)


def merge_merge(st, nc, pe, message, n, s):
    pe.wait_ge(st["same_ready"], n + 1)
    if reused(n, 1):
        pe.wait_ge(st["sums_ready"], n)
    for to in range(LANES):
        at = (to % 2) * st["width"]
        for lane in range(to, LANES):
            last = nc.tensor.matmul(st["psum"][:, to // 2, at:at + st["width"]],
                                    st["same"][:, s % 2, lane, to * P:(to + 1) * P], message(lane),
                                    start=lane == to, stop=lane == LANES - 1)
    last.then_inc(st["merged"], 1)


def merge_keep(st, nc, act, n, s):
    act.wait_ge(st["merged"], n + 1)
    if reused(n, 2):
        act.wait_ge(st["scattered"], (n - 1) * LANES * 16)
    nc.scalar.activation(st["sums"][:, s % 2, :, :].rearrange("p (b l) w -> p b (l w)", b=2),
                         st["psum"][:, :, 0:2 * st["width"]], ACT.Copy).then_inc(st["sums_ready"], 1)


def merge_scatter(st, nc, pool, accumulator, n, s):
    pool.wait_ge(st["sums_ready"], n + 1)
    pool.wait_ge(st["target_ready"], n + 1)
    if reused(n, 1):
        pool.wait_ge(st["scattered"], n * LANES * 16)
    pool.sem_inc(st["pool_passed"])
    for lane in range(LANES):
        pool.indirect_dma_start(accumulator, bass.IndirectOffsetOnAxis(ap=st["target"][:, s, lane:lane + 1], axis=0),
                                st["sums"][:, s % 2, lane, :], None, compute_op=ALU.add).then_inc(st["scattered"], 16)


def gather(pool, rows, table, numbers, lanes, done):
    for lane in range(lanes):
        pool.indirect_dma_start(rows[:, lane, :], None, table, bass.IndirectOffsetOnAxis(ap=numbers[:, lane:lane + 1], axis=0)).then_inc(done, 16)


def zero_state(sbuf, psum, sem, accumulator, n_blocks):
    st = {}
    st["acc"] = accumulator
    st["n_blocks"] = n_blocks
    if accumulator is not None:
        st["rows"], st["width"] = accumulator.shape
        st["part"] = st["rows"] // BLOCK
        st["per"] = -(-st["part"] // n_blocks)
        st["zeros"] = sbuf("zeros", [P, LANES * st["width"]])
        st["zeros_set"] = sem("zeros_set")
        st["zeroed"] = sem("zeroed")
    return st


def zero_fill(st, nc):
    if st["acc"] is not None:
        nc.vector.memset(st["zeros"][:, :], 0.0).then_inc(st["zeros_set"], 1)


def zero_begin(st, sp):
    if st["acc"] is not None:
        sp.wait_ge(st["zeros_set"], 1)


def zero_step(st, sp, first, count):
    if st["acc"] is not None:
        parts = st["acc"].rearrange("(c p r) d -> c p (r d)", p=P, r=LANES)
        for c in range(count):
            sp.dma_start(parts[bass.ds(first + c, 1), :, :].rearrange("c p w -> (c p) w"), st["zeros"][:, :]).then_inc(st["zeroed"], 16)


def zero_end(st, sp):
    if st["acc"] is not None:
        done = st["part"] // st["n_blocks"] * st["n_blocks"]
        zero_step(st, sp, done, st["part"] - done)
        sp.wait_ge(st["zeroed"], 16 * st["part"])


def flat(tile):
    return tile.rearrange("p r d -> p (r d)")


def banks(psum):
    return psum.rearrange("p b (r d) -> p (b r) d", d=D)


def gcn_layer(nc, k, name, ends, key_rows, table, accumulator, zero_next, weight, bias, x, outs, n_blocks, n_chunks, together):
    with phase(nc, name) as (sbuf, psum, sem):
        end = sbuf("end", [P, SLOTS, 2 * LANES], I32)
        rows = sbuf("rows", [P, SLOTS, LANES, D])
        ends_in = [sem(f"ends_in{s}") for s in range(SLOTS)]
        gathered = [sem(f"gathered{s}") for s in range(SLOTS)]
        mg = merge_state(sbuf, psum, sem, D)
        mg["pool_passed"] = sem("pool_passed")
        zero = zero_state(sbuf, psum, sem, zero_next, n_blocks)
        acc = sbuf("acc", [P, SLOTS, ROWS, D])
        xs = sbuf("xs", [P, SLOTS, ROWS, D]) if x is not None else None
        acc_T = sbuf("acc_T", [P, ROWS, D])
        y = sbuf("y", [P, ROWS, D])
        result = sbuf("result", [P, SLOTS, ROWS, D])
        turned = [psum(f"turned{s}", [P, 2, 512]) for s in range(2)]
        product = psum("product", [P, 2, 512])
        loaded = [sem(f"loaded{s}") for s in range(SLOTS)]
        stored = [sem(f"stored{s}") for s in range(SLOTS)]
        transposed, copied, multiplied, biased, finished = (
            sem(s) for s in ("transposed", "copied", "multiplied", "biased", "finished"))
        loads = 1 + (x is not None)
        stores = len(outs)
        behind = SLOTS + BEHIND + 1

        def pass_over(eng, edge_stages, node_stages):
            if together:
                walk(eng, n_blocks, [(behind + lag, step) for lag, step in node_stages] + edge_stages)
            else:
                walk(eng, n_blocks, edge_stages)
                walk(eng, n_chunks, node_stages)

        with nc.Block() as block:

            @block.sync
            def _(sp):
                zero_begin(zero, sp)

                def load_edges(n, s, turn):
                    if reused(n, SLOTS):
                        sp.wait_ge(mg["scattered"], (n - SLOTS + 1) * LANES * 16)
                    sp.dma_start(end[:, s, :], ends[bass.ds(n, 1), :, :].rearrange("b p w -> (b p) w")).then_inc(ends_in[s], 16)
                    merge_load(mg, sp, key_rows, n, s)

                def clear(n, s, turn):
                    if zero["acc"] is not None:
                        each = zero["part"] // n_blocks
                        zero_step(zero, sp, n * each, each)

                def load(n, s, turn):
                    if together:
                        last = n + BEHIND if not isinstance(n, int) else min(n + BEHIND, n_blocks - 1)
                        sp.wait_ge(mg["scattered"], (last + 1) * LANES * 16)
                    elif isinstance(n, int) and n == 0:
                        sp.wait_ge(mg["scattered"], n_blocks * LANES * 16)
                    sp.dma_start(flat(acc[:, s, :, :]), chunk_of(accumulator, n)).then_inc(loaded[s], 16)
                    if x is not None:
                        sp.dma_start(flat(xs[:, s, :, :]), chunk_of(x, n)).then_inc(loaded[s], 16)

                def store(n, s, turn):
                    sp.wait_ge(finished, n + 1)
                    for out in outs:
                        sp.dma_start(chunk_of(out, n), flat(result[:, s, :, :])).then_inc(stored[s], 16)

                pass_over(sp, [(0, load_edges), (0, clear)], [(0, load), (4, store)])
                zero_end(zero, sp)
                for s in range(SLOTS):
                    sp.wait_ge(stored[s], 16 * stores * uses(n_chunks, s))

            @block.gpsimd
            def _(pool):
                def fetch(n, s, turn):
                    if reused(n, SLOTS):
                        pool.wait_ge(mg["merged"], n - SLOTS + 1)
                    pool.wait_ge(ends_in[s], turn * 16 + 16)
                    pool.sem_inc(mg["pool_passed"])
                    gather(pool, rows[:, s, :, :], table, end[:, s, 0:LANES], LANES, gathered[s])

                def add(n, s, turn):
                    merge_scatter(mg, nc, pool, accumulator, n, s)

                walk(pool, n_blocks, [(0, fetch), (1, add)])
                pool.wait_ge(mg["scattered"], n_blocks * LANES * 16)

            @block.vector
            def _(dve):
                zero_fill(zero, nc)

                def compare(n, s, turn):
                    dve.wait_ge(ends_in[s], turn * 16 + 16)
                    merge_compare(mg, nc, dve, k, end[:, s, LANES:], n, s, turn)

                def add_bias(n, s, turn):
                    dve.wait_ge(multiplied, n + 1)
                    if reused(n, 1):
                        dve.wait_ge(finished, n)
                    for r in range(ROWS):
                        last = nc.vector.scalar_tensor_tensor(out=y[:, r, :], in0=banks(product[:, :, :])[:, r, :],
                                                              scalar=k["dis"][:, bass.ds(n * ROWS + r, 1)], in1=bias,
                                                              op0=ALU.mult, op1=ALU.add)
                    last.then_inc(biased, 1)
                    if x is not None:
                        dve.wait_ge(biased, n + 1)
                        if reused(n, SLOTS):
                            dve.wait_ge(stored[s], turn * 16 * stores)
                        nc.vector.scalar_tensor_tensor(out=flat(result[:, s, :, :]), in0=flat(y[:, :, :]), scalar=0.0,
                                                       in1=flat(xs[:, s, :, :]), op0=ALU.max, op1=ALU.add).then_inc(finished, 1)

                pass_over(dve, [(0, compare)], [(2, add_bias)])

            @block.tensor
            def _(pe):
                def merge(n, s, turn):
                    pe.wait_ge(gathered[s], (turn + 1) * LANES * 16)
                    merge_merge(mg, nc, pe, lambda lane: rows[:, s, lane, :], n, s)

                def turn_over(n, s, turn):
                    pe.wait_ge(loaded[s], (turn + 1) * 16 * loads)
                    if reused(n, 2):
                        pe.wait_ge(copied, n - 1)
                    for r in range(ROWS):
                        last = nc.tensor.transpose(banks(turned[s % 2][:, :, :])[:, r, :], acc[:, s, r, :], k["identity"][:, :])
                    last.then_inc(transposed, 1)

                def multiply(n, s, turn):
                    pe.wait_ge(copied, n + 1)
                    if reused(n, 1):
                        pe.wait_ge(biased, n)
                    for r in range(ROWS):
                        last = nc.tensor.matmul(banks(product[:, :, :])[:, r, :], acc_T[:, r, :], weight, start=True, stop=True)
                    last.then_inc(multiplied, 1)

                pass_over(pe, [(0, merge)], [(1, multiply), (0, turn_over)])

            @block.scalar
            def _(act):
                def copy(n, s, turn):
                    act.wait_ge(transposed, n + 1)
                    if reused(n, 1):
                        act.wait_ge(multiplied, n)
                    nc.scalar.activation(flat(acc_T[:, :, :]), turned[s % 2][:, :, :].rearrange("p b w -> p (b w)"),
                                         ACT.Copy).then_inc(copied, 1)

                def rectify(n, s, turn):
                    act.wait_ge(biased, n + 1)
                    if reused(n, SLOTS):
                        act.wait_ge(stored[s], turn * 16 * stores)
                    for r in range(ROWS):
                        last = nc.scalar.activation(result[:, s, r, :], y[:, r, :], ACT.Relu,
                                                    scale=k["dis"][:, bass.ds(n * ROWS + r, 1)])
                    last.then_inc(finished, 1)

                pass_over(act, [(0, lambda n, s, turn: merge_keep(mg, nc, act, n, s))],
                          ([(2, rectify)] if x is None else []) + [(0, copy)])


def attention_over_edges(nc, k, name, ends, key_rows, edge_weight, nodes, weights, bias, accumulator, zero_next, n_blocks):
    with phase(nc, name) as (sbuf, psum, sem):
        end = sbuf("end", [P, SLOTS, 2 * LANES], I32)
        rows = sbuf("rows", [P, SLOTS, 2 * LANES, D])
        normed = sbuf("normed", [P, 2 * LANES, D])
        normed_T = sbuf("normed_T", [P, 2 * LANES, D])
        query = sbuf("query", [P, LANES, D])
        terms = sbuf("terms", [P, LANES, D])
        dots = sbuf("dots", [P, LANES, HEADS])
        weighted = sbuf("weighted", [P, LANES, HEADS])
        clipped = sbuf("clipped", [P, LANES, HEADS])
        message = sbuf("message", [P, 2, LANES, SUMS])
        factor = sbuf("factor", [P, SLOTS, LANES])
        turned = psum("turned", [P, 2, 512])
        kvq = psum("kvq", [P, LANES, 512])
        ends_in = [sem(f"ends_in{s}") for s in range(SLOTS)]
        gathered = [sem(f"gathered{s}") for s in range(SLOTS)]
        transposed, copied, projected, query_ready, terms_ready, dots_ready, weighted_ready, clipped_ready, score_ready, \
            message_ready = (sem(x) for x in (
                "transposed", "copied", "projected", "query_ready", "terms_ready", "dots_ready", "weighted_ready",
                "clipped_ready", "score_ready", "message_ready"))
        ln = ln_state(sbuf, psum, sem, 2 * LANES)
        mg = merge_state(sbuf, psum, sem, SUMS)
        mg["pool_passed"] = sem("pool_passed")
        zero = zero_state(sbuf, psum, sem, zero_next, n_blocks)
        end_loads = 1 + (edge_weight is not None)
        w_at = MATRICES.index(weights)
        w_kv = k["matrices"][:, w_at:w_at + 2, :].rearrange("p m d -> p (m d)")
        w_q = k["matrices"][:, w_at + 2, :]
        with nc.Block() as block:

            @block.sync
            def _(sp):
                zero_begin(zero, sp)

                def load(n, s, turn):
                    if reused(n, SLOTS):
                        sp.wait_ge(mg["target_ready"], n - SLOTS + 1)
                    sp.dma_start(end[:, s, :], ends[bass.ds(n, 1), :, :].rearrange("b p w -> (b p) w")).then_inc(ends_in[s], 16)
                    if edge_weight is not None:
                        sp.dma_start(factor[:, s, :], edge_weight[bass.ds(n, 1), :, :].rearrange("b p w -> (b p) w")).then_inc(ends_in[s], 16)
                    merge_load(mg, sp, key_rows, n, s)

                def clear(n, s, turn):
                    if zero["acc"] is not None:
                        each = zero["part"] // n_blocks
                        zero_step(zero, sp, n * each, each)

                walk(sp, n_blocks, [(0, load), (0, clear)])
                zero_end(zero, sp)

            @block.gpsimd
            def _(pool):
                def fetch(n, s, turn):
                    if reused(n, SLOTS):
                        pool.wait_ge(ln["applied"], n - SLOTS + 1)
                    pool.wait_ge(ends_in[s], (turn + 1) * 16 * end_loads)
                    pool.sem_inc(mg["pool_passed"])
                    gather(pool, rows[:, s, :, :], nodes, end[:, s, :], 2 * LANES, gathered[s])

                walk(pool, n_blocks, [(0, fetch), (5, lambda n, s, turn: merge_scatter(mg, nc, pool, accumulator, n, s))])
                pool.wait_ge(mg["scattered"], n_blocks * LANES * 16)

            @block.vector
            def _(dve):
                zero_fill(zero, nc)
                ln_set_eps(ln, nc)

                def measure(n, s, turn):
                    dve.wait_ge(gathered[s], (turn + 1) * 2 * LANES * 16)
                    ln_measure(ln, nc, dve, rows[:, s, :, :], n, s)

                def compare(n, s, turn):
                    dve.wait_ge(ends_in[s], (turn + 1) * 16 * end_loads)
                    merge_compare(mg, nc, dve, k, end[:, s, LANES:], n, s, turn)

                def attend(n, s, turn):
                    dve.wait_ge(query_ready, n + 1)
                    nc.vector.tensor_tensor(terms[:, :, :], kvq[:, :, 0:D], query[:, :, :], ALU.mult).then_inc(terms_ready, 1)
                    dve.wait_ge(terms_ready, n + 1)
                    nc.vector.tensor_reduce(dots[:, :, :].rearrange("p l h -> p (l h)"),
                                            terms[:, :, :].rearrange("p l (h d) -> p (l h) d", d=HEAD_DIM),
                                            AXIS_X, ALU.add).then_inc(dots_ready, 1)
                    dve.wait_ge(dots_ready, n + 1)
                    source = dots
                    if edge_weight is not None:
                        nc.vector.tensor_tensor(weighted[:, :, :], dots[:, :, :],
                                                factor[:, s, :].unsqueeze(2).to_broadcast([P, LANES, HEADS]),
                                                ALU.mult).then_inc(weighted_ready, 1)
                        dve.wait_ge(weighted_ready, n + 1)
                        source = weighted
                    if reused(n, 1):
                        dve.wait_ge(score_ready, n)
                    nc.vector.tensor_scalar(clipped[:, :, :], source[:, :, :], 5.0, -5.0, ALU.min, ALU.max).then_inc(clipped_ready, 1)

                def weigh(n, s, turn):
                    dve.wait_ge(score_ready, n + 1)
                    m = message[:, s % 2, :, :]
                    for lane in range(LANES):
                        last = nc.vector.tensor_tensor(m[:, lane, 0:D].rearrange("p (h d) -> p h d", d=HEAD_DIM),
                                                       kvq[:, lane, D:2 * D].rearrange("p (h d) -> p h d", d=HEAD_DIM),
                                                       m[:, lane, D:SUMS].unsqueeze(2).to_broadcast([P, HEADS, HEAD_DIM]), ALU.mult)
                    last.then_inc(message_ready, 1)

                walk(dve, n_blocks, [(3, attend), (1, lambda n, s, turn: ln_centre(ln, nc, dve, n, s)), (3, weigh), (3, compare), (0, measure)])

            @block.tensor
            def _(pe):
                def merge(n, s, turn):
                    pe.wait_ge(message_ready, n + 1)
                    merge_merge(mg, nc, pe, lambda lane: message[:, s % 2, lane, :], n, s)

                def project(n, s, turn):
                    pe.wait_ge(copied, n + 1)
                    if reused(n, 1):
                        pe.wait_ge(message_ready, n)
                    for lane in range(LANES):
                        if bias is not None:
                            nc.tensor.matmul(kvq[:, lane, 0:3 * D], k["ones"][:, :], bias, start=True, stop=False)
                        nc.tensor.matmul(kvq[:, lane, 0:2 * D], normed_T[:, lane, :], w_kv, start=bias is None, stop=bias is None)
                        last = nc.tensor.matmul(kvq[:, lane, 2 * D:3 * D], normed_T[:, LANES + lane, :], w_q,
                                                start=bias is None, stop=True)
                    last.then_inc(projected, 1)

                def turn_over(n, s, turn):
                    pe.wait_ge(ln["applied"], n + 1)
                    for r in range(2 * LANES):
                        last = nc.tensor.transpose(banks(turned[:, :, :])[:, r, :], normed[:, r, :], k["identity"][:, :])
                    last.then_inc(transposed, 1)

                walk(pe, n_blocks, [(4, merge), (2, project), (1, turn_over)])

            @block.scalar
            def _(act):
                act.preload_act_table_set(TABLES)
                act.wait_ge(ln["eps_set"], 1)

                def copy_query(n, s, turn):
                    act.wait_ge(projected, n + 1)
                    if reused(n, 1):
                        act.wait_ge(terms_ready, n)
                    nc.scalar.activation(query[:, :, :], kvq[:, :, 2 * D:3 * D], ACT.Copy).then_inc(query_ready, 1)

                def score(n, s, turn):
                    act.wait_ge(clipped_ready, n + 1)
                    if reused(n, 2):
                        act.wait_ge(mg["merged"], n - 1)
                    nc.scalar.activation(message[:, s % 2, :, D:SUMS], clipped[:, :, :], ACT.Exp).then_inc(score_ready, 1)

                def norm(n, s, turn):
                    if reused(n, 1):
                        act.wait_ge(transposed, n)
                    ln_apply(ln, nc, act, normed[:, :, :], rows[:, s, :, :], n, s)

                def copy(n, s, turn):
                    act.wait_ge(transposed, n + 1)
                    if reused(n, 1):
                        act.wait_ge(projected, n)
                    nc.scalar.activation(flat(normed_T[:, :, :]), turned[:, :, :].rearrange("p b w -> p (b w)"), ACT.Copy).then_inc(copied, 1)

                walk(act, n_blocks, [(3, copy_query), (2, copy), (1, lambda n, s, turn: ln_deviate(ln, nc, act, n, s)),
                                     (3, score), (4, lambda n, s, turn: merge_keep(mg, nc, act, n, s)), (1, norm)])


"""Mean and variance of each feature over all nodes, features on the partitions, and the affine map
of the batch norm that follows from them."""


def bn_state(sbuf, psum, sem, halves):
    st = {}
    st["halves"] = halves
    st["part"] = sbuf("bn_part", [P, SLOTS, 2, 6])
    st["parts"] = sbuf("bn_parts", [P, halves, 6])
    st["moments"] = sbuf("bn_moments", [P, 2])
    st["logvar"] = sbuf("bn_logvar", [P, 1])
    st["rstd"] = sbuf("bn_rstd", [P, 1])
    st["shift"] = sbuf("bn_shift", [P, 1])
    st["eps"] = sbuf("bn_eps", [P, 1])
    st["part_done"], st["parts_done"], st["eps_set"], st["moments_done"], st["log_done"], st["rstd_done"], st["scale_done"], \
        st["shift_done"] = (sem(f"bn_{x}") for x in (
            "part_done", "parts_done", "eps_set", "moments_done", "log_done", "rstd_done", "scale_done", "shift_done"))
    return st


def bn_add(st, nc, dve, pieces, n, s):
    for i, piece in enumerate(pieces):
        last = nc.vector.bn_stats(st["part"][:, s, i, :], piece)
    last.then_inc(st["part_done"], 1)
    dve.wait_ge(st["part_done"], n + 1)
    c = len(pieces)
    nc.vector.tensor_scalar(st["parts"][:, bass.ds(n * c, c), :], st["part"][:, s, 0:c, :], 1.0, None, ALU.mult).then_inc(st["parts_done"], 1)


def bn_finish_vector(st, nc, dve, tiles, gain, offset, scale_out, shift_out):
    dve.wait_ge(st["parts_done"], tiles)
    nc.vector.bn_aggr(st["moments"][:, :], st["parts"][:, :, :].rearrange("p c w -> p (c w)")).then_inc(st["moments_done"], 1)
    dve.wait_ge(st["rstd_done"], 1)
    nc.vector.tensor_tensor(scale_out, st["rstd"][:, :], gain, ALU.mult).then_inc(st["scale_done"], 1)
    dve.wait_ge(st["scale_done"], 1)
    nc.vector.tensor_tensor(st["shift"][:, :], st["moments"][:, 0:1], scale_out, ALU.mult).then_inc(st["shift_done"], 1)
    dve.wait_ge(st["shift_done"], 1)
    nc.vector.tensor_tensor(shift_out, offset, st["shift"][:, :], ALU.subtract).then_inc(st["shift_done"], 1)


def bn_finish_scalar(st, nc, act):
    act.wait_ge(st["moments_done"], 1)
    nc.scalar.activation(st["logvar"][:, :], st["moments"][:, 1:2], ACT.Ln, bias=st["eps"][:, 0:1]).then_inc(st["log_done"], 1)
    act.wait_ge(st["log_done"], 1)
    nc.scalar.activation(st["rstd"][:, :], st["logvar"][:, :], ACT.Exp, scale=-0.5).then_inc(st["rstd_done"], 1)


def heads_state(sbuf, psum, sem):
    st = {}
    st["weight"] = sbuf("head_weight", [P, SLOTS, ROWS, HEADS])
    st["inverse"] = sbuf("head_inverse", [P, SLOTS, ROWS, HEADS])
    st["weight_done"], st["inverse_done"], st["mean_done"] = (sem(f"head_{x}") for x in ("weight_done", "inverse_done", "mean_done"))
    return st


def heads_weigh(st, nc, sums, s):
    nc.vector.tensor_scalar(st["weight"][:, s, :, :], sums[:, :, D:SUMS], Z_EPS, None, ALU.add).then_inc(st["weight_done"], 1)


def heads_invert(st, nc, dve, n, s):
    dve.wait_ge(st["weight_done"], n + 1)
    nc.vector.reciprocal(st["inverse"][:, s, :, :], st["weight"][:, s, :, :]).then_inc(st["inverse_done"], 1)


def heads_mean(st, eng, out, sums, n, s):
    eng.wait_ge(st["inverse_done"], n + 1)
    eng.tensor_tensor(out.rearrange("p r (h d) -> p r h d", d=HEAD_DIM),
                      sums[:, :, 0:D].rearrange("p r (h d) -> p r h d", d=HEAD_DIM),
                      st["inverse"][:, s, :, :].unsqueeze(3).to_broadcast([P, ROWS, HEADS, HEAD_DIM]),
                      ALU.mult).then_inc(st["mean_done"], 1)


def column_chunk(table, n, width=CHUNK):
    return table[bass.ds(n, 1), :, :].rearrange("c p w -> (c p) w")


def attention1_nodes(nc, k, x, sums, y_T, n_chunks, last_valid):
    with phase(nc, "l1_nodes") as (sbuf, psum, sem):
        xs = sbuf("xs", [P, SLOTS, ROWS, D])
        acc = sbuf("acc", [P, SLOTS, ROWS, SUMS])
        att = sbuf("att", [P, 2, ROWS, D])
        att_T = sbuf("att_T", [P, 2, 2, 512])
        normed = sbuf("normed", [P, 2, ROWS, D])
        y = sbuf("y", [P, SLOTS, CHUNK])
        turned = [psum(f"turned{s}", [P, 2, 512]) for s in range(2)]
        total = [psum(f"total{s}", [P, 2, 512]) for s in range(2)]
        loaded = [sem(f"loaded{s}") for s in range(SLOTS)]
        stored = [sem(f"stored{s}") for s in range(SLOTS)]
        transposed, copied_low, copied_high, totalled, y_ready = (
            sem(x) for x in ("transposed", "copied_low", "copied_high", "totalled", "y_ready"))
        ln = ln_state(sbuf, psum, sem, ROWS)
        heads = heads_state(sbuf, psum, sem)
        bn = bn_state(sbuf, psum, sem, 2 * n_chunks)
        with nc.Block() as block:

            @block.sync
            def _(sp):
                def load(n, s, turn):
                    if reused(n, SLOTS):
                        sp.wait_ge(totalled, n - SLOTS + 1)
                    sp.dma_start(flat(xs[:, s, :, :]), chunk_of(x, n)).then_inc(loaded[s], 16)
                    sp.dma_start(flat(acc[:, s, :, :]), chunk_of(sums, n)).then_inc(loaded[s], 16)

                def store(n, s, turn):
                    sp.wait_ge(y_ready, n + 1)
                    sp.dma_start(column_chunk(y_T, n), y[:, s, :]).then_inc(stored[s], 16)

                walk(sp, n_chunks, [(0, load), (6, store)])
                for s in range(SLOTS):
                    sp.wait_ge(stored[s], 16 * uses(n_chunks, s))

            @block.vector
            def _(dve):
                nc.vector.memset(bn["eps"][:, :], BN_EPS)
                ln_set_eps(ln, nc)

                def weigh(n, s, turn):
                    dve.wait_ge(loaded[s], (turn + 1) * 32)
                    heads_weigh(heads, nc, acc[:, s, :, :], s)

                def stats(n, s, turn):
                    dve.wait_ge(y_ready, n + 1)
                    halves = [y[:, s, h * 512:(h + 1) * 512] for h in range(2)]
                    if isinstance(n, int) and n == n_chunks - 1:
                        halves = [h.rearrange("p (r q) -> p r q", q=P)[:, :, 0:last_valid] for h in halves]
                    bn_add(bn, nc, dve, halves, n, s)

                def copy_high(n, s, turn):
                    dve.wait_ge(transposed, n + 1)
                    if reused(n, 2):
                        dve.wait_ge(totalled, n - 1)
                    nc.vector.tensor_copy(att_T[:, s % 2, 1, :], turned[s % 2][:, 1, :]).then_inc(copied_high, 1)

                walk(dve, n_chunks, [(0, weigh), (2, lambda n, s, turn: ln_centre(ln, nc, dve, n, s)),
                                     (1, lambda n, s, turn: ln_sums(ln, nc, dve, n, s)),
                                     (0, lambda n, s, turn: heads_invert(heads, nc, dve, n, s)),
                                     (1, lambda n, s, turn: ln_between(ln, nc, dve, n, s)),
                                     (5, stats),
                                     (1, lambda n, s, turn: ln_var(ln, nc, dve, n, s)),
                                     (1, copy_high),
                                     (0, lambda n, s, turn: ln_count(ln, nc, xs[:, s, :, :], s))])
                bn_finish_vector(bn, nc, dve, n_chunks, k["col"]["l1_g1"], k["col"]["l1_b1"], k["bn"][:, 0:1], k["bn"][:, 1:2])

            @block.gpsimd
            def _(pool):
                def mean(n, s, turn):
                    if reused(n, 2):
                        pool.wait_ge(transposed, n - 1)
                    heads_mean(heads, nc.gpsimd, att[:, s % 2, :, :], acc[:, s, :, :], n, s)

                walk(pool, n_chunks, [(0, mean)])

            @block.tensor
            def _(pe):
                def turn_over(n, s, turn):
                    pe.wait_ge(heads["mean_done"], n + 1)
                    if reused(n, 2):
                        pe.wait_ge(copied_low, n - 1)
                        pe.wait_ge(copied_high, n - 1)
                    for r in range(ROWS):
                        last = nc.tensor.transpose(banks(turned[s % 2][:, :, :])[:, r, :], att[:, s % 2, r, :], k["identity"][:, :])
                    last.then_inc(transposed, 1)

                def add_up(n, s, turn):
                    pe.wait_ge(copied_low, n + 1)
                    pe.wait_ge(copied_high, n + 1)
                    pe.wait_ge(ln["applied"], n + 1)
                    if reused(n, 2):
                        pe.wait_ge(y_ready, n - 1)
                    for h in range(2):
                        nc.tensor.matmul(total[s % 2][:, h, :], k["W"]["l1_o"], att_T[:, s % 2, h, :], start=True, stop=False)
                        for r in range(LANES):
                            last = nc.tensor.matmul(total[s % 2][:, h, r * P:(r + 1) * P], normed[:, s % 2, h * LANES + r, :],
                                                    k["identity"][:, :], start=False, stop=r == LANES - 1)
                    last.then_inc(totalled, 1)

                walk(pe, n_chunks, [(3, add_up), (1, turn_over)])

            @block.scalar
            def _(act):
                act.preload_act_table_set(TABLES)
                act.wait_ge(ln["eps_set"], 1)

                def copy_low(n, s, turn):
                    act.wait_ge(transposed, n + 1)
                    if reused(n, 2):
                        act.wait_ge(totalled, n - 1)
                    nc.scalar.activation(att_T[:, s % 2, 0, :], turned[s % 2][:, 0, :], ACT.Copy).then_inc(copied_low, 1)

                def norm(n, s, turn):
                    if reused(n, 2):
                        act.wait_ge(totalled, n - 1)
                    ln_apply(ln, nc, act, normed[:, s % 2, :, :], xs[:, s, :, :], n, s)

                def take(n, s, turn):
                    act.wait_ge(totalled, n + 1)
                    if reused(n, SLOTS):
                        act.wait_ge(stored[s], turn * 16)
                        act.wait_ge(bn["part_done"], n - SLOTS + 1)
                    nc.scalar.activation(y[:, s, :], total[s % 2][:, :, :].rearrange("p b w -> p (b w)"), ACT.Identity,
                                         bias=k["col"]["l1_bo"]).then_inc(y_ready, 1)

                walk(act, n_chunks, [(4, take), (2, norm), (1, lambda n, s, turn: ln_deviate(ln, nc, act, n, s)), (1, copy_low)])
                bn_finish_scalar(bn, nc, act)


def feed_forward(nc, k, y_T, z_T, n_chunks, last_valid):
    tiles = 2 * n_chunks
    half = CHUNK // 2
    with phase(nc, "ffn") as (sbuf, psum, sem):
        ys = sbuf("ys", [P, SLOTS, half])
        normed = sbuf("normed", [P, SLOTS, half])
        hidden = sbuf("hidden", [P, 2, 2, half])
        z = sbuf("z", [P, SLOTS, half])
        up = [psum(f"up{s}", [P, 2, 512]) for s in range(2)]
        down = [psum(f"down{s}", [P, 512]) for s in range(2)]
        loaded = [sem(f"loaded{s}") for s in range(SLOTS)]
        stored = [sem(f"stored{s}") for s in range(SLOTS)]
        normed_ready, raised, hidden_ready, lowered, z_ready, eps_set = (
            sem(x) for x in ("normed_ready", "raised", "hidden_ready", "lowered", "z_ready", "eps_set"))
        bn = bn_state(sbuf, psum, sem, tiles)
        with nc.Block() as block:

            def half_of(table, n_slot_even, chunk):
                return column_chunk(table, chunk)[:, n_slot_even * half:(n_slot_even + 1) * half]

            @block.sync
            def _(sp):
                def load(n, s, turn):
                    if reused(n, SLOTS):
                        sp.wait_ge(normed_ready, n - SLOTS + 1)
                    sp.dma_start(ys[:, s, :], half_of(y_T, s % 2, turn * (SLOTS // 2) + s // 2)).then_inc(loaded[s], 16)

                def store(n, s, turn):
                    sp.wait_ge(z_ready, n + 1)
                    sp.dma_start(half_of(z_T, s % 2, turn * (SLOTS // 2) + s // 2), z[:, s, :]).then_inc(stored[s], 16)

                walk(sp, tiles, [(0, load), (3, store)])
                for s in range(SLOTS):
                    sp.wait_ge(stored[s], 16 * uses(tiles, s))

            @block.vector
            def _(dve):
                nc.vector.memset(bn["eps"][:, :], BN_EPS).then_inc(eps_set, 1)

                def norm(n, s, turn):
                    dve.wait_ge(loaded[s], (turn + 1) * 16)
                    nc.vector.tensor_scalar(normed[:, s, :], ys[:, s, :], k["bn"][:, 0:1], k["bn"][:, 1:2], ALU.mult, ALU.add).then_inc(normed_ready, 1)

                def add(n, s, turn):
                    dve.wait_ge(lowered, n + 1)
                    if reused(n, SLOTS):
                        dve.wait_ge(stored[s], turn * 16)
                    nc.vector.scalar_tensor_tensor(out=z[:, s, :], in0=down[s % 2][:, :], scalar=k["col"]["l1_bf2"],
                                                   in1=normed[:, s, :], op0=ALU.add, op1=ALU.add).then_inc(z_ready, 1)
                    dve.wait_ge(z_ready, n + 1)
                    piece = z[:, s, :]
                    if isinstance(n, int) and n >= tiles - 2:
                        piece = piece.rearrange("p (r q) -> p r q", q=P)[:, :, 0:last_valid]
                    bn_add(bn, nc, dve, [piece], n, s)

                walk(dve, tiles, [(0, norm), (2, add)])
                bn_finish_vector(bn, nc, dve, tiles, k["col"]["l1_g2"], k["col"]["l1_b2"], k["bn"][:, 2:3], k["bn"][:, 3:4])

            @block.tensor
            def _(pe):
                def raise_(n, s, turn):
                    pe.wait_ge(normed_ready, n + 1)
                    if reused(n, 2):
                        pe.wait_ge(hidden_ready, n - 1)
                    for f in range(2):
                        last = nc.tensor.matmul(up[s % 2][:, f, :], k["W"][f"ffn_up{f}"], normed[:, s, :], start=True, stop=True)
                    last.then_inc(raised, 1)

                def lower(n, s, turn):
                    pe.wait_ge(hidden_ready, n + 1)
                    if reused(n, 2):
                        pe.wait_ge(z_ready, n - 1)
                    for f in range(2):
                        last = nc.tensor.matmul(down[s % 2][:, :], k["W"][f"ffn_down{f}"], hidden[:, s % 2, f, :], start=f == 0, stop=f == 1)
                    last.then_inc(lowered, 1)

                walk(pe, tiles, [(0, raise_), (1, lower)])

            @block.scalar
            def _(act):
                act.preload_act_table_set(TABLES)

                def rectify(n, s, turn):
                    act.wait_ge(raised, n + 1)
                    if reused(n, 2):
                        act.wait_ge(lowered, n - 1)
                    for f, b in enumerate(("l1_bf1a", "l1_bf1b")):
                        last = nc.scalar.activation(hidden[:, s % 2, f, :], up[s % 2][:, f, :], ACT.Relu, bias=k["col"][b])
                    last.then_inc(hidden_ready, 1)

                walk(act, tiles, [(0, rectify)])
                act.wait_ge(eps_set, 1)
                bn_finish_scalar(bn, nc, act)


def add_layer1(nc, k, x, z_T, out, n_chunks):
    with phase(nc, "l1_add") as (sbuf, psum, sem):
        xs = sbuf("xs", [P, SLOTS, ROWS, D])
        zs = sbuf("zs", [P, SLOTS, ROWS, D])
        normed = sbuf("normed", [P, 2, ROWS, D])
        result = sbuf("result", [P, SLOTS, ROWS, D])
        turned = [psum(f"turned{s}", [P, 2, 512]) for s in range(2)]
        loaded = [sem(f"loaded{s}") for s in range(SLOTS)]
        stored = [sem(f"stored{s}") for s in range(SLOTS)]
        normed_ready, transposed, finished = (sem(x) for x in ("normed_ready", "transposed", "finished"))
        with nc.Block() as block:

            @block.sync
            def _(sp):
                def load(n, s, turn):
                    if reused(n, SLOTS):
                        sp.wait_ge(finished, n - SLOTS + 1)
                    sp.dma_start(flat(zs[:, s, :, :]), column_chunk(z_T, n)).then_inc(loaded[s], 16)
                    sp.dma_start(flat(xs[:, s, :, :]), chunk_of(x, n)).then_inc(loaded[s], 16)

                def store(n, s, turn):
                    sp.wait_ge(finished, n + 1)
                    sp.dma_start(chunk_of(out, n), flat(result[:, s, :, :])).then_inc(stored[s], 16)

                walk(sp, n_chunks, [(0, load), (2, store)])
                for s in range(SLOTS):
                    sp.wait_ge(stored[s], 16 * uses(n_chunks, s))

            @block.scalar
            def _(act):
                def norm(n, s, turn):
                    act.wait_ge(loaded[s], (turn + 1) * 32)
                    if reused(n, 2):
                        act.wait_ge(transposed, n - 1)
                    nc.scalar.activation(flat(normed[:, s % 2, :, :]), flat(zs[:, s, :, :]), ACT.Identity, bias=k["bn"][:, 3:4],
                                         scale=k["bn"][:, 2:3]).then_inc(normed_ready, 1)

                walk(act, n_chunks, [(0, norm)])

            @block.tensor
            def _(pe):
                def turn_over(n, s, turn):
                    pe.wait_ge(normed_ready, n + 1)
                    if reused(n, 2):
                        pe.wait_ge(finished, n - 1)
                    for r in range(ROWS):
                        last = nc.tensor.transpose(banks(turned[s % 2][:, :, :])[:, r, :], normed[:, s % 2, r, :], k["identity"][:, :])
                    last.then_inc(transposed, 1)

                walk(pe, n_chunks, [(0, turn_over)])

            @block.vector
            def _(dve):
                def add(n, s, turn):
                    dve.wait_ge(transposed, n + 1)
                    if reused(n, SLOTS):
                        dve.wait_ge(stored[s], turn * 16)
                    nc.vector.tensor_tensor(flat(result[:, s, :, :]), turned[s % 2][:, :, :].rearrange("p b w -> p (b w)"),
                                            flat(xs[:, s, :, :]), ALU.add).then_inc(finished, 1)

                walk(dve, n_chunks, [(0, add)])


def attention2_nodes(nc, k, x, sums, x_out, accumulator, n_chunks):
    with phase(nc, "l2_nodes") as (sbuf, psum, sem):
        xs = sbuf("xs", [P, SLOTS, ROWS, D])
        acc = sbuf("acc", [P, SLOTS, ROWS, SUMS])
        att = sbuf("att", [P, 2, ROWS, D])
        new = sbuf("new", [P, SLOTS, ROWS, D])
        normed = sbuf("normed", [P, 2, ROWS, D])
        normed_T = sbuf("normed_T", [P, 2, ROWS, D])
        own = sbuf("own", [P, SLOTS, ROWS, D])
        turned = [psum(f"turned{s}", [P, 2, 512]) for s in range(2)]
        product = [psum(f"product{s}", [P, 2, 512]) for s in range(2)]
        loaded = [sem(f"loaded{s}") for s in range(SLOTS)]
        new_stored = [sem(f"new_stored{s}") for s in range(SLOTS)]
        own_stored = [sem(f"own_stored{s}") for s in range(SLOTS)]
        new_ready, transposed, copied, multiplied, own_ready = (
            sem(x) for x in ("new_ready", "transposed", "copied", "multiplied", "own_ready"))
        ln = ln_state(sbuf, psum, sem, ROWS)
        heads = heads_state(sbuf, psum, sem)
        with nc.Block() as block:

            @block.sync
            def _(sp):
                def load(n, s, turn):
                    if reused(n, SLOTS):
                        sp.wait_ge(new_ready, n - SLOTS + 1)
                    sp.dma_start(flat(xs[:, s, :, :]), chunk_of(x, n)).then_inc(loaded[s], 16)
                    sp.dma_start(flat(acc[:, s, :, :]), chunk_of(sums, n)).then_inc(loaded[s], 16)

                def store_new(n, s, turn):
                    sp.wait_ge(new_ready, n + 1)
                    sp.dma_start(chunk_of(x_out, n), flat(new[:, s, :, :])).then_inc(new_stored[s], 16)

                def store_own(n, s, turn):
                    sp.wait_ge(own_ready, n + 1)
                    sp.dma_start(chunk_of(accumulator, n), flat(own[:, s, :, :])).then_inc(own_stored[s], 16)

                walk(sp, n_chunks, [(0, load), (2, store_new), (6, store_own)])
                for s in range(SLOTS):
                    sp.wait_ge(new_stored[s], 16 * uses(n_chunks, s))
                    sp.wait_ge(own_stored[s], 16 * uses(n_chunks, s))

            @block.vector
            def _(dve):
                ln_set_eps(ln, nc)

                def weigh(n, s, turn):
                    dve.wait_ge(loaded[s], (turn + 1) * 32)
                    heads_weigh(heads, nc, acc[:, s, :, :], s)

                def mean(n, s, turn):
                    heads_mean(heads, nc.vector, att[:, s % 2, :, :], acc[:, s, :, :], n, s)

                def add(n, s, turn):
                    dve.wait_ge(heads["mean_done"], n + 1)
                    if reused(n, SLOTS):
                        dve.wait_ge(new_stored[s], turn * 16)
                        dve.wait_ge(ln["applied"], n - SLOTS + 1)
                    nc.vector.tensor_tensor(flat(new[:, s, :, :]), flat(xs[:, s, :, :]), flat(att[:, s % 2, :, :]), ALU.add).then_inc(new_ready, 1)

                def count(n, s, turn):
                    dve.wait_ge(new_ready, n + 1)
                    ln_count(ln, nc, new[:, s, :, :], s)

                walk(dve, n_chunks, [(0, weigh), (3, lambda n, s, turn: ln_centre(ln, nc, dve, n, s)),
                                     (2, lambda n, s, turn: ln_sums(ln, nc, dve, n, s)),
                                     (0, lambda n, s, turn: heads_invert(heads, nc, dve, n, s)),
                                     (2, lambda n, s, turn: ln_between(ln, nc, dve, n, s)), (1, add),
                                     (2, lambda n, s, turn: ln_var(ln, nc, dve, n, s)), (0, mean), (1, count)])

            @block.tensor
            def _(pe):
                def turn_over(n, s, turn):
                    pe.wait_ge(ln["applied"], n + 1)
                    if reused(n, 2):
                        pe.wait_ge(copied, n - 1)
                    for r in range(ROWS):
                        last = nc.tensor.transpose(banks(turned[s % 2][:, :, :])[:, r, :], normed[:, s % 2, r, :], k["identity"][:, :])
                    last.then_inc(transposed, 1)

                def multiply(n, s, turn):
                    pe.wait_ge(copied, n + 1)
                    if reused(n, 2):
                        pe.wait_ge(own_ready, n - 1)
                    for r in range(ROWS):
                        nc.tensor.matmul(banks(product[s % 2][:, :, :])[:, r, :], k["ones"][:, :], k["bias"]["l3_b_c"], start=True, stop=False)
                        last = nc.tensor.matmul(banks(product[s % 2][:, :, :])[:, r, :], normed_T[:, s % 2, r, :], k["W"]["l3_c"],
                                                start=False, stop=True)
                    last.then_inc(multiplied, 1)

                walk(pe, n_chunks, [(4, multiply), (3, turn_over)])

            @block.scalar
            def _(act):
                act.preload_act_table_set(TABLES)
                act.wait_ge(ln["eps_set"], 1)

                def norm(n, s, turn):
                    if reused(n, 2):
                        act.wait_ge(transposed, n - 1)
                    ln_apply(ln, nc, act, normed[:, s % 2, :, :], new[:, s, :, :], n, s)

                def copy(n, s, turn):
                    act.wait_ge(transposed, n + 1)
                    if reused(n, 2):
                        act.wait_ge(multiplied, n - 1)
                    nc.scalar.activation(flat(normed_T[:, s % 2, :, :]), turned[s % 2][:, :, :].rearrange("p b w -> p (b w)"),
                                         ACT.Copy).then_inc(copied, 1)

                def take(n, s, turn):
                    act.wait_ge(multiplied, n + 1)
                    if reused(n, SLOTS):
                        act.wait_ge(own_stored[s], turn * 16)
                    nc.scalar.activation(flat(own[:, s, :, :]), product[s % 2][:, :, :].rearrange("p b w -> p (b w)"),
                                         ACT.Copy).then_inc(own_ready, 1)

                walk(act, n_chunks, [(5, take), (4, copy), (3, norm), (2, lambda n, s, turn: ln_deviate(ln, nc, act, n, s))])


def softplus_state(sbuf, psum, sem, width):
    st = {}
    st["size"] = sbuf("sp_size", [P, 2, width])
    st["decay"] = sbuf("sp_decay", [P, 2, width])
    st["tail"] = sbuf("sp_tail", [P, 2, width])
    st["half"] = sbuf("sp_half", [P, 1])
    st["half_set"], st["size_done"], st["decay_done"], st["tail_done"], st["done"] = (
        sem(f"sp_{x}") for x in ("half_set", "size_done", "decay_done", "tail_done", "done"))
    return st


def softplus_set_half(st, nc):
    nc.vector.memset(st["half"][:, :], 0.5).then_inc(st["half_set"], 1)


def softplus_tails(st, nc, act, x, bias, n, s):
    u = s % 2
    nc.scalar.activation(st["size"][:, u, :], x, ACT.Abs, **({} if bias is None else {"bias": bias})).then_inc(st["size_done"], 1)
    act.wait_ge(st["size_done"], n + 1)
    nc.scalar.activation(st["decay"][:, u, :], st["size"][:, u, :], ACT.Exp, scale=-1.0).then_inc(st["decay_done"], 1)
    act.wait_ge(st["decay_done"], n + 1)
    if reused(n, 2):
        act.wait_ge(st["done"], n - 1)
    nc.scalar.activation(st["tail"][:, u, :], st["decay"][:, u, :], ACT.Ln, scale=0.5, bias=st["half"][:, 0:1]).then_inc(st["tail_done"], 1)


def messages_over_edges(nc, k, ends, key_rows, edge_T, nodes, accumulator, n_blocks):
    with phase(nc, "l3_edges") as (sbuf, psum, sem):
        end = sbuf("end", [P, SLOTS, 2 * LANES], I32)
        rows = sbuf("rows", [P, SLOTS, LANES, D])
        edge = sbuf("edge", [64, SLOTS, BLOCK])
        normed = sbuf("normed", [P, LANES, D])
        normed_T = sbuf("normed_T", [P, BLOCK])
        positive = sbuf("positive", [P, BLOCK])
        soft = sbuf("soft", [P, 2, BLOCK])
        value = sbuf("value", [P, BLOCK])
        gated = sbuf("gated", [P, BLOCK])
        message = sbuf("message", [P, 2, LANES, D])
        pre_psum, gate_psum, turned, value_psum, message_psum = (
            psum(x, [P, 512]) for x in ("pre_psum", "gate_psum", "turned", "value_psum", "message_psum"))
        ends_in = [sem(f"ends_in{s}") for s in range(SLOTS)]
        edge_in = [sem(f"edge_in{s}") for s in range(SLOTS)]
        gathered = [sem(f"gathered{s}") for s in range(SLOTS)]
        pre_ready, gate_ready, transposed, copied, value_done, value_ready, gated_ready, message_done, \
            message_ready = (sem(x) for x in (
                "pre_ready", "gate_ready", "transposed", "copied", "value_done", "value_ready",
                "gated_ready", "message_done", "message_ready"))
        ln = ln_state(sbuf, psum, sem, LANES)
        sp_ = softplus_state(sbuf, psum, sem, BLOCK)
        mg = merge_state(sbuf, psum, sem, D)
        mg["pool_passed"] = sem("pool_passed")
        with nc.Block() as block:

            @block.sync
            def _(sp):
                def load(n, s, turn):
                    if reused(n, SLOTS):
                        sp.wait_ge(mg["target_ready"], n - SLOTS + 1)
                    sp.dma_start(end[:, s, :], ends[bass.ds(n, 1), :, :].rearrange("b p w -> (b p) w")).then_inc(ends_in[s], 16)
                    sp.dma_start(edge[:, s, :], edge_T[:, bass.ds(n * BLOCK, BLOCK)]).then_inc(edge_in[s], 16)
                    merge_load(mg, sp, key_rows, n, s)

                walk(sp, n_blocks, [(0, load)])

            @block.gpsimd
            def _(pool):
                def fetch(n, s, turn):
                    if reused(n, SLOTS):
                        pool.wait_ge(ln["applied"], n - SLOTS + 1)
                    pool.wait_ge(ends_in[s], turn * 16 + 16)
                    pool.sem_inc(mg["pool_passed"])
                    gather(pool, rows[:, s, :, :], nodes, end[:, s, LANES:], LANES, gathered[s])

                walk(pool, n_blocks, [(0, fetch), (6, lambda n, s, turn: merge_scatter(mg, nc, pool, accumulator, n, s))])
                pool.wait_ge(mg["scattered"], n_blocks * LANES * 16)

            @block.vector
            def _(dve):
                ln_set_eps(ln, nc)
                softplus_set_half(sp_, nc)

                def soften(n, s, turn):
                    dve.wait_ge(sp_["tail_done"], n + 1)
                    if reused(n, 2):
                        dve.wait_ge(gate_ready, n - 1)
                    nc.vector.tensor_tensor(soft[:, s % 2, :], positive[:, :], sp_["tail"][:, s % 2, :], ALU.add).then_inc(sp_["done"], 1)

                def measure(n, s, turn):
                    dve.wait_ge(gathered[s], (turn + 1) * LANES * 16)
                    ln_measure(ln, nc, dve, rows[:, s, :, :], n, s)

                def compare(n, s, turn):
                    dve.wait_ge(ends_in[s], (turn + 1) * 16)
                    merge_compare(mg, nc, dve, k, end[:, s, 0:LANES], n, s, turn)

                def compose(n, s, turn):
                    dve.wait_ge(message_done, n + 1)
                    if reused(n, 2):
                        dve.wait_ge(mg["merged"], n - 1)
                    nc.vector.tensor_tensor(message[:, s % 2, :, :], message_psum[:, :].rearrange("p (l d) -> p l d", d=D),
                                            k["row"]["l3_b_wvl"].unsqueeze(1).to_broadcast([P, LANES, D]), ALU.add).then_inc(message_ready, 1)

                def gate(n, s, turn):
                    dve.wait_ge(gate_ready, n + 1)
                    dve.wait_ge(value_ready, n + 1)
                    if reused(n, 1):
                        dve.wait_ge(message_done, n)
                    nc.vector.scalar_tensor_tensor(out=gated[:, :], in0=gate_psum[:, :], scalar=k["col"]["l3_b_wv2"], in1=value[:, :],
                                                   op0=ALU.add, op1=ALU.mult).then_inc(gated_ready, 1)

                walk(dve, n_blocks, [(3, gate), (4, compose), (1, measure), (4, compare),
                                     (1, lambda n, s, turn: ln_centre(ln, nc, dve, n, s)), (1, soften)])

            @block.tensor
            def _(pe):
                def merge(n, s, turn):
                    pe.wait_ge(message_ready, n + 1)
                    merge_merge(mg, nc, pe, lambda lane: message[:, s % 2, lane, :], n, s)

                def gate(n, s, turn):
                    pe.wait_ge(sp_["done"], n + 1)
                    if reused(n, 1):
                        pe.wait_ge(gated_ready, n)
                    nc.tensor.matmul(gate_psum[:, :], k["W"]["l3_wv2"], soft[:, s % 2, :], start=True, stop=True).then_inc(gate_ready, 1)
                    pe.wait_ge(copied, n + 1)
                    nc.tensor.matmul(value_psum[:, :], k["W"]["l3_v"], normed_T[:, :], start=True, stop=True).then_inc(value_done, 1)

                def express(n, s, turn):
                    pe.wait_ge(gated_ready, n + 1)
                    if reused(n, 1):
                        pe.wait_ge(message_ready, n)
                    for lane in range(LANES):
                        last = nc.tensor.matmul(message_psum[:, lane * D:(lane + 1) * D], gated[:, lane * P:(lane + 1) * P], k["W"]["l3_wvl"],
                                                start=True, stop=True)
                    last.then_inc(message_done, 1)

                def embed(n, s, turn):
                    pe.wait_ge(edge_in[s], (turn + 1) * 16)
                    if reused(n, 1):
                        pe.wait_ge(sp_["size_done"], n)
                    nc.tensor.matmul(pre_psum[:, :], k["wv1"][:, :], edge[:, s, :], start=True, stop=True).then_inc(pre_ready, 1)

                def turn_over(n, s, turn):
                    pe.wait_ge(ln["applied"], n + 1)
                    for r in range(LANES):
                        last = nc.tensor.transpose(turned[:, r * P:(r + 1) * P], normed[:, r, :], k["identity"][:, :])
                    last.then_inc(transposed, 1)

                walk(pe, n_blocks, [(5, merge), (3, express), (2, gate), (0, embed), (1, turn_over)])

            @block.scalar
            def _(act):
                act.preload_act_table_set(TABLES)
                act.wait_ge(ln["eps_set"], 1)
                act.wait_ge(sp_["half_set"], 1)

                def copy_value(n, s, turn):
                    act.wait_ge(value_done, n + 1)
                    if reused(n, 1):
                        act.wait_ge(gated_ready, n)
                    nc.scalar.activation(value[:, :], value_psum[:, :], ACT.Copy).then_inc(value_ready, 1)

                def tails(n, s, turn):
                    act.wait_ge(pre_ready, n + 1)
                    if reused(n, 1):
                        act.wait_ge(sp_["done"], n)
                    nc.scalar.activation(positive[:, :], pre_psum[:, :], ACT.Relu, bias=k["col"]["l3_b_wv1"])
                    softplus_tails(sp_, nc, act, pre_psum[:, :], k["col"]["l3_b_wv1"], n, s)

                def norm(n, s, turn):
                    if reused(n, 1):
                        act.wait_ge(transposed, n)
                    ln_apply(ln, nc, act, normed[:, :, :], rows[:, s, :, :], n, s)

                def copy(n, s, turn):
                    act.wait_ge(transposed, n + 1)
                    if reused(n, 1):
                        act.wait_ge(value_done, n)
                    nc.scalar.activation(normed_T[:, :], turned[:, :], ACT.Copy).then_inc(copied, 1)

                walk(act, n_blocks, [(5, lambda n, s, turn: merge_keep(mg, nc, act, n, s)),
                                     (1, lambda n, s, turn: ln_deviate(ln, nc, act, n, s)), (2, copy_value), (1, norm), (1, copy), (0, tails)])


def output_nodes(nc, k, x, accumulator, out, n_chunks):
    with phase(nc, "l3_nodes") as (sbuf, psum, sem):
        xs = sbuf("xs", [P, SLOTS, ROWS, D])
        acc = sbuf("acc", [P, SLOTS, ROWS, D])
        biased = sbuf("biased", [P, 2, ROWS, D])
        soft = sbuf("soft", [P, 2, ROWS, D])
        soft_T = sbuf("soft_T", [P, 2, ROWS, D])
        result = sbuf("result", [P, SLOTS, ROWS, D])
        turned = [psum(f"turned{s}", [P, 2, 512]) for s in range(2)]
        product = [psum(f"product{s}", [P, 2, 512]) for s in range(2)]
        loaded = [sem(f"loaded{s}") for s in range(SLOTS)]
        stored = [sem(f"stored{s}") for s in range(SLOTS)]
        biased_ready, transposed, copied, multiplied, finished = (
            sem(x) for x in ("biased_ready", "transposed", "copied", "multiplied", "finished"))
        sp_ = softplus_state(sbuf, psum, sem, ROWS * D)
        with nc.Block() as block:

            @block.sync
            def _(sp):
                def load(n, s, turn):
                    if reused(n, SLOTS):
                        sp.wait_ge(finished, n - SLOTS + 1)
                    sp.dma_start(flat(acc[:, s, :, :]), chunk_of(accumulator, n)).then_inc(loaded[s], 16)
                    sp.dma_start(flat(xs[:, s, :, :]), chunk_of(x, n)).then_inc(loaded[s], 16)

                def store(n, s, turn):
                    sp.wait_ge(finished, n + 1)
                    sp.dma_start(chunk_of(out, n), flat(result[:, s, :, :])).then_inc(stored[s], 16)

                walk(sp, n_chunks, [(0, load), (4, store)])
                for s in range(SLOTS):
                    sp.wait_ge(stored[s], 16 * uses(n_chunks, s))

            @block.vector
            def _(dve):
                softplus_set_half(sp_, nc)

                def soften(n, s, turn):
                    dve.wait_ge(sp_["tail_done"], n + 1)
                    if reused(n, 2):
                        dve.wait_ge(transposed, n - 1)
                    nc.vector.scalar_tensor_tensor(out=flat(soft[:, s % 2, :, :]), in0=flat(acc[:, s, :, :]), scalar=0.0,
                                                   in1=sp_["tail"][:, s % 2, :], op0=ALU.max, op1=ALU.add).then_inc(sp_["done"], 1)
                    if reused(n, 2):
                        dve.wait_ge(finished, n - 1)
                    nc.vector.tensor_tensor(biased[:, s % 2, :, :], xs[:, s, :, :],
                                            k["row"]["l3_b_o"].unsqueeze(1).to_broadcast([P, ROWS, D]), ALU.add).then_inc(biased_ready, 1)

                def add(n, s, turn):
                    dve.wait_ge(biased_ready, n + 1)
                    dve.wait_ge(multiplied, n + 1)
                    if reused(n, SLOTS):
                        dve.wait_ge(stored[s], turn * 16)
                    nc.vector.tensor_tensor(flat(result[:, s, :, :]), product[s % 2][:, :, :].rearrange("p b w -> p (b w)"),
                                            flat(biased[:, s % 2, :, :]), ALU.add).then_inc(finished, 1)

                walk(dve, n_chunks, [(3, add), (1, soften)])

            @block.tensor
            def _(pe):
                def turn_over(n, s, turn):
                    pe.wait_ge(sp_["done"], n + 1)
                    if reused(n, 2):
                        pe.wait_ge(copied, n - 1)
                    for r in range(ROWS):
                        last = nc.tensor.transpose(banks(turned[s % 2][:, :, :])[:, r, :], soft[:, s % 2, r, :], k["identity"][:, :])
                    last.then_inc(transposed, 1)

                def multiply(n, s, turn):
                    pe.wait_ge(copied, n + 1)
                    if reused(n, 2):
                        pe.wait_ge(finished, n - 1)
                    for r in range(ROWS):
                        last = nc.tensor.matmul(banks(product[s % 2][:, :, :])[:, r, :], soft_T[:, s % 2, r, :], k["W"]["l3_out"],
                                                start=True, stop=True)
                    last.then_inc(multiplied, 1)

                walk(pe, n_chunks, [(2, multiply), (1, turn_over)])

            @block.scalar
            def _(act):
                act.preload_act_table_set(TABLES)
                act.wait_ge(sp_["half_set"], 1)

                def tails(n, s, turn):
                    act.wait_ge(loaded[s], (turn + 1) * 32)
                    softplus_tails(sp_, nc, act, flat(acc[:, s, :, :]), None, n, s)

                def copy(n, s, turn):
                    act.wait_ge(transposed, n + 1)
                    if reused(n, 2):
                        act.wait_ge(multiplied, n - 1)
                    nc.scalar.activation(flat(soft_T[:, s % 2, :, :]), turned[s % 2][:, :, :].rearrange("p b w -> p (b w)"),
                                         ACT.Copy).then_inc(copied, 1)

                walk(act, n_chunks, [(2, copy), (0, tails)])


def build(nc, x, ends, dst_cols, dst_rows, src_rows, edge_T, edge_weight, matrices, wv1, columns, broadcast, biases,
          out, n_nodes):
    n_chunks = x.shape[0] // CHUNK
    n_blocks = ends.shape[0]
    last = n_nodes - (n_chunks - 1) * CHUNK
    assert last % ROWS == 0 and n_chunks * ROWS >= P
    n_pad = n_chunks * CHUNK

    def dram(name, shape):
        return nc.dram_tensor(name, shape, F32).ap()

    gcn_table1, gcn_table2, x1, x2, x3 = (dram(t, [n_pad, D]) for t in ("gcn_table1", "gcn_table2", "x1", "x2", "x3"))
    gcn_sum1, gcn_sum2, l3_sum = (dram(t, [n_pad + SPARE, D]) for t in ("gcn_sum1", "gcn_sum2", "l3_sum"))
    l1_sum, l2_sum = (dram(t, [n_pad + SPARE, SUMS]) for t in ("l1_sum", "l2_sum"))
    y_T, z_T = (dram(t, [n_chunks, P, CHUNK]) for t in ("y_T", "z_T"))
    k = {}
    with ExitStack() as ctx:
        load_constants(nc, ctx, k, matrices, wv1, columns, broadcast, biases, n_chunks * ROWS)
        degrees(nc, k, dst_cols, (gcn_sum1, gcn_sum2, l3_sum), n_blocks, n_chunks)
        norm_nodes(nc, k, x, gcn_table1, gcn_sum1, n_chunks)

        def gcn_layers(together):
            path = "together" if together else "apart"
            gcn_layer(nc, k, f"gcn1_{path}", ends, dst_rows, gcn_table1, gcn_sum1, None, k["W"]["gcn_w1"], k["row"]["gcn_b1"],
                      None, (gcn_table2, gcn_sum2), n_blocks, n_chunks, together)
            gcn_layer(nc, k, f"gcn2_{path}", ends, dst_rows, gcn_table2, gcn_sum2, l1_sum, k["W"]["gcn_w2"], k["row"]["gcn_b2"],
                      x, (x1,), n_blocks, n_chunks, together)

        if n_blocks == n_chunks:
            in_time = nc.values_load(k["in_time"][0:1, 0:1], min_val=0, max_val=1)
            with nc.If(in_time > 0):
                gcn_layers(True)
            with nc.Else():
                gcn_layers(False)
        else:
            gcn_layers(False)
        attention_over_edges(nc, k, "l1_edges", ends, dst_rows, edge_weight, x1, "l1_k", None, l1_sum, l2_sum, n_blocks)
        attention1_nodes(nc, k, x1, l1_sum, y_T, n_chunks, last // ROWS)
        feed_forward(nc, k, y_T, z_T, n_chunks, last // ROWS)
        add_layer1(nc, k, x1, z_T, x2, n_chunks)
        attention_over_edges(nc, k, "l2_edges", ends, dst_rows, None, x2, "l2_k", k["bias_parts"][:, 0:3 * D], l2_sum, None, n_blocks)
        attention2_nodes(nc, k, x2, l2_sum, x3, l3_sum, n_chunks)
        messages_over_edges(nc, k, ends, src_rows, edge_T, x3, l3_sum, n_blocks)
        output_nodes(nc, k, x3, l3_sum, out, n_chunks)


def kernel(**inputs):
    import concourse.bacc as bacc
    import numpy as np
    from concourse.bass_utils import run_bass_kernel_spmd

    a = {name: np.asarray(v) for name, v in inputs.items()}
    n_nodes, n_edges = a["x"].shape[0], a["src"].shape[0]
    n_chunks, n_blocks = -(-n_nodes // CHUNK), -(-n_edges // BLOCK)
    n_pad, e_pad = n_chunks * CHUNK, n_blocks * BLOCK

    def pad_rows(v, rows, fill=0):
        return np.concatenate([v, np.full((rows - v.shape[0],) + v.shape[1:], fill, v.dtype)])

    assert n_pad > n_nodes or e_pad == n_edges
    src, dst = (pad_rows(a[s].astype(np.int32), e_pad, n_nodes).reshape(n_blocks, P, LANES) for s in ("src", "dst"))

    def lanes_first(v):
        return v.transpose(0, 2, 1).reshape(n_blocks, BLOCK)

    edge = pad_rows(a["edge_attr_64"], e_pad).reshape(n_blocks, P, LANES, 64).transpose(3, 0, 2, 1).reshape(64, e_pad)
    mats = {"gcn_w1": a["L0_gnn_W1"], "gcn_w2": a["L0_gnn_W2"], "l1_k": a["L1_gnn_Wk"], "l1_v": a["L1_gnn_Wv"],
            "l1_q": a["L1_gnn_Wq"], "l1_o": a["L1_gnn_Wo"], "ffn_up0": a["L1_gnn_W1"][:, :D], "ffn_up1": a["L1_gnn_W1"][:, D:],
            "ffn_down0": a["L1_gnn_W2"][:D], "ffn_down1": a["L1_gnn_W2"][D:], "l2_k": a["L2_gnn_Wk"], "l2_v": a["L2_gnn_Wv"],
            "l2_q": a["L2_gnn_Wq"], "l3_c": a["L3_gnn_W_c"].T, "l3_out": a["L3_gnn_W_o"].T, "l3_v": a["L3_gnn_W_v"].T,
            "l3_wv2": a["L3_gnn_W_wv2"].T, "l3_wvl": a["L3_gnn_W_wvl"].T}
    cols = {"l1_bo": a["L1_gnn_bo"], "l1_g1": a["L1_gnn_g1"], "l1_b1": a["L1_gnn_b1"], "l1_bf1a": a["L1_gnn_bf1"][:D],
            "l1_bf1b": a["L1_gnn_bf1"][D:], "l1_bf2": a["L1_gnn_bf2"], "l1_g2": a["L1_gnn_g2"], "l1_b2": a["L1_gnn_b2"],
            "l3_b_wv1": a["L3_gnn_b_wv1"], "l3_b_wv2": a["L3_gnn_b_wv2"]}
    rows = {"gcn_b1": a["L0_gnn_b1"], "gcn_b2": a["L0_gnn_b2"], "l1_e": a["L1_gnn_We"][0], 
            "l3_b_o": a["L3_gnn_b_o"], "l3_b_wvl": a["L3_gnn_b_wvl"]}
    biases = {"l2_bk": a["L2_gnn_bk"], "l2_bv": a["L2_gnn_bv"], "l2_bq": a["L2_gnn_bq"], "l3_b_c": a["L3_gnn_b_c"]}
    arrays = {
        "in_x": pad_rows(a["x"], n_pad),
        "in_ends": np.concatenate([src, dst], axis=2),
        "in_dst_cols": dst.transpose(1, 0, 2).reshape(P, n_blocks * LANES),
        "in_dst_rows": lanes_first(dst),
        "in_src_rows": lanes_first(src),
        "in_edge_T": edge,
        "in_edge_weight": pad_rows(a["edge_weight1"], e_pad).reshape(n_blocks, P, LANES),
        "in_matrices": np.concatenate([mats[m] for m in MATRICES], axis=1),
        "in_wv1": a["L3_gnn_W_wv1"].T,
        "in_columns": np.stack([cols[m] for m in COLUMNS], axis=1),
        "in_broadcast": np.concatenate([rows[m] for m in BROADCAST])[None],
        "in_biases": np.concatenate([biases[m] for m in BIASES])[None],
    }
    arrays = {name: np.ascontiguousarray(v) for name, v in arrays.items()}
    nc = bacc.Bacc("TRN2", target_bir_lowering=False, num_devices=1)
    args = {name: nc.dram_tensor(name, v.shape, mybir.dt.from_np(v.dtype), kind="ExternalInput").ap() for name, v in arrays.items()}
    out = nc.dram_tensor("out_nodes", [n_pad, D], F32, kind="ExternalOutput").ap()
    build(nc, args["in_x"], args["in_ends"], args["in_dst_cols"], args["in_dst_rows"], args["in_src_rows"], args["in_edge_T"],
          args["in_edge_weight"], args["in_matrices"], args["in_wv1"], args["in_columns"], args["in_broadcast"],
          args["in_biases"], out, n_nodes)
    result = run_bass_kernel_spmd(nc, [arrays], core_ids=[0])
    return result.results[0]["out_nodes"][:n_nodes]
```

```python
from contextlib import ExitStack, contextmanager

import concourse.bass as bass
from concourse import mybir

F32 = mybir.dt.float32
F16 = mybir.dt.float16
BF16 = mybir.dt.bfloat16
I32 = mybir.dt.int32
ALU = mybir.AluOpType
ACT = mybir.ActivationFunctionType
AXIS_X = mybir.AxisListType.X

P = 128
D = 128
ROWS = 8
CHUNK = P * ROWS
LANES = 4
BLOCK = P * LANES
HEADS, HEAD_DIM = 8, 16
SUMS = D + HEADS
SPARE = BLOCK
SLOTS = 6
BEHIND = 1
NODE_SLOTS = 3
NODES = "nodes"
NODES_LAG = 9
LN_EPS = 1e-5
BN_EPS = 1e-5
Z_EPS = 1e-6
TABLES = "natural_log_exp_and_others"
WQ_SCALE = 1.0 / HEAD_DIM ** 0.5

MATRICES = ["gcn_w1", "gcn_w2", "l1_k", "l1_v", "l1_q", "l1_o", "ffn_up0", "ffn_up1", "ffn_down0", "ffn_down1",
            "l2_k", "l2_v", "l2_q", "l3_c", "l3_out", "l3_v", "l3_wv2", "l3_wvl"]
COLUMNS = ["l1_bo", "l1_g1", "l1_b1", "l1_bf1a", "l1_bf1b", "l1_bf2", "l1_g2", "l1_b2", "l3_b_wv1", "l3_b_wv2"]
BROADCAST = ["gcn_b1", "gcn_b2", "l1_e", "l3_b_o", "l3_b_wvl"]
BIASES = ["l2_bk", "l2_bv", "l2_bq", "l3_b_c"]
PARTS = 3


def reused(n, slots):
    return not isinstance(n, int) or n >= slots


def walk(eng, count, stages):
    deepest = max(lag for lag, _ in stages)
    first = deepest + SLOTS
    first += (count - first) % SLOTS

    def peeled(t):
        for lag, step in stages:
            if 0 <= t - lag < count:
                step(t - lag, (t - lag) % SLOTS, (t - lag) // SLOTS)

    for t in range(min(first, count + deepest)):
        peeled(t)
    if first < count:
        with eng.Fori(0, (count - first) // SLOTS) as i:
            for u in range(SLOTS):
                for lag, step in stages:
                    c = first + u - lag
                    step(i * SLOTS + c, c % SLOTS, i + c // SLOTS)
    for t in range(max(count, first), count + deepest):
        peeled(t)


def uses(count, s):
    return (count - s + SLOTS - 1) // SLOTS


@contextmanager
def phase(nc, name):
    sems = []
    with ExitStack() as ctx:

        def sbuf(what, shape, dtype=F32):
            return ctx.enter_context(nc.sbuf_tensor(f"{name}_{what}", shape, dtype))

        def psum(what, shape):
            return ctx.enter_context(nc.psum_tensor(f"{name}_{what}", shape, F32))

        def sem(what):
            sems.append(nc.alloc_semaphore(f"{name}_{what}"))
            return sems[-1]

        yield sbuf, psum, sem
        nc.clear_and_free_semaphores(sems)
        nc.all_engine_barrier()


def ln_state(sbuf, psum, sem, rows, tag="ln"):
    st = {}
    st["rows"] = rows
    st["stats"] = sbuf(f"{tag}_stats", [P, SLOTS, rows, 6])
    st["mean2"] = sbuf(f"{tag}_mean2", [P, SLOTS, rows])
    st["gap"] = sbuf(f"{tag}_gap", [P, SLOTS, rows])
    st["within"] = sbuf(f"{tag}_within", [P, SLOTS, rows])
    st["between"] = sbuf(f"{tag}_between", [P, SLOTS, rows])
    st["var"] = sbuf(f"{tag}_var", [P, SLOTS, rows])
    st["logvar"] = sbuf(f"{tag}_logvar", [P, SLOTS, rows])
    st["scale"] = sbuf(f"{tag}_scale", [P, SLOTS, rows])
    st["shift"] = sbuf(f"{tag}_shift", [P, SLOTS, rows])
    st["eps"] = sbuf(f"{tag}_eps", [P, 1])
    st["stats_done"], st["sums_done"], st["between_done"], st["var_done"], st["log_done"], st["scale_done"], \
        st["shift_done"], st["applied"], st["eps_set"] = (
            sem(f"{tag}_{x}") for x in ("stats_done", "sums_done", "between_done", "var_done", "log_done",
                                        "scale_done", "shift_done", "applied", "eps_set"))
    return st


def ln_set_eps(st, nc):
    nc.vector.memset(st["eps"][:, :], LN_EPS).then_inc(st["eps_set"], 1)


def ln_count(st, nc, x, s):
    for r in range(st["rows"]):
        last = nc.vector.bn_stats(st["stats"][:, s, r, :], x[:, r, :])
    last.then_inc(st["stats_done"], 1)


def ln_sums(st, nc, dve, n, s):
    dve.wait_ge(st["stats_done"], n + 1)
    stats = st["stats"][:, s, :, :]
    nc.vector.tensor_tensor(st["gap"][:, s, :], stats[:, :, 1], stats[:, :, 4], ALU.subtract)
    nc.vector.tensor_tensor(st["mean2"][:, s, :], stats[:, :, 1], stats[:, :, 4], ALU.add)
    nc.vector.tensor_tensor(st["within"][:, s, :], stats[:, :, 2], stats[:, :, 5], ALU.add).then_inc(st["sums_done"], 1)


def ln_between(st, nc, dve, n, s):
    dve.wait_ge(st["sums_done"], n + 1)
    nc.vector.scalar_tensor_tensor(out=st["between"][:, s, :], in0=st["gap"][:, s, :], scalar=0.25,
                                   in1=st["gap"][:, s, :], op0=ALU.mult, op1=ALU.mult).then_inc(st["between_done"], 1)


def ln_var(st, nc, dve, n, s):
    dve.wait_ge(st["between_done"], n + 1)
    if reused(n, SLOTS):
        dve.wait_ge(st["log_done"], n - SLOTS + 1)
    nc.vector.scalar_tensor_tensor(out=st["var"][:, s, :], in0=st["within"][:, s, :], scalar=1.0 / D,
                                   in1=st["between"][:, s, :], op0=ALU.mult, op1=ALU.add).then_inc(st["var_done"], 1)


def ln_measure(st, nc, dve, x, n, s):
    ln_count(st, nc, x, s)
    ln_sums(st, nc, dve, n, s)
    ln_between(st, nc, dve, n, s)
    ln_var(st, nc, dve, n, s)


def ln_deviate(st, nc, act, n, s):
    act.wait_ge(st["var_done"], n + 1)
    nc.scalar.activation(st["logvar"][:, s, :], st["var"][:, s, :], ACT.Ln, bias=st["eps"][:, 0:1]).then_inc(st["log_done"], 1)
    act.wait_ge(st["log_done"], n + 1)
    nc.scalar.activation(st["scale"][:, s, :], st["logvar"][:, s, :], ACT.Exp, scale=-0.5).then_inc(st["scale_done"], 1)


def ln_centre(st, nc, dve, n, s):
    dve.wait_ge(st["scale_done"], n + 1)
    if reused(n, SLOTS):
        dve.wait_ge(st["applied"], n - SLOTS + 1)
    nc.vector.scalar_tensor_tensor(out=st["shift"][:, s, :], in0=st["mean2"][:, s, :], scalar=-0.5,
                                   in1=st["scale"][:, s, :], op0=ALU.mult, op1=ALU.mult).then_inc(st["shift_done"], 1)


def ln_apply(st, nc, act, out, x, n, s):
    act.wait_ge(st["shift_done"], n + 1)
    for r in range(st["rows"]):
        last = nc.scalar.activation(out[:, r, :], x[:, r, :], ACT.Relu, bias=st["shift"][:, s, r:r + 1],
                                    scale=st["scale"][:, s, r:r + 1])
    last.then_inc(st["applied"], 1)


def load_constants(nc, ctx, k, matrices, wv1, columns, broadcast, biases, node_cols, n_blocks):
    def keep(name, shape, dtype=F32):
        return ctx.enter_context(nc.sbuf_tensor(f"const_{name}", shape, dtype))

    k["matrices"] = keep("matrices", [P, len(MATRICES), D])
    k["wv1"] = keep("wv1", [64, D])
    k["columns"] = keep("columns", [P, len(COLUMNS)])
    k["rows"] = keep("rows", [P, len(BROADCAST), D])
    k["bias_parts"] = keep("bias_parts", [PARTS, len(BIASES) * D], BF16)
    k["bias"] = {m: k["bias_parts"][:, i * D:(i + 1) * D] for i, m in enumerate(BIASES)}
    k["ones"] = keep("ones", [PARTS, P], BF16)
    k["identity"] = keep("identity", [P, P])
    k["earlier"] = keep("earlier", [P, BLOCK])
    k["spare_rows"] = keep("spare_rows", [P, LANES])
    k["dis"] = keep("dis", [P, node_cols])
    k["bn"] = keep("bn", [P, 4])
    k["in_time"] = keep("in_time", [1, 1], I32)
    k["dst_targets"] = keep("dst_targets", [P, n_blocks * LANES])
    k["W"] = {m: k["matrices"][:, i, :] for i, m in enumerate(MATRICES)}
    k["col"] = {m: k["columns"][:, i:i + 1] for i, m in enumerate(COLUMNS)}
    k["row"] = {m: k["rows"][:, i, :] for i, m in enumerate(BROADCAST)}
    spare_first = node_cols * P
    with phase(nc, "constants") as (sbuf, psum, sem):
        loaded = sem("loaded")
        filled = sem("filled")
        made = sem("made")
        scaled = sem("scaled")
        spread = sem("spread")
        bias = sbuf("bias", [PARTS, len(BIASES) * D])
        parts = [sbuf(f"part{i}", [PARTS, len(BIASES) * D], BF16) for i in range(PARTS)]
        rest = [bias] + [sbuf(f"rest{i}", [PARTS, len(BIASES) * D]) for i in range(1, PARTS)]
        with nc.Block() as block:

            @block.sync
            def _(sp):
                sp.dma_start(k["matrices"][:, :, :], matrices.rearrange("p (m d) -> p m d", d=D)).then_inc(loaded, 16)
                sp.dma_start(k["wv1"][:, :], wv1).then_inc(loaded, 16)
                sp.dma_start(k["columns"][:, :], columns).then_inc(loaded, 16)
                sp.dma_start(k["rows"][:, :, :].rearrange("p m d -> p (m d)"), broadcast.to_broadcast([P, len(BROADCAST) * D])).then_inc(loaded, 16)
                sp.dma_start(bias[:, :], biases.to_broadcast([PARTS, len(BIASES) * D])).then_inc(loaded, 16)
                sp.wait_ge(scaled, 2 * PARTS)
                for i in range(PARTS):
                    sp.dma_start(k["bias_parts"][i:i + 1, :], parts[i][i:i + 1, :]).then_inc(spread, 16)
                sp.wait_ge(spread, 16 * PARTS)

            @block.gpsimd
            def _(pool):
                nc.gpsimd.memset(k["identity"][:, :], 0.0)
                nc.gpsimd.memset(k["earlier"][:, :], 1.0).then_inc(filled, 1)
                pool.wait_ge(filled, 1)
                nc.gpsimd.affine_select(out=k["identity"][:, :], in_=k["identity"][:, :], compare_op=ALU.not_equal, fill=1.0,
                                        base=0, pattern=[[-1, P]], channel_multiplier=1)
                nc.gpsimd.affine_select(out=k["earlier"][:, BLOCK - P:], in_=k["earlier"][:, BLOCK - P:], compare_op=ALU.is_gt,
                                        fill=0.0, base=0, pattern=[[-1, P]], channel_multiplier=1)
                nc.gpsimd.iota(k["spare_rows"][:, :], pattern=[[P, LANES]], base=spare_first, channel_multiplier=1,
                               allow_small_or_imprecise_dtypes=True).then_inc(made, 1)

            @block.vector
            def _(dve):
                nc.vector.memset(k["ones"][:, :], 1.0)
                dve.wait_ge(loaded, 5 * 16)
                nc.vector.scalar_tensor_tensor(out=k["W"]["l1_q"], in0=k["W"]["l1_q"], scalar=WQ_SCALE, in1=k["row"]["l1_e"],
                                               op0=ALU.mult, op1=ALU.mult)
                nc.vector.tensor_scalar(k["W"]["l2_q"], k["W"]["l2_q"], WQ_SCALE, None, ALU.mult)
                nc.vector.tensor_scalar(bias[:, 2 * D:3 * D], bias[:, 2 * D:3 * D], WQ_SCALE, None, ALU.mult).then_inc(scaled, 1)
                for i in range(PARTS):
                    dve.wait_ge(scaled, 2 * i + 1)
                    nc.vector.tensor_copy(parts[i][:, :], rest[i][:, :]).then_inc(scaled, 1)
                    if i < PARTS - 1:
                        dve.wait_ge(scaled, 2 * i + 2)
                        nc.vector.tensor_tensor(rest[i + 1][:, :], rest[i][:, :], parts[i][:, :], ALU.subtract).then_inc(scaled, 1)


def degrees(nc, k, dst_cols, accumulators, n_blocks, n_chunks):
    cols = n_chunks * ROWS
    half = cols // 2
    with phase(nc, "degrees") as (sbuf, psum, sem):
        keys = sbuf("keys", [P, n_blocks * LANES], I32)
        part_i = sbuf("part_i", [P, n_blocks * LANES], I32)
        high_i = sbuf("high_i", [P, n_blocks * LANES], I32)
        low_i = sbuf("low_i", [P, n_blocks * LANES], I32)
        part = sbuf("part", [P, n_blocks * LANES])
        col = sbuf("col", [P, n_blocks * LANES])
        numbers = sbuf("numbers", [P, cols], F16)
        hot_part = sbuf("hot_part", [P, SLOTS, LANES, P], F16)
        hot_col = sbuf("hot_col", [P, SLOTS, LANES, cols], F16)
        zeros = sbuf("zeros", [P, LANES * D])
        log_deg = sbuf("log_deg", [P, cols])
        chunk_i = sbuf("chunk_i", [P, n_blocks * LANES], I32)
        block_i = sbuf("block_i", [P, n_blocks * LANES], I32)
        ahead = sbuf("ahead", [P, n_blocks * LANES])
        least = sbuf("least", [P, 1])
        least_of_all = sbuf("least_of_all", [1, 1])
        least_T = psum("least_T", [P, 512])
        counts = psum("counts", [P, 2, 512])
        keys_in, split, numbered, hot, counted, zeros_set, zeroed, logged, ended, least_ready, least_turned = (
            sem(x) for x in ("keys_in", "split", "numbered", "hot", "counted", "zeros_set", "zeroed", "logged", "ended",
                             "least_ready", "least_turned"))
        with nc.Block() as block:

            @block.sync
            def _(sp):
                sp.dma_start(keys[:, :], dst_cols).then_inc(keys_in, 16)
                sp.wait_ge(zeros_set, 1)
                for accumulator in accumulators:
                    spare = accumulator[n_chunks * CHUNK:, :].rearrange("(p r) d -> p (r d)", p=P)
                    sp.dma_start(spare, zeros[:, :]).then_inc(zeroed, 16)
                sp.wait_ge(zeroed, 16 * len(accumulators))

            @block.gpsimd
            def _(pool):
                nc.gpsimd.iota(block_i[:, :], pattern=[[1, n_blocks], [0, LANES]], base=0, channel_multiplier=0)
                nc.gpsimd.iota(numbers[:, :], pattern=[[1, cols]], base=0, channel_multiplier=0,
                               allow_small_or_imprecise_dtypes=True).then_inc(numbered, 1)

            @block.vector
            def _(dve):
                nc.vector.memset(zeros[:, :], 0.0).then_inc(zeros_set, 1)
                dve.wait_ge(keys_in, 16)
                nc.vector.tensor_scalar(part_i[:, :], keys[:, :], 3, P - 1, ALU.logical_shift_right, ALU.bitwise_and)
                nc.vector.tensor_scalar(high_i[:, :], keys[:, :], 10, 3, ALU.logical_shift_right, ALU.logical_shift_left)
                nc.vector.tensor_scalar(chunk_i[:, :], keys[:, :], 10, None, ALU.logical_shift_right)
                nc.vector.tensor_scalar(low_i[:, :], keys[:, :], ROWS - 1, None, ALU.bitwise_and).then_inc(split, 1)
                dve.wait_ge(split, 1)
                nc.vector.tensor_copy(part[:, :], part_i[:, :])
                nc.vector.tensor_tensor(col[:, :], high_i[:, :], low_i[:, :], ALU.add).then_inc(split, 1)
                dve.wait_ge(numbered, 1)
                nc.vector.tensor_tensor(ahead[:, :], chunk_i[:, :], block_i[:, :], ALU.subtract).then_inc(split, 1)
                dve.wait_ge(split, 3)
                nc.vector.tensor_reduce(least[:, :], ahead[:, :], AXIS_X, ALU.min).then_inc(least_ready, 1)

                def one_hot(n, s, turn):
                    if reused(n, SLOTS):
                        dve.wait_ge(counted, n - SLOTS + 1)
                    for lane in range(LANES):
                        at = bass.ds(n * LANES + lane, 1)
                        nc.vector.tensor_scalar(hot_part[:, s, lane, :], numbers[:, 0:P], part[:, at], None, ALU.is_equal)
                        last = nc.vector.tensor_scalar(hot_col[:, s, lane, :], numbers[:, :], col[:, at], None, ALU.is_equal)
                    last.then_inc(hot, 1)

                walk(dve, n_blocks, [(0, one_hot)])
                dve.wait_ge(least_turned, 1)
                nc.vector.tensor_reduce(least_of_all[:, :], least_T[0:1, 0:P], AXIS_X, ALU.min).then_inc(least_ready, 1)
                dve.wait_ge(least_ready, 2)
                nc.vector.tensor_scalar(k["in_time"][:, :], least_of_all[:, :], float(-BEHIND), None, ALU.is_ge).then_inc(ended, 1)

            @block.tensor
            def _(pe):
                def count(n, s, turn):
                    pe.wait_ge(hot, n + 1)
                    for lane in range(LANES):
                        for h in range(2):
                            start = isinstance(n, int) and n == 0 and lane == 0
                            stop = isinstance(n, int) and n == n_blocks - 1 and lane == LANES - 1
                            last = nc.tensor.matmul(counts[:, h, 0:half], hot_part[:, s, lane, :],
                                                    hot_col[:, s, lane, h * half:(h + 1) * half], start=start, stop=stop)
                    last.then_inc(counted, 1)

                pe.wait_ge(least_ready, 1)
                nc.tensor.transpose(least_T[0:1, 0:P], least[:, :], k["identity"][:, :]).then_inc(least_turned, 1)
                walk(pe, n_blocks - 1, [(0, count)])
                count(n_blocks - 1, (n_blocks - 1) % SLOTS, 0)

            @block.scalar
            def _(act):
                act.preload_act_table_set(TABLES)
                act.wait_ge(counted, n_blocks)
                nc.scalar.activation(log_deg[:, :].rearrange("p (h c) -> p h c", h=2), counts[:, :, 0:half], ACT.Ln, bias=1.0).then_inc(logged, 1)
                act.wait_ge(logged, 1)
                nc.scalar.activation(k["dis"][:, :], log_deg[:, :], ACT.Exp, scale=-0.5).then_inc(ended, 1)


def chunk_of(table, n, width=D):
    t = table[0:table.shape[0] // CHUNK * CHUNK, :].rearrange("(c p r) d -> c p (r d)", p=P, r=ROWS)
    return t[bass.ds(n, 1), :, :].rearrange("c p w -> (c p) w")


def norm_nodes(nc, k, x, table, accumulator, n_chunks):
    with phase(nc, "norm_nodes") as (sbuf, psum, sem):
        xs = sbuf("xs", [P, SLOTS, ROWS, D])
        out = sbuf("out", [P, SLOTS, ROWS, D])
        ln = ln_state(sbuf, psum, sem, ROWS)
        scale = sbuf("scale", [P, SLOTS, ROWS])
        loaded = [sem(f"loaded{s}") for s in range(SLOTS)]
        stored = [sem(f"stored{s}") for s in range(SLOTS)]
        scaled = sem("scaled")
        with nc.Block() as block:

            @block.sync
            def _(sp):
                def load(n, s, turn):
                    if reused(n, SLOTS):
                        sp.wait_ge(ln["applied"], n - SLOTS + 1)
                    sp.dma_start(xs[:, s, :, :].rearrange("p r d -> p (r d)"), chunk_of(x, n)).then_inc(loaded[s], 16)

                def store(n, s, turn):
                    sp.wait_ge(ln["applied"], n + 1)
                    sp.dma_start(chunk_of(table, n), flat(out[:, s, :, :])).then_inc(stored[s], 16)
                    sp.dma_start(chunk_of(accumulator, n), flat(out[:, s, :, :])).then_inc(stored[s], 16)

                walk(sp, n_chunks, [(0, load), (3, store)])
                for s in range(SLOTS):
                    sp.wait_ge(stored[s], 32 * uses(n_chunks, s))

            @block.vector
            def _(dve):
                ln_set_eps(ln, nc)

                def measure(n, s, turn):
                    dve.wait_ge(loaded[s], turn * 16 + 16)
                    ln_measure(ln, nc, dve, xs[:, s, :, :], n, s)

                def centre(n, s, turn):
                    dve.wait_ge(ln["scale_done"], n + 1)
                    if reused(n, SLOTS):
                        dve.wait_ge(ln["applied"], n - SLOTS + 1)
                    nc.vector.tensor_tensor(scale[:, s, :], ln["scale"][:, s, :], k["dis"][:, bass.ds(n * ROWS, ROWS)], ALU.mult).then_inc(scaled, 1)
                    dve.wait_ge(scaled, n + 1)
                    nc.vector.scalar_tensor_tensor(out=ln["shift"][:, s, :], in0=ln["mean2"][:, s, :], scalar=-0.5,
                                                   in1=scale[:, s, :], op0=ALU.mult, op1=ALU.mult).then_inc(ln["shift_done"], 1)

                walk(dve, n_chunks, [(1, centre), (0, measure)])

            @block.scalar
            def _(act):
                act.preload_act_table_set(TABLES)
                act.wait_ge(ln["eps_set"], 1)

                def deviate(n, s, turn):
                    if reused(n, SLOTS):
                        act.wait_ge(scaled, n - SLOTS + 1)
                    ln_deviate(ln, nc, act, n, s)

                def apply(n, s, turn):
                    if reused(n, SLOTS):
                        act.wait_ge(stored[s], turn * 32)
                    act.wait_ge(ln["shift_done"], n + 1)
                    for r in range(ROWS):
                        last = nc.scalar.activation(out[:, s, r, :], xs[:, s, r, :], ACT.Relu, bias=ln["shift"][:, s, r:r + 1],
                                                    scale=scale[:, s, r:r + 1])
                    last.then_inc(ln["applied"], 1)

                walk(act, n_chunks, [(1, apply), (0, deviate)])


def merge_state(sbuf, psum, sem, width):
    st = {}
    st["width"] = width
    st["key_rows"] = sbuf("key_rows", [P, SLOTS, BLOCK], I32)
    st["key"] = sbuf("key", [P, SLOTS, LANES])
    st["same"] = sbuf("same", [P, 2, LANES, BLOCK])
    st["masked"] = sbuf("masked", [P, LANES, BLOCK], F16)
    st["before"] = sbuf("before", [P, SLOTS, LANES])
    st["away"] = sbuf("away", [P, SLOTS, LANES])
    st["step"] = sbuf("step", [P, SLOTS, LANES])
    st["target"] = sbuf("target", [P, SLOTS, LANES], I32)
    st["sums"] = sbuf("sums", [P, 2, LANES, width])
    st["psum"] = psum("merge_psum", [P, 2, 512])
    st["keys_in"] = [sem(f"keys_in{s}") for s in range(SLOTS)]
    st["key_ready"], st["same_ready"], st["before_ready"], st["step_ready"], st["target_ready"], st["merged"], \
        st["sums_ready"], st["scattered"] = (
            sem(x) for x in ("key_ready", "same_ready", "before_ready", "step_ready", "target_ready", "merged",
                                "sums_ready", "scattered"))
    return st


def merge_load(st, sp, key_rows, n, s):
    sp.dma_start(st["key_rows"][:, s, :], key_rows[bass.ds(n, 1), :].to_broadcast([P, BLOCK])).then_inc(st["keys_in"][s], 16)


def merge_compare(st, nc, dve, key_cols, n, s, turn):
    dve.wait_ge(st["keys_in"][s], turn * 16 + 16)
    nc.vector.tensor_copy(st["key"][:, s, :], key_cols).then_inc(st["key_ready"], 1)
    dve.wait_ge(st["key_ready"], n + 1)
    if reused(n, 2):
        dve.wait_ge(st["merged"], n - 1)
    for lane in range(LANES):
        upto = (lane + 1) * P
        last = nc.vector.tensor_scalar(st["same"][:, s % 2, lane, 0:upto], st["key_rows"][:, s, 0:upto],
                                       st["key"][:, s, lane:lane + 1], None, ALU.is_equal)
    last.then_inc(st["same_ready"], 1)


def merge_place(st, nc, dve, k, n, s, keep=None):
    dve.wait_ge(st["same_ready"], n + 1)
    for lane in range(LANES):
        upto = (lane + 1) * P
        last = nc.vector.tensor_tensor_reduce(out=st["masked"][:, lane, 0:upto], in0=st["same"][:, s % 2, lane, 0:upto],
                                              in1=k["earlier"][:, BLOCK - upto:], scale=1.0, scalar=0.0, op0=ALU.mult,
                                              op1=ALU.add, accum_out=st["before"][:, s, lane:lane + 1])
    nc.vector.tensor_tensor(st["away"][:, s, :], k["spare_rows"][:, :], st["key"][:, s, :], ALU.subtract).then_inc(st["before_ready"], 1)
    dve.wait_ge(st["before_ready"], n + 1)
    nc.vector.scalar_tensor_tensor(out=st["step"][:, s, :], in0=st["before"][:, s, :], scalar=1.0,
                                   in1=st["away"][:, s, :], op0=ALU.min, op1=ALU.mult).then_inc(st["step_ready"], 1)
    dve.wait_ge(st["step_ready"], n + 1)
    if reused(n, SLOTS):
        dve.wait_ge(st["scattered"], (n - SLOTS + 1) * LANES * 16)
    if keep is not None:
        nc.vector.tensor_tensor(keep[:, bass.ds(n * LANES, LANES)], st["step"][:, s, :], st["key"][:, s, :], ALU.add)
    nc.vector.tensor_tensor(st["target"][:, s, :], st["step"][:, s, :], st["key"][:, s, :], ALU.add).then_inc(st["target_ready"], 1)


def merge_recall(st, nc, dve, kept, n, s):
    if reused(n, SLOTS):
        dve.wait_ge(st["scattered"], (n - SLOTS + 1) * LANES * 16)
    nc.vector.tensor_copy(st["target"][:, s, :], kept[:, bass.ds(n * LANES, LANES)]).then_inc(st["target_ready"], 1)


def merge_merge(st, nc, pe, message, n, s):
    pe.wait_ge(st["same_ready"], n + 1)
    if reused(n, 1):
        pe.wait_ge(st["sums_ready"], n)
    for to in range(LANES):
        at = (to % 2) * st["width"]
        for lane in range(to, LANES):
            last = nc.tensor.matmul(st["psum"][:, to // 2, at:at + st["width"]],
                                    st["same"][:, s % 2, lane, to * P:(to + 1) * P], message(lane),
                                    start=lane == to, stop=lane == LANES - 1)
    last.then_inc(st["merged"], 1)


def merge_keep(st, nc, act, n, s):
    act.wait_ge(st["merged"], n + 1)
    if reused(n, 2):
        act.wait_ge(st["scattered"], (n - 1) * LANES * 16)
    nc.scalar.activation(st["sums"][:, s % 2, :, :].rearrange("p (b l) w -> p b (l w)", b=2),
                         st["psum"][:, :, 0:2 * st["width"]], ACT.Copy).then_inc(st["sums_ready"], 1)


def merge_scatter(st, nc, pool, accumulator, n, s):
    pool.wait_ge(st["sums_ready"], n + 1)
    pool.wait_ge(st["target_ready"], n + 1)
    if reused(n, 1):
        pool.wait_ge(st["scattered"], n * LANES * 16)
    pool.sem_inc(st["pool_passed"])
    for lane in range(LANES):
        pool.indirect_dma_start(accumulator, bass.IndirectOffsetOnAxis(ap=st["target"][:, s, lane:lane + 1], axis=0),
                                st["sums"][:, s % 2, lane, :], None, compute_op=ALU.add).then_inc(st["scattered"], 16)


def gather(pool, rows, table, numbers, lanes, done):
    for lane in range(lanes):
        pool.indirect_dma_start(rows[:, lane, :], None, table, bass.IndirectOffsetOnAxis(ap=numbers[:, lane:lane + 1], axis=0)).then_inc(done, 16)


def zero_state(sbuf, psum, sem, accumulator, n_blocks):
    st = {}
    st["acc"] = accumulator
    st["n_blocks"] = n_blocks
    if accumulator is not None:
        st["rows"], st["width"] = accumulator.shape
        st["part"] = st["rows"] // BLOCK
        st["per"] = -(-st["part"] // n_blocks)
        st["zeros"] = sbuf("zeros", [P, LANES * st["width"]])
        st["zeros_set"] = sem("zeros_set")
        st["zeroed"] = sem("zeroed")
    return st


def zero_fill(st, nc):
    if st["acc"] is not None:
        nc.vector.memset(st["zeros"][:, :], 0.0).then_inc(st["zeros_set"], 1)


def zero_begin(st, sp):
    if st["acc"] is not None:
        sp.wait_ge(st["zeros_set"], 1)


def zero_step(st, sp, first, count):
    if st["acc"] is not None:
        parts = st["acc"].rearrange("(c p r) d -> c p (r d)", p=P, r=LANES)
        for c in range(count):
            sp.dma_start(parts[bass.ds(first + c, 1), :, :].rearrange("c p w -> (c p) w"), st["zeros"][:, :]).then_inc(st["zeroed"], 16)


def zero_end(st, sp):
    if st["acc"] is not None:
        done = st["part"] // st["n_blocks"] * st["n_blocks"]
        zero_step(st, sp, done, st["part"] - done)
        sp.wait_ge(st["zeroed"], 16 * st["part"])


def flat(tile):
    return tile.rearrange("p r d -> p (r d)")


def banks(psum):
    return psum.rearrange("p b (r d) -> p (b r) d", d=D)


def gcn_layer(nc, k, name, ends, key_rows, table, accumulator, zero_next, weight, bias, x, outs, n_blocks, n_chunks, together, places_known):
    with phase(nc, name) as (sbuf, psum, sem):
        end = sbuf("end", [P, SLOTS, 2 * LANES], I32)
        rows = sbuf("rows", [P, SLOTS, LANES, D])
        ends_in = [sem(f"ends_in{s}") for s in range(SLOTS)]
        gathered = [sem(f"gathered{s}") for s in range(SLOTS)]
        mg = merge_state(sbuf, psum, sem, D)
        mg["pool_passed"] = sem("pool_passed")
        zero = zero_state(sbuf, psum, sem, zero_next, n_blocks)
        acc = sbuf("acc", [P, SLOTS, ROWS, D])
        xs = sbuf("xs", [P, SLOTS, ROWS, D]) if x is not None else None
        acc_T = sbuf("acc_T", [P, ROWS, D])
        y = sbuf("y", [P, ROWS, D])
        result = sbuf("result", [P, SLOTS, ROWS, D])
        turned = [psum(f"turned{s}", [P, 2, 512]) for s in range(2)]
        product = psum("product", [P, 2, 512])
        loaded = [sem(f"loaded{s}") for s in range(SLOTS)]
        stored = [sem(f"stored{s}") for s in range(SLOTS)]
        transposed, copied, multiplied, biased, finished = (
            sem(s) for s in ("transposed", "copied", "multiplied", "biased", "finished"))
        loads = 1 + (x is not None)
        stores = len(outs)
        behind = SLOTS + BEHIND + 1

        def pass_over(eng, edge_stages, node_stages):
            if together:
                walk(eng, n_blocks, [(behind + lag, step) for lag, step in node_stages] + edge_stages)
            else:
                walk(eng, n_blocks, edge_stages)
                walk(eng, n_chunks, node_stages)

        with nc.Block() as block:

            @block.sync
            def _(sp):
                zero_begin(zero, sp)

                def load_edges(n, s, turn):
                    if reused(n, SLOTS):
                        sp.wait_ge(mg["scattered"], (n - SLOTS + 1) * LANES * 16)
                    sp.dma_start(end[:, s, :], ends[bass.ds(n, 1), :, :].rearrange("b p w -> (b p) w")).then_inc(ends_in[s], 16)
                    merge_load(mg, sp, key_rows, n, s)

                def clear(n, s, turn):
                    if zero["acc"] is not None:
                        each = zero["part"] // n_blocks
                        zero_step(zero, sp, n * each, each)

                def load(n, s, turn):
                    if together:
                        last = n + BEHIND if not isinstance(n, int) else min(n + BEHIND, n_blocks - 1)
                        sp.wait_ge(mg["scattered"], (last + 1) * LANES * 16)
                    elif isinstance(n, int) and n == 0:
                        sp.wait_ge(mg["scattered"], n_blocks * LANES * 16)
                    sp.dma_start(flat(acc[:, s, :, :]), chunk_of(accumulator, n)).then_inc(loaded[s], 16)
                    if x is not None:
                        sp.dma_start(flat(xs[:, s, :, :]), chunk_of(x, n)).then_inc(loaded[s], 16)

                def store(n, s, turn):
                    sp.wait_ge(finished, n + 1)
                    for out in outs:
                        sp.dma_start(chunk_of(out, n), flat(result[:, s, :, :])).then_inc(stored[s], 16)

                pass_over(sp, [(0, load_edges), (0, clear)], [(0, load), (4, store)])
                zero_end(zero, sp)
                for s in range(SLOTS):
                    sp.wait_ge(stored[s], 16 * stores * uses(n_chunks, s))

            @block.gpsimd
            def _(pool):
                def fetch(n, s, turn):
                    if reused(n, SLOTS):
                        pool.wait_ge(mg["merged"], n - SLOTS + 1)
                    pool.wait_ge(ends_in[s], turn * 16 + 16)
                    pool.sem_inc(mg["pool_passed"])
                    gather(pool, rows[:, s, :, :], table, end[:, s, 0:LANES], LANES, gathered[s])

                def add(n, s, turn):
                    merge_scatter(mg, nc, pool, accumulator, n, s)

                walk(pool, n_blocks, [(0, fetch), (1, add)])
                pool.wait_ge(mg["scattered"], n_blocks * LANES * 16)

            @block.vector
            def _(dve):
                zero_fill(zero, nc)

                def compare(n, s, turn):
                    dve.wait_ge(ends_in[s], turn * 16 + 16)
                    merge_compare(mg, nc, dve, end[:, s, LANES:], n, s, turn)
                    if places_known:
                        merge_recall(mg, nc, dve, k["dst_targets"], n, s)
                    else:
                        merge_place(mg, nc, dve, k, n, s, k["dst_targets"])

                def add_bias(n, s, turn):
                    dve.wait_ge(multiplied, n + 1)
                    if reused(n, 1):
                        dve.wait_ge(finished, n)
                    for r in range(ROWS):
                        last = nc.vector.scalar_tensor_tensor(out=y[:, r, :], in0=banks(product[:, :, :])[:, r, :],
                                                              scalar=k["dis"][:, bass.ds(n * ROWS + r, 1)], in1=bias,
                                                              op0=ALU.mult, op1=ALU.add)
                    last.then_inc(biased, 1)
                    if x is not None:
                        dve.wait_ge(biased, n + 1)
                        if reused(n, SLOTS):
                            dve.wait_ge(stored[s], turn * 16 * stores)
                        nc.vector.scalar_tensor_tensor(out=flat(result[:, s, :, :]), in0=flat(y[:, :, :]), scalar=0.0,
                                                       in1=flat(xs[:, s, :, :]), op0=ALU.max, op1=ALU.add).then_inc(finished, 1)

                pass_over(dve, [(0, compare)], [(2, add_bias)])

            @block.tensor
            def _(pe):
                def merge(n, s, turn):
                    pe.wait_ge(gathered[s], (turn + 1) * LANES * 16)
                    merge_merge(mg, nc, pe, lambda lane: rows[:, s, lane, :], n, s)

                def turn_over(n, s, turn):
                    pe.wait_ge(loaded[s], (turn + 1) * 16 * loads)
                    if reused(n, 2):
                        pe.wait_ge(copied, n - 1)
                    for r in range(ROWS):
                        last = nc.tensor.transpose(banks(turned[s % 2][:, :, :])[:, r, :], acc[:, s, r, :], k["identity"][:, :])
                    last.then_inc(transposed, 1)

                def multiply(n, s, turn):
                    pe.wait_ge(copied, n + 1)
                    if reused(n, 1):
                        pe.wait_ge(biased, n)
                    for r in range(ROWS):
                        last = nc.tensor.matmul(banks(product[:, :, :])[:, r, :], acc_T[:, r, :], weight, start=True, stop=True)
                    last.then_inc(multiplied, 1)

                pass_over(pe, [(0, merge)], [(1, multiply), (0, turn_over)])

            @block.scalar
            def _(act):
                def copy(n, s, turn):
                    act.wait_ge(transposed, n + 1)
                    if reused(n, 1):
                        act.wait_ge(multiplied, n)
                    nc.scalar.activation(flat(acc_T[:, :, :]), turned[s % 2][:, :, :].rearrange("p b w -> p (b w)"),
                                         ACT.Copy).then_inc(copied, 1)

                def rectify(n, s, turn):
                    act.wait_ge(biased, n + 1)
                    if reused(n, SLOTS):
                        act.wait_ge(stored[s], turn * 16 * stores)
                    for r in range(ROWS):
                        last = nc.scalar.activation(result[:, s, r, :], y[:, r, :], ACT.Relu,
                                                    scale=k["dis"][:, bass.ds(n * ROWS + r, 1)])
                    last.then_inc(finished, 1)

                pass_over(act, [(0, lambda n, s, turn: merge_keep(mg, nc, act, n, s))],
                          ([(2, rectify)] if x is None else []) + [(0, copy)])


def attention_over_edges(nc, k, name, ends, key_rows, edge_weight, nodes, weights, bias, accumulator, zero_next, n_blocks):
    with phase(nc, name) as (sbuf, psum, sem):
        end = sbuf("end", [P, SLOTS, 2 * LANES], I32)
        rows = sbuf("rows", [P, SLOTS, 2 * LANES, D])
        normed = sbuf("normed", [P, 2 * LANES, D])
        normed_T = sbuf("normed_T", [P, 2 * LANES, D])
        query = sbuf("query", [P, LANES, D])
        terms = sbuf("terms", [P, LANES, D])
        dots = sbuf("dots", [P, LANES, HEADS])
        weighted = sbuf("weighted", [P, LANES, HEADS])
        clipped = sbuf("clipped", [P, LANES, HEADS])
        message = sbuf("message", [P, 2, LANES, SUMS])
        factor = sbuf("factor", [P, SLOTS, LANES])
        turned = psum("turned", [P, 2, 512])
        kvq = psum("kvq", [P, LANES, 512])
        ends_in = [sem(f"ends_in{s}") for s in range(SLOTS)]
        gathered = [sem(f"gathered{s}") for s in range(SLOTS)]
        transposed, copied, projected, query_ready, terms_ready, dots_ready, weighted_ready, clipped_ready, score_ready, \
            message_ready = (sem(x) for x in (
                "transposed", "copied", "projected", "query_ready", "terms_ready", "dots_ready", "weighted_ready",
                "clipped_ready", "score_ready", "message_ready"))
        ln = ln_state(sbuf, psum, sem, 2 * LANES)
        mg = merge_state(sbuf, psum, sem, SUMS)
        mg["pool_passed"] = sem("pool_passed")
        zero = zero_state(sbuf, psum, sem, zero_next, n_blocks)
        end_loads = 1 + (edge_weight is not None)
        w_at = MATRICES.index(weights)
        w_kv = k["matrices"][:, w_at:w_at + 2, :].rearrange("p m d -> p (m d)")
        w_q = k["matrices"][:, w_at + 2, :]
        with nc.Block() as block:

            @block.sync
            def _(sp):
                zero_begin(zero, sp)

                def load(n, s, turn):
                    if reused(n, SLOTS):
                        sp.wait_ge(mg["target_ready"], n - SLOTS + 1)
                    sp.dma_start(end[:, s, :], ends[bass.ds(n, 1), :, :].rearrange("b p w -> (b p) w")).then_inc(ends_in[s], 16)
                    if edge_weight is not None:
                        sp.dma_start(factor[:, s, :], edge_weight[bass.ds(n, 1), :, :].rearrange("b p w -> (b p) w")).then_inc(ends_in[s], 16)
                    merge_load(mg, sp, key_rows, n, s)

                def clear(n, s, turn):
                    if zero["acc"] is not None:
                        each = zero["part"] // n_blocks
                        zero_step(zero, sp, n * each, each)

                walk(sp, n_blocks, [(0, load), (0, clear)])
                zero_end(zero, sp)

            @block.gpsimd
            def _(pool):
                def fetch(n, s, turn):
                    if reused(n, SLOTS):
                        pool.wait_ge(ln["applied"], n - SLOTS + 1)
                    pool.wait_ge(ends_in[s], (turn + 1) * 16 * end_loads)
                    pool.sem_inc(mg["pool_passed"])
                    gather(pool, rows[:, s, :, :], nodes, end[:, s, :], 2 * LANES, gathered[s])

                walk(pool, n_blocks, [(0, fetch), (5, lambda n, s, turn: merge_scatter(mg, nc, pool, accumulator, n, s))])
                pool.wait_ge(mg["scattered"], n_blocks * LANES * 16)

            @block.vector
            def _(dve):
                zero_fill(zero, nc)
                ln_set_eps(ln, nc)

                def measure(n, s, turn):
                    dve.wait_ge(gathered[s], (turn + 1) * 2 * LANES * 16)
                    ln_measure(ln, nc, dve, rows[:, s, :, :], n, s)

                def compare(n, s, turn):
                    dve.wait_ge(ends_in[s], (turn + 1) * 16 * end_loads)
                    merge_compare(mg, nc, dve, end[:, s, LANES:], n, s, turn)
                    merge_recall(mg, nc, dve, k["dst_targets"], n, s)

                def attend(n, s, turn):
                    dve.wait_ge(query_ready, n + 1)
                    nc.vector.tensor_tensor(terms[:, :, :], kvq[:, :, 0:D], query[:, :, :], ALU.mult).then_inc(terms_ready, 1)
                    dve.wait_ge(terms_ready, n + 1)
                    nc.vector.tensor_reduce(dots[:, :, :].rearrange("p l h -> p (l h)"),
                                            terms[:, :, :].rearrange("p l (h d) -> p (l h) d", d=HEAD_DIM),
                                            AXIS_X, ALU.add).then_inc(dots_ready, 1)
                    dve.wait_ge(dots_ready, n + 1)
                    source = dots
                    if edge_weight is not None:
                        nc.vector.tensor_tensor(weighted[:, :, :], dots[:, :, :],
                                                factor[:, s, :].unsqueeze(2).to_broadcast([P, LANES, HEADS]),
                                                ALU.mult).then_inc(weighted_ready, 1)
                        dve.wait_ge(weighted_ready, n + 1)
                        source = weighted
                    if reused(n, 1):
                        dve.wait_ge(score_ready, n)
                    nc.vector.tensor_scalar(clipped[:, :, :], source[:, :, :], 5.0, -5.0, ALU.min, ALU.max).then_inc(clipped_ready, 1)

                def weigh(n, s, turn):
                    dve.wait_ge(score_ready, n + 1)
                    m = message[:, s % 2, :, :]
                    for lane in range(LANES):
                        last = nc.vector.tensor_tensor(m[:, lane, 0:D].rearrange("p (h d) -> p h d", d=HEAD_DIM),
                                                       kvq[:, lane, D:2 * D].rearrange("p (h d) -> p h d", d=HEAD_DIM),
                                                       m[:, lane, D:SUMS].unsqueeze(2).to_broadcast([P, HEADS, HEAD_DIM]), ALU.mult)
                    last.then_inc(message_ready, 1)

                walk(dve, n_blocks, [(3, attend), (1, lambda n, s, turn: ln_centre(ln, nc, dve, n, s)), (3, weigh), (3, compare), (0, measure)])

            @block.tensor
            def _(pe):
                def merge(n, s, turn):
                    pe.wait_ge(message_ready, n + 1)
                    merge_merge(mg, nc, pe, lambda lane: message[:, s % 2, lane, :], n, s)

                def project(n, s, turn):
                    pe.wait_ge(copied, n + 1)
                    if reused(n, 1):
                        pe.wait_ge(message_ready, n)
                    for lane in range(LANES):
                        if bias is not None:
                            nc.tensor.matmul(kvq[:, lane, 0:3 * D], k["ones"][:, :], bias, start=True, stop=False)
                        nc.tensor.matmul(kvq[:, lane, 0:2 * D], normed_T[:, lane, :], w_kv, start=bias is None, stop=bias is None)
                        last = nc.tensor.matmul(kvq[:, lane, 2 * D:3 * D], normed_T[:, LANES + lane, :], w_q,
                                                start=bias is None, stop=True)
                    last.then_inc(projected, 1)

                def turn_over(n, s, turn):
                    pe.wait_ge(ln["applied"], n + 1)
                    for r in range(2 * LANES):
                        last = nc.tensor.transpose(banks(turned[:, :, :])[:, r, :], normed[:, r, :], k["identity"][:, :])
                    last.then_inc(transposed, 1)

                walk(pe, n_blocks, [(4, merge), (2, project), (1, turn_over)])

            @block.scalar
            def _(act):
                act.preload_act_table_set(TABLES)
                act.wait_ge(ln["eps_set"], 1)

                def copy_query(n, s, turn):
                    act.wait_ge(projected, n + 1)
                    if reused(n, 1):
                        act.wait_ge(terms_ready, n)
                    nc.scalar.activation(query[:, :, :], kvq[:, :, 2 * D:3 * D], ACT.Copy).then_inc(query_ready, 1)

                def score(n, s, turn):
                    act.wait_ge(clipped_ready, n + 1)
                    if reused(n, 2):
                        act.wait_ge(mg["merged"], n - 1)
                    nc.scalar.activation(message[:, s % 2, :, D:SUMS], clipped[:, :, :], ACT.Exp).then_inc(score_ready, 1)

                def norm(n, s, turn):
                    if reused(n, 1):
                        act.wait_ge(transposed, n)
                    ln_apply(ln, nc, act, normed[:, :, :], rows[:, s, :, :], n, s)

                def copy(n, s, turn):
                    act.wait_ge(transposed, n + 1)
                    if reused(n, 1):
                        act.wait_ge(projected, n)
                    nc.scalar.activation(flat(normed_T[:, :, :]), turned[:, :, :].rearrange("p b w -> p (b w)"), ACT.Copy).then_inc(copied, 1)

                walk(act, n_blocks, [(3, copy_query), (2, copy), (1, lambda n, s, turn: ln_deviate(ln, nc, act, n, s)),
                                     (3, score), (4, lambda n, s, turn: merge_keep(mg, nc, act, n, s)), (1, norm)])


def attend_state(sbuf, psum, sem, end_loads, zero_next, n_blocks):
    st = {}
    st["end_loads"] = end_loads
    st["end"] = sbuf("end", [P, SLOTS, 2 * LANES], I32)
    st["rows"] = sbuf("rows", [P, SLOTS, 2 * LANES, D])
    st["factor"] = sbuf("factor", [P, SLOTS, LANES])
    st["normed"] = sbuf("edge_normed", [P, 2 * LANES, D])
    st["normed_T"] = sbuf("edge_normed_T", [P, 2 * LANES, D])
    st["query"] = sbuf("query", [P, LANES, D])
    st["terms"] = sbuf("terms", [P, LANES, D])
    st["dots"] = sbuf("dots", [P, LANES, HEADS])
    st["weighted"] = sbuf("weighted", [P, LANES, HEADS])
    st["clipped"] = sbuf("clipped", [P, LANES, HEADS])
    st["message"] = sbuf("message", [P, 2, LANES, SUMS])
    st["turned"] = psum("edge_turned", [P, 512])
    st["kv"] = psum("kv", [P, 2, 512])
    st["q"] = psum("q", [P, 512])
    st["ends_in"] = [sem(f"ends_in{s}") for s in range(SLOTS)]
    st["gathered"] = [sem(f"gathered{s}") for s in range(SLOTS)]
    for x in ("src_turned", "dst_turned", "src_copied", "dst_copied", "projected", "query_ready", "terms_ready",
              "dots_ready", "weighted_ready", "clipped_ready", "score_ready", "message_ready"):
        st[x] = sem(x)
    st["ln"] = ln_state(sbuf, psum, sem, 2 * LANES, "edge_ln")
    st["mg"] = merge_state(sbuf, psum, sem, SUMS)
    st["mg"]["pool_passed"] = sem("pool_passed")
    st["zero"] = zero_state(sbuf, psum, sem, zero_next, n_blocks)
    return st


def attend_load(st, sp, ends, edge_weight, key_rows, n, s):
    if reused(n, SLOTS):
        sp.wait_ge(st["mg"]["target_ready"], n - SLOTS + 1)
    sp.dma_start(st["end"][:, s, :], ends[bass.ds(n, 1), :, :].rearrange("b p w -> (b p) w")).then_inc(st["ends_in"][s], 16)
    if edge_weight is not None:
        sp.dma_start(st["factor"][:, s, :], edge_weight[bass.ds(n, 1), :, :].rearrange("b p w -> (b p) w")).then_inc(st["ends_in"][s], 16)
    merge_load(st["mg"], sp, key_rows, n, s)


def attend_fetch(st, pool, nodes, n, s, turn):
    if reused(n, SLOTS):
        pool.wait_ge(st["ln"]["applied"], n - SLOTS + 1)
    pool.wait_ge(st["ends_in"][s], (turn + 1) * 16 * st["end_loads"])
    pool.sem_inc(st["mg"]["pool_passed"])
    gather(pool, st["rows"][:, s, :, :], nodes, st["end"][:, s, :], 2 * LANES, st["gathered"][s])


def attend_measure(st, nc, dve, n, s, turn):
    dve.wait_ge(st["gathered"][s], (turn + 1) * 2 * LANES * 16)
    ln_measure(st["ln"], nc, dve, st["rows"][:, s, :, :], n, s)


def attend_compare(st, nc, dve, k, n, s, turn):
    dve.wait_ge(st["ends_in"][s], (turn + 1) * 16 * st["end_loads"])
    merge_compare(st["mg"], nc, dve, st["end"][:, s, LANES:], n, s, turn)
    merge_recall(st["mg"], nc, dve, k["dst_targets"], n, s)


def attend_dot(st, nc, dve, edge_weight, n, s):
    dve.wait_ge(st["query_ready"], n + 1)
    nc.vector.tensor_tensor(st["terms"][:, :, :], st["kv"][:, :, :].rearrange("p b (l w) -> p (b l) w", w=2 * D)[:, :, 0:D],
                            st["query"][:, :, :], ALU.mult).then_inc(st["terms_ready"], 1)
    dve.wait_ge(st["terms_ready"], n + 1)
    nc.vector.tensor_reduce(st["dots"][:, :, :].rearrange("p l h -> p (l h)"),
                            st["terms"][:, :, :].rearrange("p l (h d) -> p (l h) d", d=HEAD_DIM),
                            AXIS_X, ALU.add).then_inc(st["dots_ready"], 1)
    dve.wait_ge(st["dots_ready"], n + 1)
    source = st["dots"]
    if edge_weight is not None:
        nc.vector.tensor_tensor(st["weighted"][:, :, :], st["dots"][:, :, :],
                                st["factor"][:, s, :].unsqueeze(2).to_broadcast([P, LANES, HEADS]),
                                ALU.mult).then_inc(st["weighted_ready"], 1)
        dve.wait_ge(st["weighted_ready"], n + 1)
        source = st["weighted"]
    if reused(n, 1):
        dve.wait_ge(st["score_ready"], n)
    nc.vector.tensor_scalar(st["clipped"][:, :, :], source[:, :, :], 5.0, -5.0, ALU.min, ALU.max).then_inc(st["clipped_ready"], 1)


def attend_weigh(st, nc, dve, n, s):
    dve.wait_ge(st["score_ready"], n + 1)
    m = st["message"][:, s % 2, :, :]
    for lane in range(LANES):
        at = lane % 2 * 2 * D + D
        last = nc.vector.tensor_tensor(m[:, lane, 0:D].rearrange("p (h d) -> p h d", d=HEAD_DIM),
                                       st["kv"][:, lane // 2, at:at + D].rearrange("p (h d) -> p h d", d=HEAD_DIM),
                                       m[:, lane, D:SUMS].unsqueeze(2).to_broadcast([P, HEADS, HEAD_DIM]), ALU.mult)
    last.then_inc(st["message_ready"], 1)


def attend_merge(st, nc, pe, n, s):
    pe.wait_ge(st["message_ready"], n + 1)
    merge_merge(st["mg"], nc, pe, lambda lane: st["message"][:, s % 2, lane, :], n, s)


def attend_project(st, nc, pe, k, w_kv, w_q, bias, n):
    pe.wait_ge(st["dst_copied"], n + 1)
    if reused(n, 1):
        pe.wait_ge(st["message_ready"], n)
    for lane in range(LANES):
        kv = st["kv"][:, lane // 2, lane % 2 * 2 * D:(lane % 2 + 1) * 2 * D]
        if bias is not None:
            nc.tensor.matmul(kv, k["ones"][:, :], bias[:, 0:2 * D], start=True, stop=False)
        nc.tensor.matmul(kv, st["normed_T"][:, lane, :], w_kv, start=bias is None, stop=True)
    for lane in range(LANES):
        q = st["q"][:, lane * D:(lane + 1) * D]
        if bias is not None:
            nc.tensor.matmul(q, k["ones"][:, :], bias[:, 2 * D:3 * D], start=True, stop=False)
        last = nc.tensor.matmul(q, st["normed_T"][:, LANES + lane, :], w_q, start=bias is None, stop=True)
    last.then_inc(st["projected"], 1)


def attend_turn_src(st, nc, pe, k, n):
    pe.wait_ge(st["ln"]["applied"], n + 1)
    if reused(n, 1):
        pe.wait_ge(st["dst_copied"], n)
    for r in range(LANES):
        last = nc.tensor.transpose(st["turned"][:, r * D:(r + 1) * D], st["normed"][:, r, :], k["identity"][:, :])
    last.then_inc(st["src_turned"], 1)


def attend_turn_dst(st, nc, pe, k, n):
    pe.wait_ge(st["src_copied"], n + 1)
    for r in range(LANES):
        last = nc.tensor.transpose(st["turned"][:, r * D:(r + 1) * D], st["normed"][:, LANES + r, :], k["identity"][:, :])
    last.then_inc(st["dst_turned"], 1)


def attend_copy_src(st, nc, act, n):
    act.wait_ge(st["src_turned"], n + 1)
    if reused(n, 1):
        act.wait_ge(st["projected"], n)
    nc.scalar.activation(flat(st["normed_T"][:, 0:LANES, :]), st["turned"][:, :], ACT.Copy).then_inc(st["src_copied"], 1)


def attend_copy_dst(st, nc, act, n):
    act.wait_ge(st["dst_turned"], n + 1)
    nc.scalar.activation(flat(st["normed_T"][:, LANES:, :]), st["turned"][:, :], ACT.Copy).then_inc(st["dst_copied"], 1)


def attend_copy_query(st, nc, act, n):
    act.wait_ge(st["projected"], n + 1)
    if reused(n, 1):
        act.wait_ge(st["terms_ready"], n)
    nc.scalar.activation(flat(st["query"][:, :, :]), st["q"][:, :], ACT.Copy).then_inc(st["query_ready"], 1)


def attend_score(st, nc, act, n, s):
    act.wait_ge(st["clipped_ready"], n + 1)
    if reused(n, 2):
        act.wait_ge(st["mg"]["merged"], n - 1)
    nc.scalar.activation(st["message"][:, s % 2, :, D:SUMS], st["clipped"][:, :, :], ACT.Exp).then_inc(st["score_ready"], 1)


def attend_norm(st, nc, act, n, s):
    if reused(n, 1):
        act.wait_ge(st["dst_turned"], n)
    ln_apply(st["ln"], nc, act, st["normed"][:, :, :], st["rows"][:, s, :, :], n, s)


def slot_stored(eng, stored, s, turn, n):
    if reused(n, NODE_SLOTS):
        eng.wait_ge(stored[(s - NODE_SLOTS) % SLOTS], 16 * (turn + (s >= NODE_SLOTS)))


"""Mean and variance of each feature over all nodes, features on the partitions, and the affine map
of the batch norm that follows from them."""


def bn_state(sbuf, psum, sem, halves):
    st = {}
    st["halves"] = halves
    st["part"] = sbuf("bn_part", [P, SLOTS, 2, 6])
    st["parts"] = sbuf("bn_parts", [P, halves, 6])
    st["moments"] = sbuf("bn_moments", [P, 2])
    st["logvar"] = sbuf("bn_logvar", [P, 1])
    st["rstd"] = sbuf("bn_rstd", [P, 1])
    st["shift"] = sbuf("bn_shift", [P, 1])
    st["eps"] = sbuf("bn_eps", [P, 1])
    st["part_done"], st["parts_done"], st["eps_set"], st["moments_done"], st["log_done"], st["rstd_done"], st["scale_done"], \
        st["shift_done"] = (sem(f"bn_{x}") for x in (
            "part_done", "parts_done", "eps_set", "moments_done", "log_done", "rstd_done", "scale_done", "shift_done"))
    return st


def bn_add(st, nc, dve, pieces, n, s):
    for i, piece in enumerate(pieces):
        last = nc.vector.bn_stats(st["part"][:, s, i, :], piece)
    last.then_inc(st["part_done"], 1)
    dve.wait_ge(st["part_done"], n + 1)
    c = len(pieces)
    nc.vector.tensor_scalar(st["parts"][:, bass.ds(n * c, c), :], st["part"][:, s, 0:c, :], 1.0, None, ALU.mult).then_inc(st["parts_done"], 1)


def bn_finish_vector(st, nc, dve, tiles, gain, offset, scale_out, shift_out):
    dve.wait_ge(st["parts_done"], tiles)
    nc.vector.bn_aggr(st["moments"][:, :], st["parts"][:, :, :].rearrange("p c w -> p (c w)")).then_inc(st["moments_done"], 1)
    dve.wait_ge(st["rstd_done"], 1)
    nc.vector.tensor_tensor(scale_out, st["rstd"][:, :], gain, ALU.mult).then_inc(st["scale_done"], 1)
    dve.wait_ge(st["scale_done"], 1)
    nc.vector.tensor_tensor(st["shift"][:, :], st["moments"][:, 0:1], scale_out, ALU.mult).then_inc(st["shift_done"], 1)
    dve.wait_ge(st["shift_done"], 1)
    nc.vector.tensor_tensor(shift_out, offset, st["shift"][:, :], ALU.subtract).then_inc(st["shift_done"], 1)


def bn_finish_scalar(st, nc, act):
    act.wait_ge(st["moments_done"], 1)
    nc.scalar.activation(st["logvar"][:, :], st["moments"][:, 1:2], ACT.Ln, bias=st["eps"][:, 0:1]).then_inc(st["log_done"], 1)
    act.wait_ge(st["log_done"], 1)
    nc.scalar.activation(st["rstd"][:, :], st["logvar"][:, :], ACT.Exp, scale=-0.5).then_inc(st["rstd_done"], 1)


def heads_state(sbuf, psum, sem):
    st = {}
    st["weight"] = sbuf("head_weight", [P, SLOTS, ROWS, HEADS])
    st["inverse"] = sbuf("head_inverse", [P, SLOTS, ROWS, HEADS])
    st["weight_done"], st["inverse_done"], st["mean_done"] = (sem(f"head_{x}") for x in ("weight_done", "inverse_done", "mean_done"))
    return st


def heads_weigh(st, nc, sums, s):
    nc.vector.tensor_scalar(st["weight"][:, s, :, :], sums[:, :, D:SUMS], Z_EPS, None, ALU.add).then_inc(st["weight_done"], 1)


def heads_invert(st, nc, dve, n, s):
    dve.wait_ge(st["weight_done"], n + 1)
    nc.vector.reciprocal(st["inverse"][:, s, :, :], st["weight"][:, s, :, :]).then_inc(st["inverse_done"], 1)


def heads_mean(st, eng, out, sums, n, s):
    eng.wait_ge(st["inverse_done"], n + 1)
    eng.tensor_tensor(out.rearrange("p r (h d) -> p r h d", d=HEAD_DIM),
                      sums[:, :, 0:D].rearrange("p r (h d) -> p r h d", d=HEAD_DIM),
                      st["inverse"][:, s, :, :].unsqueeze(3).to_broadcast([P, ROWS, HEADS, HEAD_DIM]),
                      ALU.mult).then_inc(st["mean_done"], 1)


def column_chunk(table, n, width=CHUNK):
    return table[bass.ds(n, 1), :, :].rearrange("c p w -> (c p) w")


def attention1_nodes(nc, k, x, sums, y_T, n_chunks, last_valid):
    with phase(nc, "l1_nodes") as (sbuf, psum, sem):
        xs = sbuf("xs", [P, SLOTS, ROWS, D])
        acc = sbuf("acc", [P, SLOTS, ROWS, SUMS])
        att = sbuf("att", [P, 2, ROWS, D])
        att_T = sbuf("att_T", [P, 2, 2, 512])
        normed = sbuf("normed", [P, 2, ROWS, D])
        y = sbuf("y", [P, SLOTS, CHUNK])
        turned = [psum(f"turned{s}", [P, 2, 512]) for s in range(2)]
        total = [psum(f"total{s}", [P, 2, 512]) for s in range(2)]
        loaded = [sem(f"loaded{s}") for s in range(SLOTS)]
        stored = [sem(f"stored{s}") for s in range(SLOTS)]
        transposed, copied_low, copied_high, totalled, y_ready = (
            sem(x) for x in ("transposed", "copied_low", "copied_high", "totalled", "y_ready"))
        ln = ln_state(sbuf, psum, sem, ROWS)
        heads = heads_state(sbuf, psum, sem)
        bn = bn_state(sbuf, psum, sem, 2 * n_chunks)
        with nc.Block() as block:

            @block.sync
            def _(sp):
                def load(n, s, turn):
                    if reused(n, SLOTS):
                        sp.wait_ge(totalled, n - SLOTS + 1)
                    sp.dma_start(flat(xs[:, s, :, :]), chunk_of(x, n)).then_inc(loaded[s], 16)
                    sp.dma_start(flat(acc[:, s, :, :]), chunk_of(sums, n)).then_inc(loaded[s], 16)

                def store(n, s, turn):
                    sp.wait_ge(y_ready, n + 1)
                    sp.dma_start(column_chunk(y_T, n), y[:, s, :]).then_inc(stored[s], 16)

                walk(sp, n_chunks, [(0, load), (6, store)])
                for s in range(SLOTS):
                    sp.wait_ge(stored[s], 16 * uses(n_chunks, s))

            @block.vector
            def _(dve):
                nc.vector.memset(bn["eps"][:, :], BN_EPS)
                ln_set_eps(ln, nc)

                def weigh(n, s, turn):
                    dve.wait_ge(loaded[s], (turn + 1) * 32)
                    heads_weigh(heads, nc, acc[:, s, :, :], s)

                def stats(n, s, turn):
                    dve.wait_ge(y_ready, n + 1)
                    halves = [y[:, s, h * 512:(h + 1) * 512] for h in range(2)]
                    if isinstance(n, int) and n == n_chunks - 1:
                        halves = [h.rearrange("p (r q) -> p r q", q=P)[:, :, 0:last_valid] for h in halves]
                    bn_add(bn, nc, dve, halves, n, s)

                def copy_high(n, s, turn):
                    dve.wait_ge(transposed, n + 1)
                    if reused(n, 2):
                        dve.wait_ge(totalled, n - 1)
                    nc.vector.tensor_copy(att_T[:, s % 2, 1, :], turned[s % 2][:, 1, :]).then_inc(copied_high, 1)

                walk(dve, n_chunks, [(0, weigh), (2, lambda n, s, turn: ln_centre(ln, nc, dve, n, s)),
                                     (1, lambda n, s, turn: ln_sums(ln, nc, dve, n, s)),
                                     (0, lambda n, s, turn: heads_invert(heads, nc, dve, n, s)),
                                     (1, lambda n, s, turn: ln_between(ln, nc, dve, n, s)),
                                     (5, stats),
                                     (1, lambda n, s, turn: ln_var(ln, nc, dve, n, s)),
                                     (1, copy_high),
                                     (0, lambda n, s, turn: ln_count(ln, nc, xs[:, s, :, :], s))])
                bn_finish_vector(bn, nc, dve, n_chunks, k["col"]["l1_g1"], k["col"]["l1_b1"], k["bn"][:, 0:1], k["bn"][:, 1:2])

            @block.gpsimd
            def _(pool):
                def mean(n, s, turn):
                    if reused(n, 2):
                        pool.wait_ge(transposed, n - 1)
                    heads_mean(heads, nc.gpsimd, att[:, s % 2, :, :], acc[:, s, :, :], n, s)

                walk(pool, n_chunks, [(0, mean)])

            @block.tensor
            def _(pe):
                def turn_over(n, s, turn):
                    pe.wait_ge(heads["mean_done"], n + 1)
                    if reused(n, 2):
                        pe.wait_ge(copied_low, n - 1)
                        pe.wait_ge(copied_high, n - 1)
                    for r in range(ROWS):
                        last = nc.tensor.transpose(banks(turned[s % 2][:, :, :])[:, r, :], att[:, s % 2, r, :], k["identity"][:, :])
                    last.then_inc(transposed, 1)

                def add_up(n, s, turn):
                    pe.wait_ge(copied_low, n + 1)
                    pe.wait_ge(copied_high, n + 1)
                    pe.wait_ge(ln["applied"], n + 1)
                    if reused(n, 2):
                        pe.wait_ge(y_ready, n - 1)
                    for h in range(2):
                        nc.tensor.matmul(total[s % 2][:, h, :], k["W"]["l1_o"], att_T[:, s % 2, h, :], start=True, stop=False)
                        for r in range(LANES):
                            last = nc.tensor.matmul(total[s % 2][:, h, r * P:(r + 1) * P], normed[:, s % 2, h * LANES + r, :],
                                                    k["identity"][:, :], start=False, stop=r == LANES - 1)
                    last.then_inc(totalled, 1)

                walk(pe, n_chunks, [(3, add_up), (1, turn_over)])

            @block.scalar
            def _(act):
                act.preload_act_table_set(TABLES)
                act.wait_ge(ln["eps_set"], 1)

                def copy_low(n, s, turn):
                    act.wait_ge(transposed, n + 1)
                    if reused(n, 2):
                        act.wait_ge(totalled, n - 1)
                    nc.scalar.activation(att_T[:, s % 2, 0, :], turned[s % 2][:, 0, :], ACT.Copy).then_inc(copied_low, 1)

                def norm(n, s, turn):
                    if reused(n, 2):
                        act.wait_ge(totalled, n - 1)
                    ln_apply(ln, nc, act, normed[:, s % 2, :, :], xs[:, s, :, :], n, s)

                def take(n, s, turn):
                    act.wait_ge(totalled, n + 1)
                    if reused(n, SLOTS):
                        act.wait_ge(stored[s], turn * 16)
                        act.wait_ge(bn["part_done"], n - SLOTS + 1)
                    nc.scalar.activation(y[:, s, :], total[s % 2][:, :, :].rearrange("p b w -> p (b w)"), ACT.Identity,
                                         bias=k["col"]["l1_bo"]).then_inc(y_ready, 1)

                walk(act, n_chunks, [(4, take), (2, norm), (1, lambda n, s, turn: ln_deviate(ln, nc, act, n, s)), (1, copy_low)])
                bn_finish_scalar(bn, nc, act)


def feed_forward(nc, k, y_T, z_T, n_chunks, last_valid):
    tiles = 2 * n_chunks
    half = CHUNK // 2
    with phase(nc, "ffn") as (sbuf, psum, sem):
        ys = sbuf("ys", [P, SLOTS, half])
        normed = sbuf("normed", [P, SLOTS, half])
        hidden = sbuf("hidden", [P, 2, 2, half])
        z = sbuf("z", [P, SLOTS, half])
        up = [psum(f"up{s}", [P, 2, 512]) for s in range(2)]
        down = [psum(f"down{s}", [P, 512]) for s in range(2)]
        loaded = [sem(f"loaded{s}") for s in range(SLOTS)]
        stored = [sem(f"stored{s}") for s in range(SLOTS)]
        normed_ready, raised, hidden_ready, lowered, z_ready, eps_set = (
            sem(x) for x in ("normed_ready", "raised", "hidden_ready", "lowered", "z_ready", "eps_set"))
        bn = bn_state(sbuf, psum, sem, tiles)
        with nc.Block() as block:

            def half_of(table, n_slot_even, chunk):
                return column_chunk(table, chunk)[:, n_slot_even * half:(n_slot_even + 1) * half]

            @block.sync
            def _(sp):
                def load(n, s, turn):
                    if reused(n, SLOTS):
                        sp.wait_ge(normed_ready, n - SLOTS + 1)
                    sp.dma_start(ys[:, s, :], half_of(y_T, s % 2, turn * (SLOTS // 2) + s // 2)).then_inc(loaded[s], 16)

                def store(n, s, turn):
                    sp.wait_ge(z_ready, n + 1)
                    sp.dma_start(half_of(z_T, s % 2, turn * (SLOTS // 2) + s // 2), z[:, s, :]).then_inc(stored[s], 16)

                walk(sp, tiles, [(0, load), (3, store)])
                for s in range(SLOTS):
                    sp.wait_ge(stored[s], 16 * uses(tiles, s))

            @block.vector
            def _(dve):
                nc.vector.memset(bn["eps"][:, :], BN_EPS).then_inc(eps_set, 1)

                def norm(n, s, turn):
                    dve.wait_ge(loaded[s], (turn + 1) * 16)
                    nc.vector.tensor_scalar(normed[:, s, :], ys[:, s, :], k["bn"][:, 0:1], k["bn"][:, 1:2], ALU.mult, ALU.add).then_inc(normed_ready, 1)

                def add(n, s, turn):
                    dve.wait_ge(lowered, n + 1)
                    if reused(n, SLOTS):
                        dve.wait_ge(stored[s], turn * 16)
                    nc.vector.scalar_tensor_tensor(out=z[:, s, :], in0=down[s % 2][:, :], scalar=k["col"]["l1_bf2"],
                                                   in1=normed[:, s, :], op0=ALU.add, op1=ALU.add).then_inc(z_ready, 1)
                    dve.wait_ge(z_ready, n + 1)
                    piece = z[:, s, :]
                    if isinstance(n, int) and n >= tiles - 2:
                        piece = piece.rearrange("p (r q) -> p r q", q=P)[:, :, 0:last_valid]
                    bn_add(bn, nc, dve, [piece], n, s)

                walk(dve, tiles, [(0, norm), (2, add)])
                bn_finish_vector(bn, nc, dve, tiles, k["col"]["l1_g2"], k["col"]["l1_b2"], k["bn"][:, 2:3], k["bn"][:, 3:4])

            @block.tensor
            def _(pe):
                def raise_(n, s, turn):
                    pe.wait_ge(normed_ready, n + 1)
                    if reused(n, 2):
                        pe.wait_ge(hidden_ready, n - 1)
                    for f in range(2):
                        last = nc.tensor.matmul(up[s % 2][:, f, :], k["W"][f"ffn_up{f}"], normed[:, s, :], start=True, stop=True)
                    last.then_inc(raised, 1)

                def lower(n, s, turn):
                    pe.wait_ge(hidden_ready, n + 1)
                    if reused(n, 2):
                        pe.wait_ge(z_ready, n - 1)
                    for f in range(2):
                        last = nc.tensor.matmul(down[s % 2][:, :], k["W"][f"ffn_down{f}"], hidden[:, s % 2, f, :], start=f == 0, stop=f == 1)
                    last.then_inc(lowered, 1)

                walk(pe, tiles, [(0, raise_), (1, lower)])

            @block.scalar
            def _(act):
                act.preload_act_table_set(TABLES)

                def rectify(n, s, turn):
                    act.wait_ge(raised, n + 1)
                    if reused(n, 2):
                        act.wait_ge(lowered, n - 1)
                    for f, b in enumerate(("l1_bf1a", "l1_bf1b")):
                        last = nc.scalar.activation(hidden[:, s % 2, f, :], up[s % 2][:, f, :], ACT.Relu, bias=k["col"][b])
                    last.then_inc(hidden_ready, 1)

                walk(act, tiles, [(0, rectify)])
                act.wait_ge(eps_set, 1)
                bn_finish_scalar(bn, nc, act)


def add_layer1(nc, k, x, z_T, out, n_chunks):
    with phase(nc, "l1_add") as (sbuf, psum, sem):
        xs = sbuf("xs", [P, SLOTS, ROWS, D])
        zs = sbuf("zs", [P, SLOTS, ROWS, D])
        normed = sbuf("normed", [P, 2, ROWS, D])
        result = sbuf("result", [P, SLOTS, ROWS, D])
        turned = [psum(f"turned{s}", [P, 2, 512]) for s in range(2)]
        loaded = [sem(f"loaded{s}") for s in range(SLOTS)]
        stored = [sem(f"stored{s}") for s in range(SLOTS)]
        normed_ready, transposed, finished = (sem(x) for x in ("normed_ready", "transposed", "finished"))
        with nc.Block() as block:

            @block.sync
            def _(sp):
                def load(n, s, turn):
                    if reused(n, SLOTS):
                        sp.wait_ge(finished, n - SLOTS + 1)
                    sp.dma_start(flat(zs[:, s, :, :]), column_chunk(z_T, n)).then_inc(loaded[s], 16)
                    sp.dma_start(flat(xs[:, s, :, :]), chunk_of(x, n)).then_inc(loaded[s], 16)

                def store(n, s, turn):
                    sp.wait_ge(finished, n + 1)
                    sp.dma_start(chunk_of(out, n), flat(result[:, s, :, :])).then_inc(stored[s], 16)

                walk(sp, n_chunks, [(0, load), (2, store)])
                for s in range(SLOTS):
                    sp.wait_ge(stored[s], 16 * uses(n_chunks, s))

            @block.scalar
            def _(act):
                def norm(n, s, turn):
                    act.wait_ge(loaded[s], (turn + 1) * 32)
                    if reused(n, 2):
                        act.wait_ge(transposed, n - 1)
                    nc.scalar.activation(flat(normed[:, s % 2, :, :]), flat(zs[:, s, :, :]), ACT.Identity, bias=k["bn"][:, 3:4],
                                         scale=k["bn"][:, 2:3]).then_inc(normed_ready, 1)

                walk(act, n_chunks, [(0, norm)])

            @block.tensor
            def _(pe):
                def turn_over(n, s, turn):
                    pe.wait_ge(normed_ready, n + 1)
                    if reused(n, 2):
                        pe.wait_ge(finished, n - 1)
                    for r in range(ROWS):
                        last = nc.tensor.transpose(banks(turned[s % 2][:, :, :])[:, r, :], normed[:, s % 2, r, :], k["identity"][:, :])
                    last.then_inc(transposed, 1)

                walk(pe, n_chunks, [(0, turn_over)])

            @block.vector
            def _(dve):
                def add(n, s, turn):
                    dve.wait_ge(transposed, n + 1)
                    if reused(n, SLOTS):
                        dve.wait_ge(stored[s], turn * 16)
                    nc.vector.tensor_tensor(flat(result[:, s, :, :]), turned[s % 2][:, :, :].rearrange("p b w -> p (b w)"),
                                            flat(xs[:, s, :, :]), ALU.add).then_inc(finished, 1)

                walk(dve, n_chunks, [(0, add)])


def attention2_layer(nc, k, name, ends, key_rows, x, sums, x_out, accumulator, n_blocks, n_chunks, together):
    with phase(nc, name) as (sbuf, psum, sem):
        ed = attend_state(sbuf, psum, sem, 1, None, n_blocks)
        mg = ed["mg"]
        w_at = MATRICES.index("l2_k")
        w_kv = k["matrices"][:, w_at:w_at + 2, :].rearrange("p m d -> p (m d)")
        w_q = k["matrices"][:, w_at + 2, :]
        xs = sbuf("xs", [P, NODE_SLOTS, ROWS, D])
        acc = sbuf("acc", [P, NODE_SLOTS, ROWS, SUMS])
        att = sbuf("att", [P, ROWS, D])
        new = sbuf("new", [P, NODE_SLOTS, ROWS, D])
        normed = sbuf("normed", [P, ROWS, D])
        normed_T = sbuf("normed_T", [P, 2, ROWS, D])
        own = sbuf("own", [P, NODE_SLOTS, ROWS, D])
        turned = psum("turned", [P, 512])
        product = psum("product", [P, 512])
        loaded = [sem(f"loaded{s}") for s in range(SLOTS)]
        new_stored = [sem(f"new_stored{s}") for s in range(SLOTS)]
        own_stored = [sem(f"own_stored{s}") for s in range(SLOTS)]
        new_ready = sem("new_ready")
        transposed, copied, multiplied, own_ready = ([sem(f"{x}_{h}") for h in ("low", "high")]
                                                     for x in ("transposed", "copied", "multiplied", "own_ready"))
        ln = ln_state(sbuf, psum, sem, ROWS)
        heads = heads_state(sbuf, psum, sem)

        def pass_over(eng, stages):
            if together:
                walk(eng, n_blocks, [(stage[0] + NODES_LAG * (len(stage) > 2), stage[1]) for stage in stages])
            else:
                walk(eng, n_blocks, [stage for stage in stages if len(stage) == 2])
                walk(eng, n_chunks, [stage[0:2] for stage in stages if len(stage) > 2])

        with nc.Block() as block:

            @block.sync
            def _(sp):
                def load_edges(n, s, turn):
                    attend_load(ed, sp, ends, None, key_rows, n, s)

                def load(n, s, turn):
                    if reused(n, NODE_SLOTS):
                        sp.wait_ge(new_ready, n - NODE_SLOTS + 1)
                    sp.dma_start(flat(xs[:, s % NODE_SLOTS, :, :]), chunk_of(x, n)).then_inc(loaded[s], 16)
                    if together:
                        last = n + BEHIND if not isinstance(n, int) else min(n + BEHIND, n_blocks - 1)
                        sp.wait_ge(mg["scattered"], (last + 1) * LANES * 16)
                    elif isinstance(n, int) and n == 0:
                        sp.wait_ge(mg["scattered"], n_blocks * LANES * 16)
                    sp.dma_start(flat(acc[:, s % NODE_SLOTS, :, :]), chunk_of(sums, n)).then_inc(loaded[s], 16)

                def store_new(n, s, turn):
                    sp.wait_ge(new_ready, n + 1)
                    sp.dma_start(chunk_of(x_out, n), flat(new[:, s % NODE_SLOTS, :, :])).then_inc(new_stored[s], 16)

                def store_own(n, s, turn):
                    sp.wait_ge(own_ready[1], n + 1)
                    sp.dma_start(chunk_of(accumulator, n), flat(own[:, s % NODE_SLOTS, :, :])).then_inc(own_stored[s], 16)

                pass_over(sp, [(8, store_own, NODES), (0, load_edges), (4, store_new, NODES), (0, load, NODES)]
                          if together else [(0, load_edges), (6, store_own, NODES), (2, store_new, NODES), (0, load, NODES)])
                for s in range(SLOTS):
                    sp.wait_ge(new_stored[s], 16 * uses(n_chunks, s))
                    sp.wait_ge(own_stored[s], 16 * uses(n_chunks, s))

            @block.gpsimd
            def _(pool):
                walk(pool, n_blocks, [(0, lambda n, s, turn: attend_fetch(ed, pool, x, n, s, turn)),
                                      (5, lambda n, s, turn: merge_scatter(mg, nc, pool, sums, n, s))])
                pool.wait_ge(mg["scattered"], n_blocks * LANES * 16)

            @block.vector
            def _(dve):
                ln_set_eps(ed["ln"], nc)
                ln_set_eps(ln, nc)

                def weigh(n, s, turn):
                    dve.wait_ge(loaded[s], (turn + 1) * 32)
                    heads_weigh(heads, nc, acc[:, s % NODE_SLOTS, :, :], s)

                def mean(n, s, turn):
                    if reused(n, 1):
                        dve.wait_ge(new_ready, n)
                    heads_mean(heads, nc.vector, att[:, :, :], acc[:, s % NODE_SLOTS, :, :], n, s)

                def add(n, s, turn):
                    dve.wait_ge(heads["mean_done"], n + 1)
                    slot_stored(dve, new_stored, s, turn, n)
                    if reused(n, NODE_SLOTS):
                        dve.wait_ge(ln["applied"], n - NODE_SLOTS + 1)
                    nc.vector.tensor_tensor(flat(new[:, s % NODE_SLOTS, :, :]), flat(xs[:, s % NODE_SLOTS, :, :]),
                                            flat(att[:, :, :]), ALU.add).then_inc(new_ready, 1)

                def count(n, s, turn):
                    dve.wait_ge(new_ready, n + 1)
                    ln_count(ln, nc, new[:, s % NODE_SLOTS, :, :], s)

                pass_over(dve, [(3, lambda n, s, turn: attend_dot(ed, nc, dve, None, n, s)),
                                (1, lambda n, s, turn: ln_centre(ed["ln"], nc, dve, n, s)),
                                (0, weigh, NODES),
                                (3, lambda n, s, turn: ln_centre(ln, nc, dve, n, s), NODES),
                                (3, lambda n, s, turn: attend_weigh(ed, nc, dve, n, s)),
                                (2, lambda n, s, turn: ln_sums(ln, nc, dve, n, s), NODES),
                                (0, lambda n, s, turn: heads_invert(heads, nc, dve, n, s), NODES),
                                (3, lambda n, s, turn: attend_compare(ed, nc, dve, k, n, s, turn)),
                                (2, lambda n, s, turn: ln_between(ln, nc, dve, n, s), NODES),
                                (1, add, NODES),
                                (2, lambda n, s, turn: ln_var(ln, nc, dve, n, s), NODES),
                                (0, mean, NODES),
                                (1, count, NODES),
                                (0, lambda n, s, turn: attend_measure(ed, nc, dve, n, s, turn))])

            @block.tensor
            def _(pe):
                def turn_low(n, s, turn):
                    pe.wait_ge(ln["applied"], n + 1)
                    if reused(n, 1):
                        pe.wait_ge(copied[1], n)
                    for r in range(LANES):
                        last = nc.tensor.transpose(turned[:, r * D:(r + 1) * D], normed[:, r, :], k["identity"][:, :])
                    last.then_inc(transposed[0], 1)

                def turn_high(n, s, turn):
                    pe.wait_ge(copied[0], n + 1)
                    for r in range(LANES):
                        last = nc.tensor.transpose(turned[:, r * D:(r + 1) * D], normed[:, LANES + r, :], k["identity"][:, :])
                    last.then_inc(transposed[1], 1)

                def multiply_half(h, s):
                    for r in range(LANES):
                        nc.tensor.matmul(product[:, r * D:(r + 1) * D], k["ones"][:, :], k["bias"]["l3_b_c"], start=True, stop=False)
                        last = nc.tensor.matmul(product[:, r * D:(r + 1) * D], normed_T[:, s % 2, h * LANES + r, :], k["W"]["l3_c"],
                                                start=False, stop=True)
                    last.then_inc(multiplied[h], 1)

                def multiply_low(n, s, turn):
                    pe.wait_ge(copied[1], n + 1)
                    if reused(n, 1):
                        pe.wait_ge(own_ready[1], n)
                    multiply_half(0, s)

                def multiply_high(n, s, turn):
                    pe.wait_ge(own_ready[0], n + 1)
                    multiply_half(1, s)

                pass_over(pe, [(5, multiply_low, NODES),
                               (4, lambda n, s, turn: attend_merge(ed, nc, pe, n, s)),
                               (4, turn_low, NODES),
                               (5, multiply_high, NODES),
                               (2, lambda n, s, turn: attend_project(ed, nc, pe, k, w_kv, w_q, k["bias_parts"][:, 0:3 * D], n)),
                               (1, lambda n, s, turn: attend_turn_src(ed, nc, pe, k, n)),
                               (4, turn_high, NODES),
                               (1, lambda n, s, turn: attend_turn_dst(ed, nc, pe, k, n))])

            @block.scalar
            def _(act):
                act.preload_act_table_set(TABLES)
                act.wait_ge(ed["ln"]["eps_set"], 1)
                act.wait_ge(ln["eps_set"], 1)

                def norm(n, s, turn):
                    if reused(n, 1):
                        act.wait_ge(transposed[1], n)
                    ln_apply(ln, nc, act, normed[:, :, :], new[:, s % NODE_SLOTS, :, :], n, s)

                def copy_low(n, s, turn):
                    act.wait_ge(transposed[0], n + 1)
                    if reused(n, 2):
                        act.wait_ge(multiplied[1], n - 1)
                    nc.scalar.activation(flat(normed_T[:, s % 2, 0:LANES, :]), turned[:, :], ACT.Copy).then_inc(copied[0], 1)

                def copy_high(n, s, turn):
                    act.wait_ge(transposed[1], n + 1)
                    nc.scalar.activation(flat(normed_T[:, s % 2, LANES:, :]), turned[:, :], ACT.Copy).then_inc(copied[1], 1)

                def take_low(n, s, turn):
                    act.wait_ge(multiplied[0], n + 1)
                    slot_stored(act, own_stored, s, turn, n)
                    nc.scalar.activation(flat(own[:, s % NODE_SLOTS, 0:LANES, :]), product[:, :], ACT.Copy).then_inc(own_ready[0], 1)

                def take_high(n, s, turn):
                    act.wait_ge(multiplied[1], n + 1)
                    nc.scalar.activation(flat(own[:, s % NODE_SLOTS, LANES:, :]), product[:, :], ACT.Copy).then_inc(own_ready[1], 1)

                pass_over(act, [(3, lambda n, s, turn: attend_copy_query(ed, nc, act, n)),
                                (2, lambda n, s, turn: attend_copy_dst(ed, nc, act, n)),
                                (5, take_low, NODES),
                                (1, lambda n, s, turn: ln_deviate(ed["ln"], nc, act, n, s)),
                                (3, lambda n, s, turn: attend_score(ed, nc, act, n, s)),
                                (4, copy_low, NODES),
                                (4, lambda n, s, turn: merge_keep(mg, nc, act, n, s)),
                                (1, lambda n, s, turn: attend_norm(ed, nc, act, n, s)),
                                (5, take_high, NODES),
                                (2, lambda n, s, turn: ln_deviate(ln, nc, act, n, s), NODES),
                                (1, lambda n, s, turn: attend_copy_src(ed, nc, act, n)),
                                (4, copy_high, NODES),
                                (3, norm, NODES)])


def softplus_state(sbuf, psum, sem, width):
    st = {}
    st["size"] = sbuf("sp_size", [P, 2, width])
    st["decay"] = sbuf("sp_decay", [P, 2, width])
    st["tail"] = sbuf("sp_tail", [P, 2, width])
    st["half"] = sbuf("sp_half", [P, 1])
    st["half_set"], st["size_done"], st["decay_done"], st["tail_done"], st["done"] = (
        sem(f"sp_{x}") for x in ("half_set", "size_done", "decay_done", "tail_done", "done"))
    return st


def softplus_set_half(st, nc):
    nc.vector.memset(st["half"][:, :], 0.5).then_inc(st["half_set"], 1)


def softplus_tails(st, nc, act, x, bias, n, s):
    u = s % 2
    nc.scalar.activation(st["size"][:, u, :], x, ACT.Abs, **({} if bias is None else {"bias": bias})).then_inc(st["size_done"], 1)
    act.wait_ge(st["size_done"], n + 1)
    nc.scalar.activation(st["decay"][:, u, :], st["size"][:, u, :], ACT.Exp, scale=-1.0).then_inc(st["decay_done"], 1)
    act.wait_ge(st["decay_done"], n + 1)
    if reused(n, 2):
        act.wait_ge(st["done"], n - 1)
    nc.scalar.activation(st["tail"][:, u, :], st["decay"][:, u, :], ACT.Ln, scale=0.5, bias=st["half"][:, 0:1]).then_inc(st["tail_done"], 1)


def messages_over_edges(nc, k, ends, key_rows, edge_T, nodes, accumulator, n_blocks):
    with phase(nc, "l3_edges") as (sbuf, psum, sem):
        end = sbuf("end", [P, SLOTS, 2 * LANES], I32)
        rows = sbuf("rows", [P, SLOTS, LANES, D])
        edge = sbuf("edge", [64, SLOTS, BLOCK])
        normed = sbuf("normed", [P, LANES, D])
        normed_T = sbuf("normed_T", [P, BLOCK])
        positive = sbuf("positive", [P, BLOCK])
        soft = sbuf("soft", [P, 2, BLOCK])
        value = sbuf("value", [P, BLOCK])
        gated = sbuf("gated", [P, BLOCK])
        message = sbuf("message", [P, 2, LANES, D])
        pre_psum, gate_psum, turned, value_psum, message_psum = (
            psum(x, [P, 512]) for x in ("pre_psum", "gate_psum", "turned", "value_psum", "message_psum"))
        ends_in = [sem(f"ends_in{s}") for s in range(SLOTS)]
        edge_in = [sem(f"edge_in{s}") for s in range(SLOTS)]
        gathered = [sem(f"gathered{s}") for s in range(SLOTS)]
        pre_ready, gate_ready, transposed, copied, value_done, value_ready, gated_ready, message_done, \
            message_ready = (sem(x) for x in (
                "pre_ready", "gate_ready", "transposed", "copied", "value_done", "value_ready",
                "gated_ready", "message_done", "message_ready"))
        ln = ln_state(sbuf, psum, sem, LANES)
        sp_ = softplus_state(sbuf, psum, sem, BLOCK)
        mg = merge_state(sbuf, psum, sem, D)
        mg["pool_passed"] = sem("pool_passed")
        with nc.Block() as block:

            @block.sync
            def _(sp):
                def load(n, s, turn):
                    if reused(n, SLOTS):
                        sp.wait_ge(mg["target_ready"], n - SLOTS + 1)
                    sp.dma_start(end[:, s, :], ends[bass.ds(n, 1), :, :].rearrange("b p w -> (b p) w")).then_inc(ends_in[s], 16)
                    sp.dma_start(edge[:, s, :], edge_T[:, bass.ds(n * BLOCK, BLOCK)]).then_inc(edge_in[s], 16)
                    merge_load(mg, sp, key_rows, n, s)

                walk(sp, n_blocks, [(0, load)])

            @block.gpsimd
            def _(pool):
                def fetch(n, s, turn):
                    if reused(n, SLOTS):
                        pool.wait_ge(ln["applied"], n - SLOTS + 1)
                    pool.wait_ge(ends_in[s], turn * 16 + 16)
                    pool.sem_inc(mg["pool_passed"])
                    gather(pool, rows[:, s, :, :], nodes, end[:, s, LANES:], LANES, gathered[s])

                walk(pool, n_blocks, [(0, fetch), (6, lambda n, s, turn: merge_scatter(mg, nc, pool, accumulator, n, s))])
                pool.wait_ge(mg["scattered"], n_blocks * LANES * 16)

            @block.vector
            def _(dve):
                ln_set_eps(ln, nc)
                softplus_set_half(sp_, nc)

                def soften(n, s, turn):
                    dve.wait_ge(sp_["tail_done"], n + 1)
                    if reused(n, 2):
                        dve.wait_ge(gate_ready, n - 1)
                    nc.vector.tensor_tensor(soft[:, s % 2, :], positive[:, :], sp_["tail"][:, s % 2, :], ALU.add).then_inc(sp_["done"], 1)

                def measure(n, s, turn):
                    dve.wait_ge(gathered[s], (turn + 1) * LANES * 16)
                    ln_measure(ln, nc, dve, rows[:, s, :, :], n, s)

                def compare(n, s, turn):
                    dve.wait_ge(ends_in[s], (turn + 1) * 16)
                    merge_compare(mg, nc, dve, end[:, s, 0:LANES], n, s, turn)
                    merge_place(mg, nc, dve, k, n, s)

                def compose(n, s, turn):
                    dve.wait_ge(message_done, n + 1)
                    if reused(n, 2):
                        dve.wait_ge(mg["merged"], n - 1)
                    nc.vector.tensor_tensor(message[:, s % 2, :, :], message_psum[:, :].rearrange("p (l d) -> p l d", d=D),
                                            k["row"]["l3_b_wvl"].unsqueeze(1).to_broadcast([P, LANES, D]), ALU.add).then_inc(message_ready, 1)

                def gate(n, s, turn):
                    dve.wait_ge(gate_ready, n + 1)
                    dve.wait_ge(value_ready, n + 1)
                    if reused(n, 1):
                        dve.wait_ge(message_done, n)
                    nc.vector.scalar_tensor_tensor(out=gated[:, :], in0=gate_psum[:, :], scalar=k["col"]["l3_b_wv2"], in1=value[:, :],
                                                   op0=ALU.add, op1=ALU.mult).then_inc(gated_ready, 1)

                walk(dve, n_blocks, [(3, gate), (4, compose), (1, measure), (4, compare),
                                     (1, lambda n, s, turn: ln_centre(ln, nc, dve, n, s)), (1, soften)])

            @block.tensor
            def _(pe):
                def merge(n, s, turn):
                    pe.wait_ge(message_ready, n + 1)
                    merge_merge(mg, nc, pe, lambda lane: message[:, s % 2, lane, :], n, s)

                def gate(n, s, turn):
                    pe.wait_ge(sp_["done"], n + 1)
                    if reused(n, 1):
                        pe.wait_ge(gated_ready, n)
                    nc.tensor.matmul(gate_psum[:, :], k["W"]["l3_wv2"], soft[:, s % 2, :], start=True, stop=True).then_inc(gate_ready, 1)
                    pe.wait_ge(copied, n + 1)
                    nc.tensor.matmul(value_psum[:, :], k["W"]["l3_v"], normed_T[:, :], start=True, stop=True).then_inc(value_done, 1)

                def express(n, s, turn):
                    pe.wait_ge(gated_ready, n + 1)
                    if reused(n, 1):
                        pe.wait_ge(message_ready, n)
                    for lane in range(LANES):
                        last = nc.tensor.matmul(message_psum[:, lane * D:(lane + 1) * D], gated[:, lane * P:(lane + 1) * P], k["W"]["l3_wvl"],
                                                start=True, stop=True)
                    last.then_inc(message_done, 1)

                def embed(n, s, turn):
                    pe.wait_ge(edge_in[s], (turn + 1) * 16)
                    if reused(n, 1):
                        pe.wait_ge(sp_["size_done"], n)
                    nc.tensor.matmul(pre_psum[:, :], k["wv1"][:, :], edge[:, s, :], start=True, stop=True).then_inc(pre_ready, 1)

                def turn_over(n, s, turn):
                    pe.wait_ge(ln["applied"], n + 1)
                    for r in range(LANES):
                        last = nc.tensor.transpose(turned[:, r * P:(r + 1) * P], normed[:, r, :], k["identity"][:, :])
                    last.then_inc(transposed, 1)

                walk(pe, n_blocks, [(5, merge), (3, express), (2, gate), (0, embed), (1, turn_over)])

            @block.scalar
            def _(act):
                act.preload_act_table_set(TABLES)
                act.wait_ge(ln["eps_set"], 1)
                act.wait_ge(sp_["half_set"], 1)

                def copy_value(n, s, turn):
                    act.wait_ge(value_done, n + 1)
                    if reused(n, 1):
                        act.wait_ge(gated_ready, n)
                    nc.scalar.activation(value[:, :], value_psum[:, :], ACT.Copy).then_inc(value_ready, 1)

                def tails(n, s, turn):
                    act.wait_ge(pre_ready, n + 1)
                    if reused(n, 1):
                        act.wait_ge(sp_["done"], n)
                    nc.scalar.activation(positive[:, :], pre_psum[:, :], ACT.Relu, bias=k["col"]["l3_b_wv1"])
                    softplus_tails(sp_, nc, act, pre_psum[:, :], k["col"]["l3_b_wv1"], n, s)

                def norm(n, s, turn):
                    if reused(n, 1):
                        act.wait_ge(transposed, n)
                    ln_apply(ln, nc, act, normed[:, :, :], rows[:, s, :, :], n, s)

                def copy(n, s, turn):
                    act.wait_ge(transposed, n + 1)
                    if reused(n, 1):
                        act.wait_ge(value_done, n)
                    nc.scalar.activation(normed_T[:, :], turned[:, :], ACT.Copy).then_inc(copied, 1)

                walk(act, n_blocks, [(5, lambda n, s, turn: merge_keep(mg, nc, act, n, s)),
                                     (1, lambda n, s, turn: ln_deviate(ln, nc, act, n, s)), (2, copy_value), (1, norm), (1, copy), (0, tails)])


def output_nodes(nc, k, x, accumulator, out, n_chunks):
    with phase(nc, "l3_nodes") as (sbuf, psum, sem):
        xs = sbuf("xs", [P, SLOTS, ROWS, D])
        acc = sbuf("acc", [P, SLOTS, ROWS, D])
        biased = sbuf("biased", [P, 2, ROWS, D])
        soft = sbuf("soft", [P, 2, ROWS, D])
        soft_T = sbuf("soft_T", [P, 2, ROWS, D])
        result = sbuf("result", [P, SLOTS, ROWS, D])
        turned = [psum(f"turned{s}", [P, 2, 512]) for s in range(2)]
        product = [psum(f"product{s}", [P, 2, 512]) for s in range(2)]
        loaded = [sem(f"loaded{s}") for s in range(SLOTS)]
        stored = [sem(f"stored{s}") for s in range(SLOTS)]
        biased_ready, transposed, copied, multiplied, finished = (
            sem(x) for x in ("biased_ready", "transposed", "copied", "multiplied", "finished"))
        sp_ = softplus_state(sbuf, psum, sem, ROWS * D)
        with nc.Block() as block:

            @block.sync
            def _(sp):
                def load(n, s, turn):
                    if reused(n, SLOTS):
                        sp.wait_ge(finished, n - SLOTS + 1)
                    sp.dma_start(flat(acc[:, s, :, :]), chunk_of(accumulator, n)).then_inc(loaded[s], 16)
                    sp.dma_start(flat(xs[:, s, :, :]), chunk_of(x, n)).then_inc(loaded[s], 16)

                def store(n, s, turn):
                    sp.wait_ge(finished, n + 1)
                    sp.dma_start(chunk_of(out, n), flat(result[:, s, :, :])).then_inc(stored[s], 16)

                walk(sp, n_chunks, [(0, load), (4, store)])
                for s in range(SLOTS):
                    sp.wait_ge(stored[s], 16 * uses(n_chunks, s))

            @block.vector
            def _(dve):
                softplus_set_half(sp_, nc)

                def soften(n, s, turn):
                    dve.wait_ge(sp_["tail_done"], n + 1)
                    if reused(n, 2):
                        dve.wait_ge(transposed, n - 1)
                    nc.vector.scalar_tensor_tensor(out=flat(soft[:, s % 2, :, :]), in0=flat(acc[:, s, :, :]), scalar=0.0,
                                                   in1=sp_["tail"][:, s % 2, :], op0=ALU.max, op1=ALU.add).then_inc(sp_["done"], 1)
                    if reused(n, 2):
                        dve.wait_ge(finished, n - 1)
                    nc.vector.tensor_tensor(biased[:, s % 2, :, :], xs[:, s, :, :],
                                            k["row"]["l3_b_o"].unsqueeze(1).to_broadcast([P, ROWS, D]), ALU.add).then_inc(biased_ready, 1)

                def add(n, s, turn):
                    dve.wait_ge(biased_ready, n + 1)
                    dve.wait_ge(multiplied, n + 1)
                    if reused(n, SLOTS):
                        dve.wait_ge(stored[s], turn * 16)
                    nc.vector.tensor_tensor(flat(result[:, s, :, :]), product[s % 2][:, :, :].rearrange("p b w -> p (b w)"),
                                            flat(biased[:, s % 2, :, :]), ALU.add).then_inc(finished, 1)

                walk(dve, n_chunks, [(3, add), (1, soften)])

            @block.tensor
            def _(pe):
                def turn_over(n, s, turn):
                    pe.wait_ge(sp_["done"], n + 1)
                    if reused(n, 2):
                        pe.wait_ge(copied, n - 1)
                    for r in range(ROWS):
                        last = nc.tensor.transpose(banks(turned[s % 2][:, :, :])[:, r, :], soft[:, s % 2, r, :], k["identity"][:, :])
                    last.then_inc(transposed, 1)

                def multiply(n, s, turn):
                    pe.wait_ge(copied, n + 1)
                    if reused(n, 2):
                        pe.wait_ge(finished, n - 1)
                    for r in range(ROWS):
                        last = nc.tensor.matmul(banks(product[s % 2][:, :, :])[:, r, :], soft_T[:, s % 2, r, :], k["W"]["l3_out"],
                                                start=True, stop=True)
                    last.then_inc(multiplied, 1)

                walk(pe, n_chunks, [(2, multiply), (1, turn_over)])

            @block.scalar
            def _(act):
                act.preload_act_table_set(TABLES)
                act.wait_ge(sp_["half_set"], 1)

                def tails(n, s, turn):
                    act.wait_ge(loaded[s], (turn + 1) * 32)
                    softplus_tails(sp_, nc, act, flat(acc[:, s, :, :]), None, n, s)

                def copy(n, s, turn):
                    act.wait_ge(transposed, n + 1)
                    if reused(n, 2):
                        act.wait_ge(multiplied, n - 1)
                    nc.scalar.activation(flat(soft_T[:, s % 2, :, :]), turned[s % 2][:, :, :].rearrange("p b w -> p (b w)"),
                                         ACT.Copy).then_inc(copied, 1)

                walk(act, n_chunks, [(2, copy), (0, tails)])


def build(nc, x, ends, dst_cols, dst_rows, src_rows, edge_T, edge_weight, matrices, wv1, columns, broadcast, biases,
          out, n_nodes):
    n_chunks = x.shape[0] // CHUNK
    n_blocks = ends.shape[0]
    last = n_nodes - (n_chunks - 1) * CHUNK
    assert last % ROWS == 0 and n_chunks * ROWS >= P
    n_pad = n_chunks * CHUNK

    def dram(name, shape):
        return nc.dram_tensor(name, shape, F32).ap()

    gcn_table1, gcn_table2, x1, x2, x3 = (dram(t, [n_pad, D]) for t in ("gcn_table1", "gcn_table2", "x1", "x2", "x3"))
    gcn_sum1, gcn_sum2, l3_sum = (dram(t, [n_pad + SPARE, D]) for t in ("gcn_sum1", "gcn_sum2", "l3_sum"))
    l1_sum, l2_sum = (dram(t, [n_pad + SPARE, SUMS]) for t in ("l1_sum", "l2_sum"))
    y_T, z_T = (dram(t, [n_chunks, P, CHUNK]) for t in ("y_T", "z_T"))
    k = {}
    with ExitStack() as ctx:
        load_constants(nc, ctx, k, matrices, wv1, columns, broadcast, biases, n_chunks * ROWS, n_blocks)
        degrees(nc, k, dst_cols, (gcn_sum1, gcn_sum2, l3_sum), n_blocks, n_chunks)
        norm_nodes(nc, k, x, gcn_table1, gcn_sum1, n_chunks)

        def gcn_layers(together):
            path = "together" if together else "apart"
            gcn_layer(nc, k, f"gcn1_{path}", ends, dst_rows, gcn_table1, gcn_sum1, None, k["W"]["gcn_w1"], k["row"]["gcn_b1"],
                      None, (gcn_table2, gcn_sum2), n_blocks, n_chunks, together, False)
            gcn_layer(nc, k, f"gcn2_{path}", ends, dst_rows, gcn_table2, gcn_sum2, l1_sum, k["W"]["gcn_w2"], k["row"]["gcn_b2"],
                      x, (x1,), n_blocks, n_chunks, together, True)

        if n_blocks == n_chunks:
            in_time = nc.values_load(k["in_time"][0:1, 0:1], min_val=0, max_val=1)
            with nc.If(in_time > 0):
                gcn_layers(True)
            with nc.Else():
                gcn_layers(False)
        else:
            gcn_layers(False)
        attention_over_edges(nc, k, "l1_edges", ends, dst_rows, edge_weight, x1, "l1_k", None, l1_sum, l2_sum, n_blocks)
        attention1_nodes(nc, k, x1, l1_sum, y_T, n_chunks, last // ROWS)
        feed_forward(nc, k, y_T, z_T, n_chunks, last // ROWS)
        add_layer1(nc, k, x1, z_T, x2, n_chunks)

        def layer2(together):
            path = "together" if together else "apart"
            attention2_layer(nc, k, f"l2_{path}", ends, dst_rows, x2, l2_sum, x3, l3_sum, n_blocks, n_chunks, together)

        if n_blocks == n_chunks:
            in_time = nc.values_load(k["in_time"][0:1, 0:1], min_val=0, max_val=1)
            with nc.If(in_time > 0):
                layer2(True)
            with nc.Else():
                layer2(False)
        else:
            layer2(False)
        messages_over_edges(nc, k, ends, src_rows, edge_T, x3, l3_sum, n_blocks)
        output_nodes(nc, k, x3, l3_sum, out, n_chunks)


def kernel(**inputs):
    import concourse.bacc as bacc
    import numpy as np
    from concourse.bass_utils import run_bass_kernel_spmd

    a = {name: np.asarray(v) for name, v in inputs.items()}
    n_nodes, n_edges = a["x"].shape[0], a["src"].shape[0]
    n_chunks, n_blocks = -(-n_nodes // CHUNK), -(-n_edges // BLOCK)
    n_pad, e_pad = n_chunks * CHUNK, n_blocks * BLOCK

    def pad_rows(v, rows, fill=0):
        return np.concatenate([v, np.full((rows - v.shape[0],) + v.shape[1:], fill, v.dtype)])

    assert n_pad > n_nodes or e_pad == n_edges
    src, dst = (pad_rows(a[s].astype(np.int32), e_pad, n_nodes).reshape(n_blocks, P, LANES) for s in ("src", "dst"))

    def lanes_first(v):
        return v.transpose(0, 2, 1).reshape(n_blocks, BLOCK)

    edge = pad_rows(a["edge_attr_64"], e_pad).reshape(n_blocks, P, LANES, 64).transpose(3, 0, 2, 1).reshape(64, e_pad)
    mats = {"gcn_w1": a["L0_gnn_W1"], "gcn_w2": a["L0_gnn_W2"], "l1_k": a["L1_gnn_Wk"], "l1_v": a["L1_gnn_Wv"],
            "l1_q": a["L1_gnn_Wq"], "l1_o": a["L1_gnn_Wo"], "ffn_up0": a["L1_gnn_W1"][:, :D], "ffn_up1": a["L1_gnn_W1"][:, D:],
            "ffn_down0": a["L1_gnn_W2"][:D], "ffn_down1": a["L1_gnn_W2"][D:], "l2_k": a["L2_gnn_Wk"], "l2_v": a["L2_gnn_Wv"],
            "l2_q": a["L2_gnn_Wq"], "l3_c": a["L3_gnn_W_c"].T, "l3_out": a["L3_gnn_W_o"].T, "l3_v": a["L3_gnn_W_v"].T,
            "l3_wv2": a["L3_gnn_W_wv2"].T, "l3_wvl": a["L3_gnn_W_wvl"].T}
    cols = {"l1_bo": a["L1_gnn_bo"], "l1_g1": a["L1_gnn_g1"], "l1_b1": a["L1_gnn_b1"], "l1_bf1a": a["L1_gnn_bf1"][:D],
            "l1_bf1b": a["L1_gnn_bf1"][D:], "l1_bf2": a["L1_gnn_bf2"], "l1_g2": a["L1_gnn_g2"], "l1_b2": a["L1_gnn_b2"],
            "l3_b_wv1": a["L3_gnn_b_wv1"], "l3_b_wv2": a["L3_gnn_b_wv2"]}
    rows = {"gcn_b1": a["L0_gnn_b1"], "gcn_b2": a["L0_gnn_b2"], "l1_e": a["L1_gnn_We"][0], 
            "l3_b_o": a["L3_gnn_b_o"], "l3_b_wvl": a["L3_gnn_b_wvl"]}
    biases = {"l2_bk": a["L2_gnn_bk"], "l2_bv": a["L2_gnn_bv"], "l2_bq": a["L2_gnn_bq"], "l3_b_c": a["L3_gnn_b_c"]}
    arrays = {
        "in_x": pad_rows(a["x"], n_pad),
        "in_ends": np.concatenate([src, dst], axis=2),
        "in_dst_cols": dst.transpose(1, 0, 2).reshape(P, n_blocks * LANES),
        "in_dst_rows": lanes_first(dst),
        "in_src_rows": lanes_first(src),
        "in_edge_T": edge,
        "in_edge_weight": pad_rows(a["edge_weight1"], e_pad).reshape(n_blocks, P, LANES),
        "in_matrices": np.concatenate([mats[m] for m in MATRICES], axis=1),
        "in_wv1": a["L3_gnn_W_wv1"].T,
        "in_columns": np.stack([cols[m] for m in COLUMNS], axis=1),
        "in_broadcast": np.concatenate([rows[m] for m in BROADCAST])[None],
        "in_biases": np.concatenate([biases[m] for m in BIASES])[None],
    }
    arrays = {name: np.ascontiguousarray(v) for name, v in arrays.items()}
    nc = bacc.Bacc("TRN2", target_bir_lowering=False, num_devices=1)
    args = {name: nc.dram_tensor(name, v.shape, mybir.dt.from_np(v.dtype), kind="ExternalInput").ap() for name, v in arrays.items()}
    out = nc.dram_tensor("out_nodes", [n_pad, D], F32, kind="ExternalOutput").ap()
    build(nc, args["in_x"], args["in_ends"], args["in_dst_cols"], args["in_dst_rows"], args["in_src_rows"], args["in_edge_T"],
          args["in_edge_weight"], args["in_matrices"], args["in_wv1"], args["in_columns"], args["in_broadcast"],
          args["in_biases"], out, n_nodes)
    result = run_bass_kernel_spmd(nc, [arrays], core_ids=[0])
    return result.results[0]["out_nodes"][:n_nodes]
```
